# Optimizing a Trainium2 kernel written in Bass

```python
import numpy as np
import jax
import jax.numpy as jnp

def _softmax(x, axis=-1):
    return jax.nn.softmax(x, axis=axis)

def _gelu(x):
    return jax.nn.gelu(x, approximate=True)

def _silu(x):
    return jax.nn.silu(x)

def _sigmoid(x):
    return jax.nn.sigmoid(x)

def _layernorm(x, axis=-1, eps=1e-05):
    m = jnp.mean(x, axis=axis, keepdims=True)
    v = jnp.var(x, axis=axis, keepdims=True)
    return (x - m) / jnp.sqrt(v + eps)

def _scatter_add(tgt, idx, src, axis=0):
    return tgt.at[idx].add(src)

def _segment_sum(src, seg, n):
    return jax.ops.segment_sum(src, seg, n)
kernel_name = 'mk_perceiver_d1_seqx_r4_a92f51'

def setup_inputs(seed: int=0):
    np.random.seed(seed)
    _w = jnp.asarray

    def _rec_inputs():
        import jax
        import jax.numpy as jnp
        _rk = jax.random.key(seed)
        x = 7.22e-05 + 1 * jax.random.normal(jax.random.fold_in(_rk, 1), (8, 64, 256), jnp.float32)
        _lenS = 64 - jax.random.randint(jax.random.fold_in(_rk, 7), (8,), 0, max(1, 64 // 4) + 1, jnp.int32)
        _lenS2 = 256 - jax.random.randint(jax.random.fold_in(_rk, 8), (8,), 0, max(1, 256 // 4) + 1, jnp.int32)
        _ctx_1024P = jax.random.normal(jax.random.fold_in(_rk, 11), (8, 16, 256), jnp.float32)
        _ctx_1024c = jax.random.dirichlet(jax.random.fold_in(_rk, 511), 0.3 * jnp.ones((16,), jnp.float32), (8, 256))
        _ctx_1024t = jnp.einsum('bsk,bkd->bsd', _ctx_1024c, _ctx_1024P)
        _ctx_1024t = _ctx_1024t * jax.lax.rsqrt(jnp.mean(jnp.square(_ctx_1024t)) + 1e-12) * 0.953939
        ctx_1024 = 4.13588e-05 + 0.999923 * (_ctx_1024t + 0.3 * jax.random.normal(jax.random.fold_in(_rk, 611), (8, 256, 256), jnp.float32))
        _validS = jnp.arange(64)[None, :] < _lenS[:, None]
        _validS2 = jnp.arange(256)[None, :] < _lenS2[:, None]
        _causal = jnp.tril(jnp.ones((64, 64), dtype=bool))
        mask_BxS2_ik0 = jnp.where(jnp.broadcast_to(_validS2[:, :], (8, 256)), 0, 1).astype(jnp.int32)
        return (x, ctx_1024, mask_BxS2_ik0)
    x, ctx_1024, mask_BxS2_ik0 = _rec_inputs()

    def _L0_xattn_setup():
        import jax, jax.numpy as jnp
        import numpy as np
        B, LQ, LK, D = (4, 512, 512, 256)
        H = 16
        HD = D // H

        def _split_heads(x):
            b, l, _ = x.shape
            return x.reshape(b, l, H, HD).transpose(0, 2, 1, 3)
        key = jax.random.key(seed)
        ks = jax.random.split(key, 10)
        s = 0.02
        return {'hidden_states': jax.random.normal(ks[0], (B, LQ, D), jnp.float32), 'context': jax.random.normal(ks[1], (B, LK, D), jnp.float32), 'attention_mask': jax.random.randint(ks[2], (B, LK), 0, 2, jnp.int32), 'q_w': jax.random.normal(ks[3], (D, D), jnp.float32) * s, 'q_b': jnp.zeros((D,), jnp.float32), 'k_w': jax.random.normal(ks[4], (D, D), jnp.float32) * s, 'k_b': jnp.zeros((D,), jnp.float32), 'v_w': jax.random.normal(ks[5], (D, D), jnp.float32) * s, 'v_b': jnp.zeros((D,), jnp.float32)}
    _L0_xattn_all = _L0_xattn_setup()
    _L0_xattn_in = {k: v for k, v in _L0_xattn_all.items() if k in ('q_w', 'q_b', 'k_w', 'k_b', 'v_w', 'v_b')}
    del _L0_xattn_all

    def _L0_attn_setup():
        import jax, jax.numpy as jnp
        import numpy as np
        B, S, D, H, R = (8, 256, 256, 8, 32)
        DH = D // H

        def _lowrank(xh, U, V, b):
            t = jnp.einsum('bshd,hrd->bshr', xh, V)
            return jnp.einsum('bshr,hdr->bshd', t, U) + b
        key = jax.random.key(seed)
        ks = jax.random.split(key, 10)
        p = lambda k, shape: jax.random.normal(k, shape, dtype=jnp.float32) * 0.02
        return {'x': jax.random.normal(ks[0], (B, S, D), dtype=jnp.float32), 'Uq': p(ks[1], (H, DH, R)), 'Vq': p(ks[2], (H, R, DH)), 'bq': p(ks[3], (H, DH)), 'Uk': p(ks[4], (H, DH, R)), 'Vk': p(ks[5], (H, R, DH)), 'bk': p(ks[6], (H, DH)), 'Uv': p(ks[7], (H, DH, R)), 'Vv': p(ks[8], (H, R, DH)), 'bv': p(ks[9], (H, DH))}
    _L0_attn_all = _L0_attn_setup()
    _L0_attn_in = {k: v for k, v in _L0_attn_all.items() if k in ('Uq', 'Vq', 'bq', 'Uk', 'Vk', 'bk', 'Uv', 'Vv', 'bv')}
    del _L0_attn_all

    def _L0_ffn_setup():
        import jax, jax.numpy as jnp
        import numpy as np
        EMB, HID, E, TOPK = (256, 1024, 8, 2)
        key = jax.random.key(seed)
        ks = jax.random.split(key, 10)
        s = 0.02
        return {'x': jax.random.normal(ks[0], (4, 512, EMB), jnp.float32), 'rw1': s * jax.random.normal(ks[1], (EMB, HID), jnp.float32), 'rb1': jnp.zeros((HID,), jnp.float32), 'rw2': s * jax.random.normal(ks[2], (HID, E), jnp.float32), 'rb2': jnp.zeros((E,), jnp.float32), 'w1': s * jax.random.normal(ks[3], (E, EMB, HID), jnp.float32), 'b1': jnp.zeros((E, HID), jnp.float32), 'w2': s * jax.random.normal(ks[4], (E, HID, EMB), jnp.float32), 'b2': jnp.zeros((E, EMB), jnp.float32)}
    _L0_ffn_all = _L0_ffn_setup()
    _L0_ffn_in = {k: v for k, v in _L0_ffn_all.items() if k in ('rw1', 'rb1', 'rw2', 'rb2', 'w1', 'b1', 'w2', 'b2')}
    del _L0_ffn_all
    return {'x': x, 'ctx_1024': ctx_1024, 'mask_BxS2_ik0': mask_BxS2_ik0, 'L0_xattn_q_w': _L0_xattn_in['q_w'], 'L0_xattn_q_b': _L0_xattn_in['q_b'], 'L0_xattn_k_w': _L0_xattn_in['k_w'], 'L0_xattn_k_b': _L0_xattn_in['k_b'], 'L0_xattn_v_w': _L0_xattn_in['v_w'], 'L0_xattn_v_b': _L0_xattn_in['v_b'], 'L0_attn_Uq': _L0_attn_in['Uq'], 'L0_attn_Vq': _L0_attn_in['Vq'], 'L0_attn_bq': _L0_attn_in['bq'], 'L0_attn_Uk': _L0_attn_in['Uk'], 'L0_attn_Vk': _L0_attn_in['Vk'], 'L0_attn_bk': _L0_attn_in['bk'], 'L0_attn_Uv': _L0_attn_in['Uv'], 'L0_attn_Vv': _L0_attn_in['Vv'], 'L0_attn_bv': _L0_attn_in['bv'], 'L0_ffn_rw1': _L0_ffn_in['rw1'], 'L0_ffn_rb1': _L0_ffn_in['rb1'], 'L0_ffn_rw2': _L0_ffn_in['rw2'], 'L0_ffn_rb2': _L0_ffn_in['rb2'], 'L0_ffn_w1': _L0_ffn_in['w1'], 'L0_ffn_b1': _L0_ffn_in['b1'], 'L0_ffn_w2': _L0_ffn_in['w2'], 'L0_ffn_b2': _L0_ffn_in['b2']}

def reference(x, ctx_1024, mask_BxS2_ik0, L0_xattn_q_w, L0_xattn_q_b, L0_xattn_k_w, L0_xattn_k_b, L0_xattn_v_w, L0_xattn_v_b, L0_attn_Uq, L0_attn_Vq, L0_attn_bq, L0_attn_Uk, L0_attn_Vk, L0_attn_bk, L0_attn_Uv, L0_attn_Vv, L0_attn_bv, L0_ffn_rw1, L0_ffn_rb1, L0_ffn_rw2, L0_ffn_rb2, L0_ffn_w1, L0_ffn_b1, L0_ffn_w2, L0_ffn_b2):
    import jax
    import jax.numpy as jnp

    def _L0_xattn_ref(hidden_states, context, attention_mask, q_w, q_b, k_w, k_b, v_w, v_b):
        import jax, jax.numpy as jnp
        import numpy as np
        B, LQ, LK, D = (4, 512, 512, 256)
        H = 16
        HD = D // H

        def _split_heads(x):
            b, l, _ = x.shape
            return x.reshape(b, l, H, HD).transpose(0, 2, 1, 3)
        q = _split_heads(hidden_states @ q_w.T + q_b)
        k = _split_heads(context @ k_w.T + k_b)
        v = _split_heads(context @ v_w.T + v_b)
        scores = jnp.einsum('bhqd,bhkd->bhqk', q, k) / jnp.sqrt(jnp.float32(HD))
        mask = (attention_mask > 0)[:, None, None, :]
        scores = jnp.where(mask, -jnp.inf, scores)
        probs = jax.nn.softmax(scores, axis=-1)
        ctx = jnp.einsum('bhqk,bhkd->bhqd', probs, v)
        ctx = ctx.transpose(0, 2, 1, 3).reshape(ctx.shape[0], ctx.shape[2], H * HD)
        return ctx

    def _L0_attn_ref(x, Uq, Vq, bq, Uk, Vk, bk, Uv, Vv, bv):
        import jax, jax.numpy as jnp
        import numpy as np
        B, S, D, H, R = (8, 256, 256, 8, 32)
        DH = D // H

        def _lowrank(xh, U, V, b):
            t = jnp.einsum('bshd,hrd->bshr', xh, V)
            return jnp.einsum('bshr,hdr->bshd', t, U) + b
        b_, s_, _ = x.shape
        xh = x.reshape(b_, s_, H, DH)
        q = _lowrank(xh, Uq, Vq, bq)
        k = _lowrank(xh, Uk, Vk, bk)
        v = _lowrank(xh, Uv, Vv, bv)
        scores = jnp.einsum('bqhd,bkhd->bhqk', q, k) / DH ** 0.5
        attn = jax.nn.softmax(scores, axis=-1)
        out = jnp.einsum('bhqk,bkhd->bqhd', attn, v)
        return out.reshape(b_, s_, D)

    def _L0_ffn_ref(x, rw1, rb1, rw2, rb2, w1, b1, w2, b2):
        import jax, jax.numpy as jnp
        import numpy as np
        EMB, HID, E, TOPK = (256, 1024, 8, 2)
        B, S, D = x.shape
        logits = jax.nn.silu(jnp.einsum('bsd,dh->bsh', x, rw1) + rb1)
        logits = jnp.einsum('bsh,he->bse', logits, rw2) + rb2
        k_logits, k_index = jax.lax.top_k(logits, TOPK)
        k_prob = jax.nn.softmax(k_logits, axis=-1)
        xf = x.reshape(B * S, D)
        k_index_f = k_index.reshape(B * S, TOPK)
        k_prob_f = k_prob.reshape(B * S, TOPK)
        out = jnp.zeros_like(xf)
        for e in range(E):
            we = jnp.sum(jnp.where(k_index_f == e, k_prob_f, 0.0), axis=-1)
            h = jax.nn.silu(xf @ w1[e] + b1[e]) @ w2[e] + b2[e]
            out = out + we[:, None] * h
        return out.reshape(B, S, D)
    x = x + _L0_xattn_ref(_layernorm(x, axis=-1), ctx_1024, mask_BxS2_ik0, L0_xattn_q_w, L0_xattn_q_b, L0_xattn_k_w, L0_xattn_k_b, L0_xattn_v_w, L0_xattn_v_b)
    x = x + _L0_attn_ref(_layernorm(x, axis=-1), L0_attn_Uq, L0_attn_Vq, L0_attn_bq, L0_attn_Uk, L0_attn_Vk, L0_attn_bk, L0_attn_Uv, L0_attn_Vv, L0_attn_bv)
    x = x + _L0_ffn_ref(_layernorm(x, axis=-1), L0_ffn_rw1, L0_ffn_rb1, L0_ffn_rw2, L0_ffn_rb2, L0_ffn_w1, L0_ffn_b1, L0_ffn_w2, L0_ffn_b2)
    return x

_drawn_inputs = setup_inputs


def setup_inputs(seed=0):
    import zlib

    import numpy as np

    out = dict(_drawn_inputs(seed))
    spreads = {'L0_xattn_q_b': (0.0, 0.8),
     'L0_xattn_k_b': (0.0, 2.0),
     'L0_xattn_v_b': (0.0, 0.1),
     'L0_ffn_rb1': (0.0, 0.1),
     'L0_ffn_rb2': (0.0, 0.1),
     'L0_ffn_b1': (0.0, 0.34),
     'L0_ffn_b2': (0.0, 0.1)}
    factors = {'L0_xattn_q_w': 7.199,
     'L0_xattn_k_w': 8.0,
     'L0_attn_Uq': 8.0,
     'L0_attn_Vq': 8.0,
     'L0_attn_bq': 21.719,
     'L0_attn_Uk': 8.0,
     'L0_attn_Vk': 8.0,
     'L0_attn_bk': 64.0,
     'L0_attn_Uv': 8.0,
     'L0_attn_Vv': 8.0}
    for name, (base, spread) in spreads.items():
        noise = np.random.default_rng([zlib.crc32(name.encode()), seed]).standard_normal(out[name].shape)
        drawn = base * np.exp(spread * noise) if base else spread * noise
        out[name] = jnp.asarray(drawn.astype(out[name].dtype))
    for name, factor in factors.items():
        out[name] = (out[name] * factor).astype(out[name].dtype)
    return out
```

```python
from contextlib import ExitStack

import concourse.bass as bass
from concourse import mybir

F32 = mybir.dt.float32
F16 = mybir.dt.float16
BF16 = mybir.dt.bfloat16
I32 = mybir.dt.int32
U32 = mybir.dt.uint32
ALU = mybir.AluOpType
ACT = mybir.ActivationFunctionType
AX = mybir.AxisListType

P = 128
EPS = 1e-5
MASKED = -1e30


def perceiver_layer(nc, x, ctx_in, mask, q_w, q_b, k_w, k_b, v_w, v_b, Uq, Vq, bq, Uk, Vk, bk, Uv, Vv, bv,
                    rw1, rb1, rw2, rb2, w1, b1, w2, b2, out):
    B, SQ, D = x.shape
    SK = ctx_in.shape[1]
    XH = 16
    XD = D // XH
    H, DH, R = Uq.shape
    E, _, HID = w1.shape
    DC = D // P
    NT = B * SQ // P
    KT = B * SK // P
    HC = HID // P
    NTOK = B * SQ
    NU = B * DC
    PAIRS = P // XD // 2
    RING = 2
    XSCALE = XD ** -0.5
    SSCALE = DH ** -0.5
    VW = XD + 1

    es = ExitStack()
    with es:
        def sb(name, shape, dt=F32):
            return es.enter_context(nc.sbuf_tensor(name, shape, dt))

        def sem(name):
            return es.enter_context(nc.semaphore(name))

        xs = sb("xs", [P, NT, D])
        xn = sb("xn", [P, NT, D])
        xnT = sb("xnT", [P, DC, NTOK])
        stats = sb("stats", [P, 3, NT, 6])
        mv = sb("mv", [P, 3, NT, 2])
        vareps = sb("vareps", [P, 3, NT])
        rstd = sb("rstd", [P, 3, NT])
        minus_half = sb("minus_half", [P, NT])
        ident = sb("ident", [P, P])
        headmask = sb("headmask", [P, P // XD])
        blockmask = sb("blockmask", [P, P // DH])
        iota_i = sb("iota_i", [P, E], I32)
        iota_f = sb("iota_f", [P, E])
        ones_row = sb("ones_row", [1, P], BF16)
        mask_i = sb("mask_i", [1, B * SK], I32)
        mask_row = sb("mask_row", [1, B * SK], BF16)
        wraw = sb("wraw", [P, 3, DC, D])
        wT = sb("wT", [P, 3, DC, D])
        NB = 4 * DC + HC + E * HC
        brow = sb("brow", [NB, P])
        biasT = sb("biasT", [P, NB])
        vb_all = sb("vb_all", [P, D])
        bv_all = sb("bv_all", [P, D])
        rb2_all = sb("rb2_all", [P, E])
        b2_sb = sb("b2_sb", [E, D])
        hT = sb("hT", [P, HC, NTOK])
        ctx_sb = hT[:, 0:4].rearrange("p a n -> p (a n)").rearrange("p (g k d) -> p g k d", g=2, d=D)
        ctxT = hT[:, 4:8].rearrange("p (c g) n -> p c g n", g=2)
        kT_hi = sb("kT_hi", [P, DC, B * SK], F16)
        kT_lo = sb("kT_lo", [P, DC, B * SK], F16)
        v_hi = sb("v_hi", [P, KT, XH, VW], F16)
        v_lo = sb("v_lo", [P, KT, XH, VW], F16)
        q32 = sb("q32", [P, DC, NTOK])
        qh = sb("qh", [P, DC, NTOK], F16)
        ql = sb("ql", [P, DC, NTOK], F16)
        qbd_hi = sb("qbd_hi", [P, DC, B, P // XD, SQ], F16)
        qbd_lo = sb("qbd_lo", [P, DC, B, P // XD, SQ], F16)
        nmax = sb("nmax", [P, NU, PAIRS])
        prob = sb("prob", [P, 2, PAIRS, SK])
        pT_hi = sb("pT_hi", [P, 2, 2, PAIRS, P], F16)
        pT_lo = sb("pT_lo", [P, 2, 2, PAIRS, P], F16)
        orec = sb("orec", [P, B, DC * PAIRS])
        on = sb("on", [P, B, DC * PAIRS, XD])
        uv = sb("uv", [P, 6, DC, R])
        uvbd = sb("uvbd", [P, 6, DC, P])
        uT = sb("uT", [P, 3, DC, P])
        mbd = sb("mbd", [P, 3, DC, P])
        s_q32, s_qh, s_ql = q32, qh, ql
        s_qbd_hi, s_qbd_lo = qbd_hi[:, :, :, 0:P // DH, :], qbd_lo[:, :, :, 0:P // DH, :]
        s_kh, s_kl = kT_hi[:, :, 0:NTOK], kT_lo[:, :, 0:NTOK]
        s_vh, s_vl = (a[:, 0:4].rearrange("p t h d -> p (t h d)")[:, 0:NT * D].rearrange("p (t d) -> p t d", d=D)
                      for a in (v_hi, v_lo))
        s_max = sb("s_max", [P, NT, 8])
        s_sc = prob[:, :, :, :].rearrange("p u g k -> p (u g k)").rearrange("p (t k q) -> p t k q", t=NT, q=SQ)
        s_sum = sb("s_sum", [P, NT, 8])
        s_rec = sb("s_rec", [P, NT, 8])
        s_pTh, s_pTl = (a[:, :, :, :, :].rearrange("p u k g q -> p (u k) g q") for a in (pT_hi, pT_lo))
        s_on = on[:, :, :, :].rearrange("p b o d -> p (b o d)").rearrange("p (t k d) -> p t k d", t=NT, d=DH)
        rw1_sb = sb("rw1_sb", [P, DC, HID])
        rw2_sb = sb("rw2_sb", [P, HC, E])
        logit = sb("logit", [P, NT, E])
        top = sb("top", [P, NT, 8])
        topi = sb("topi", [P, NT, 8], U32)
        topf = sb("topf", [P, NT, 8])
        gap = sb("gap", [P, NT])
        th = sb("th", [P, NT])
        p1 = sb("p1", [P, NT])
        p2 = sb("p2", [P, NT])
        we1 = sb("we1", [P, NT, E])
        we2 = sb("we2", [P, NT, E])
        we = sb("we", [P, NT, E])
        weT = uT[0:E].rearrange("p i c n -> p (i c) n")[:, 0:NT]
        w1_sb = sb("w1_sb", [P, RING, DC, HID])
        w2_sb = sb("w2_sb", [P, RING, HC, D])
        acc = xn

        ps = es.enter_context(nc.psum_tensor("ps", [P, 8, 512], F32))

        in_x, in_brow, in_mask, in_uv, in_misc, in_router = (
            sem(n) for n in ("in_x", "in_brow", "in_mask", "in_uv", "in_misc", "in_router"))
        in_w = [sem(f"in_w{i}") for i in range(3)]
        in_ctx = [sem(f"in_ctx{i}") for i in range(4)]
        in_e = [sem(f"in_e{i}") for i in range(RING)]
        consts = sem("consts")
        bd_ready = sem("bd_ready")
        rstd_ready = sem("rstd_ready")
        var_ready = sem("var_ready")
        xn_ready = sem("xn_ready")
        dve_step = sem("dve_step")
        mask_ready = sem("mask_ready")
        wt_done = sem("wt_done")
        wt_out = sem("wt_out")
        xt_done = sem("xt_done")
        xt_out = sem("xt_out")
        q_done = sem("q_done")
        q_out = sem("q_out")
        qbd_ready = sem("qbd_ready")
        ct_done = sem("ct_done")
        ct_out_d = sem("ct_out_d")
        ct_out_a = sem("ct_out_a")
        k_done = sem("k_done")
        k_hi_out = sem("k_hi_out")
        k_lo_out = sem("k_lo_out")
        v_done = sem("v_done")
        v_hi_out = sem("v_hi_out")
        v_lo_out = sem("v_lo_out")
        ut_done = sem("ut_done")
        ut_out = sem("ut_out")
        m_done = sem("m_done")
        m_out = sem("m_out")
        sc_done = sem("sc_done")
        max_ready = sem("max_ready")
        exp_ready = sem("exp_ready")
        pt_done = sem("pt_done")
        pt_hi_out = sem("pt_hi_out")
        pt_lo_out = sem("pt_lo_out")
        pv_done = sem("pv_done")
        on_ready = sem("on_ready")
        sh_done = sem("sh_done")
        x1_ready = sem("x1_ready")
        x2t_done = sem("x2t_done")
        x2t_out = sem("x2t_out")
        sq_done = sem("sq_done")
        sk_done = sem("sk_done")
        sv_done = sem("sv_done")
        sq_out = sem("sq_out")
        sqbd_ready = sem("sqbd_ready")
        sk_hi_out = sem("sk_hi_out")
        sk_lo_out = sem("sk_lo_out")
        sv_hi_out = sem("sv_hi_out")
        sv_lo_out = sem("sv_lo_out")
        ssc_done = sem("ssc_done")
        ssub_ready = sem("ssub_ready")
        sexp_ready = sem("sexp_ready")
        spt_done = sem("spt_done")
        spt_hi_out = sem("spt_hi_out")
        spt_lo_out = sem("spt_lo_out")
        spv_done = sem("spv_done")
        son_ready = sem("son_ready")
        ssh_done = sem("ssh_done")
        x2_ready = sem("x2_ready")
        x3t_done = sem("x3t_done")
        x3t_out = sem("x3t_out")
        r1_done = sem("r1_done")
        r1_out = sem("r1_out")
        lg_done = sem("lg_done")
        gap_ready = sem("gap_ready")
        th_ready = sem("th_ready")
        we_ready = sem("we_ready")
        wet_done = sem("wet_done")
        wet_out = sem("wet_out")
        b2_done = sem("b2_done")
        acc_ready = sem("acc_ready")
        h_done = sem("h_done")
        h_out = sem("h_out")
        y_done = sem("y_done")
        y_out = sem("y_out")
        stored = sem("stored")

        block = es.enter_context(nc.Block())

        QB, KB, SQB, SKB, RB, EB = 0, DC, 2 * DC, 3 * DC, 4 * DC, 4 * DC + HC

        CONSTS = 14

        @block.sync
        def _(sp):
            sp.dma_start(xs[:, :, :], x.rearrange("(t b) s d -> (b s) t d", b=2)).then_inc(in_x, 16)
            for i, w in enumerate((q_w, k_w, v_w)):
                sp.dma_start(wraw[:, i], w.rearrange("(c p) d -> p c d", p=P)).then_inc(in_w[i], 16)
            rows = [(q_b, 0), (k_b, DC)]
            for a, r in rows:
                sp.dma_start(brow[r:r + DC, :], a.rearrange("(c p) -> c p", p=P)).then_inc(in_brow, 16)
            for a, r in ((bq, SQB), (bk, SKB)):
                sp.dma_start(brow[r:r + DC, :], a.rearrange("(c h) d -> c (h d)", c=DC)).then_inc(in_brow, 16)
            sp.dma_start(brow[RB:RB + HC, :], rb1.rearrange("(c p) -> c p", p=P)).then_inc(in_brow, 16)
            sp.dma_start(brow[EB:EB + E * HC, :], b1.rearrange("e (c p) -> (e c) p", p=P)).then_inc(in_brow, 16)
            sp.dma_start(mask_i[:, :], mask.rearrange("b k -> (b k)").unsqueeze(0)).then_inc(in_mask, 16)
            ctx_g = ctx_in.rearrange("b (k p) d -> p (b k) d", p=P)
            for n in range(2):
                sp.dma_start(ctx_sb[:, n], ctx_g[:, 4 * n:4 * n + 4]).then_inc(in_ctx[n], 16)
            for i, a in enumerate((Vq, Vk, Vv, Uq, Uk, Uv)):
                sp.dma_start(uv[:, i], a.rearrange("(c h) r d -> (h r) c d", c=DC)).then_inc(in_uv, 16)
            sp.dma_start(vb_all[:, :], v_b.partition_broadcast(P)).then_inc(in_misc, 16)
            sp.dma_start(bv_all[:, :], bv.rearrange("h d -> (h d)").partition_broadcast(P)).then_inc(in_misc, 16)
            sp.dma_start(rb2_all[:, :], rb2.partition_broadcast(P)).then_inc(in_misc, 16)
            sp.dma_start(b2_sb[:, :], b2).then_inc(in_misc, 16)
            for n in range(2, 4):
                sp.wait_ge(ct_done, 2 * (n - 1))
                sp.dma_start(ctx_sb[:, n % 2], ctx_g[:, 4 * n:4 * n + 4]).then_inc(in_ctx[n], 16)
            sp.dma_start(rw1_sb[:, :, :], rw1.rearrange("(c p) h -> p c h", p=P)).then_inc(in_router, 16)
            sp.dma_start(rw2_sb[:, :, :], rw2.rearrange("(c p) e -> p c e", p=P)).then_inc(in_router, 16)
            for e in range(E):
                if e >= RING:
                    sp.wait_ge(y_done, 2 * (e - RING + 1))
                sp.dma_start(w1_sb[:, e % RING], w1[e].rearrange("(c p) h -> p c h", p=P)).then_inc(in_e[e % RING], 16)
                sp.dma_start(w2_sb[:, e % RING], w2[e].rearrange("(c p) d -> p c d", p=P)).then_inc(in_e[e % RING], 16)
            for t in range(2):
                sp.wait_ge(y_out, 4 * (E - 1) + 2 * t + 2)
                sp.dma_start(out.rearrange("(t b) s d -> (b s) t d", b=2)[:, 2 * t:2 * t + 2],
                             acc[:, 2 * t:2 * t + 2]).then_inc(stored, 16)
            sp.wait_ge(stored, 32)

        @block.gpsimd
        def _(pool):
            step = [0]

            def link(ins):
                step[0] += 1
                ins.then_inc(consts, 1)
                pool.wait_ge(consts, step[0])

            link(pool.memset(ident[:, :], 0.0))
            link(pool.affine_select(out=ident[:, :], in_=ident[:, :], compare_op=ALU.not_equal, fill=1.0,
                                    base=0, pattern=[[-1, P]], channel_multiplier=1))
            link(pool.memset(minus_half[:, :], -0.5))
            link(pool.memset(ones_row[:, :], 1.0))
            for m, width in ((headmask, XD), (blockmask, DH)):
                n = P // width
                link(pool.memset(m[:, :], 1.0))
                link(pool.affine_select(out=m[:, :], in_=m[:, :], compare_op=ALU.is_ge, fill=0.0,
                                        base=0, pattern=[[-width, n]], channel_multiplier=1))
                link(pool.affine_select(out=m[:, :], in_=m[:, :], compare_op=ALU.is_ge, fill=0.0,
                                        base=width - 1, pattern=[[width, n]], channel_multiplier=-1))
            link(pool.memset(v_hi[:, :, :, :], 1.0))
            link(pool.memset(v_lo[:, :, :, :], 0.0))
            link(pool.iota(iota_i[:, :], pattern=[[1, E]], base=0, channel_multiplier=0))
            link(pool.tensor_copy(iota_f[:, :], iota_i[:, :]))
            assert step[0] == CONSTS

            def norm_scale(n, t):
                pool.wait_ge(var_ready, n * NT + t + 1)
                pool.tensor_tensor(rstd[:, n, t:t + 1], vareps[:, n, t:t + 1], minus_half[:, t:t + 1],
                                   ALU.pow).then_inc(rstd_ready, 1)

            for t in range(NT):
                norm_scale(0, t)
            pool.wait_ge(in_uv, 96)
            for i in range(6):
                pool.tensor_tensor(uvbd[:, i].rearrange("p c (h r) -> p c h r", r=R),
                                   uv[:, i].unsqueeze(2).broadcast_to([P, DC, P // DH, R]),
                                   blockmask[:, :].unsqueeze(1).unsqueeze(3).broadcast_to([P, DC, P // DH, R]),
                                   ALU.mult).then_inc(bd_ready, 1)
            for n in (1, 2):
                for t in range(NT):
                    norm_scale(n, t)

        @block.tensor
        def _(pe):
            pe.wait_ge(consts, 2)
            for i in range(3):
                pe.wait_ge(in_w[i], 16)
                for dc in range(DC):
                    for oc in range(DC):
                        m = pe.transpose(ps[:, i, (dc * DC + oc) * P:(dc * DC + oc + 1) * P],
                                         wraw[:, i, oc, dc * P:(dc + 1) * P], ident[:, :])
                m.then_inc(wt_done, 1)
            pe.wait_ge(in_brow, 96)
            pe.transpose(ps[:, 3, 0:NB], brow[:, :], ident[0:NB, 0:NB]).then_inc(wt_done, 1)

            def turn_tiles(t, bank, done):
                for j in range(2):
                    pe.wait_ge(xn_ready, done[1] + t + j + 1)
                    for dc in range(DC):
                        m = pe.transpose(ps[:, bank, (dc * 2 + j) * P:(dc * 2 + j + 1) * P],
                                         xn[:, t + j, dc * P:(dc + 1) * P], ident[:, :])
                m.then_inc(done[0], 1)

            turn_tiles(0, 4, (xt_done, 0))
            turn_tiles(2, 5, (xt_done, 0))
            pe.wait_ge(wt_out, 4)
            pe.wait_ge(xt_out, 2)
            for oc in range(DC):
                for dc in range(DC):
                    m = pe.matmul(ps[:, 6 + oc, :], wT[:, 0, dc, oc * P:(oc + 1) * P], xnT[:, dc, :],
                                  start=(dc == 0), stop=(dc == DC - 1))
                m.then_inc(q_done, 1)
            for n in range(4):
                pe.wait_ge(in_ctx[n], 16)
                if n:
                    pe.wait_ge(ct_out_d, n)
                    pe.wait_ge(ct_out_a, n)
                for j in range(2):
                    for i in range(2):
                        for dc in range(DC):
                            m = pe.transpose(ps[:, j, (dc * 2 + i) * P:(dc * 2 + i + 1) * P],
                                             ctx_sb[:, n % 2, 2 * j + i, dc * P:(dc + 1) * P], ident[:, :])
                    m.then_inc(ct_done, 1)
                pe.wait_ge(ct_out_d, n + 1)
                pe.wait_ge(ct_out_a, n + 1)
                for oc in range(DC):
                    if n:
                        pe.wait_ge(k_lo_out, DC * (n - 1) + oc + 1)
                    for dc in range(DC):
                        m = pe.matmul(ps[:, 2 + oc, :], wT[:, 1, dc, oc * P:(oc + 1) * P], ctxT[:, dc, n % 2, :],
                                      start=(dc == 0), stop=(dc == DC - 1))
                    m.then_inc(k_done, 1)
                for j in range(2):
                    if n:
                        pe.wait_ge(v_lo_out, 2 * (n - 1) + j + 1)
                    for i in range(2):
                        for dc in range(DC):
                            m = pe.matmul(ps[:, 4 + j, i * D:(i + 1) * D],
                                          ctxT[:, dc, n % 2, (2 * j + i) * P:(2 * j + i + 1) * P], wT[:, 2, dc, :],
                                          start=(dc == 0), stop=(dc == DC - 1))
                    m.then_inc(v_done, 1)
            pe.wait_ge(bd_ready, 6)
            pe.wait_ge(q_out, DC)
            for i in range(3):
                for c in range(DC):
                    k = i * DC + c
                    m = pe.transpose(ps[:, 6 + k // 4, (k % 4) * P:(k % 4 + 1) * P], uvbd[:, 3 + i, c, :], ident[:, :])
            m.then_inc(ut_done, 1)
            pe.wait_ge(ut_out, 1)
            for i in range(3):
                for c in range(DC):
                    k = i * DC + c
                    m = pe.matmul(ps[:, 6 + k // 4, (k % 4) * P:(k % 4 + 1) * P], uvbd[:, i, c, :], uT[:, i, c, :],
                                  start=True, stop=True)
            m.then_inc(m_done, 1)

            def scores(u):
                b, c = divmod(u, DC)
                if u == 0:
                    pe.wait_ge(mask_ready, 1)
                    pe.wait_ge(k_lo_out, 4 * DC)
                    pe.wait_ge(ct_out_a, 4)
                if u < DC:
                    pe.wait_ge(qbd_ready, u + 1)
                if u >= 2:
                    pe.wait_ge(exp_ready, u - 1)
                for half in range(2):
                    bank = 2 * (u % 2) + half
                    pe.matmul(ps[:, bank, :], ones_row[:, :],
                              mask_row[:, b * SK:(b + 1) * SK].unsqueeze(1).broadcast_to([1, 2, SK]),
                              start=True, stop=False, skip_group_check=True)
                    for i in range(2):
                        pair = 2 * half + i
                        dst = ps[:, bank, i * SK:(i + 1) * SK]
                        lh = qbd_hi[:, c, b, 2 * pair:2 * pair + 2, :]
                        ll = qbd_lo[:, c, b, 2 * pair:2 * pair + 2, :]
                        keys = slice(b * SK, (b + 1) * SK)
                        pe.matmul(dst, ll, kT_hi[:, c, keys], start=False, stop=False, skip_group_check=True)
                        pe.matmul(dst, lh, kT_lo[:, c, keys], start=False, stop=False, skip_group_check=True)
                        m = pe.matmul(dst, lh, kT_hi[:, c, keys], start=False, stop=(i == 1),
                                      skip_group_check=True)
                m.then_inc(sc_done, 1)

            def turn_probs(u):
                pe.wait_ge(exp_ready, u + 1)
                for kt in range(2):
                    if u:
                        pe.wait_ge(pt_lo_out, 2 * (u - 1) + kt + 1)
                    else:
                        pe.wait_ge(v_lo_out, 8)
                    for pair in range(PAIRS):
                        m = pe.transpose(ps[:, 4 + kt, pair * P:(pair + 1) * P],
                                         prob[:, u % 2, pair, kt * P:(kt + 1) * P], ident[:, :])
                    m.then_inc(pt_done, 1)

            def times_values(u):
                b, c = divmod(u, DC)
                if u == 0:
                    pe.wait_ge(m_out, 1)
                if c == 0 and b >= 2:
                    pe.wait_ge(on_ready, b - 1)
                pe.wait_ge(pt_lo_out, 2 * u + 2)
                for pair in range(PAIRS):
                    o = c * PAIRS + pair
                    dst = ps[:, 6 + b % 2, o * 2 * VW:(o + 1) * 2 * VW]
                    h0 = 2 * o
                    n = 0
                    for kt in range(2):
                        vh = v_hi[:, 2 * b + kt, h0:h0 + 2, :]
                        vl = v_lo[:, 2 * b + kt, h0:h0 + 2, :]
                        for lhs, rhs in ((pT_lo, vh), (pT_hi, vl), (pT_hi, vh)):
                            m = pe.matmul(dst, lhs[:, u % 2, kt, pair, :], rhs, start=(n == 0), stop=(n == 5))
                            n += 1
                m.then_inc(pv_done, 1)

            scores(0)
            for u in range(NU):
                if u + 1 < NU:
                    scores(u + 1)
                turn_probs(u)
                if u:
                    times_values(u - 1)
            times_values(NU - 1)

            def shift(t):
                for j in range(2):
                    b = 2 * t + j
                    pe.wait_ge(on_ready, b + 1)
                    for h2 in range(2):
                        dst = ps[64 * j:64 * j + 64, t, 0:D].rearrange(
                            "q (o h d) -> q o h d", h=2, d=XD)[:, :, h2, :]
                        m = pe.matmul(dst, ident[:, 64 * h2:64 * h2 + 64], on[:, b, :, :], start=True, stop=True)
                m.then_inc(sh_done, 1)

            pe.wait_ge(exp_ready, NU)
            for t in range(NT):
                shift(t)

            pe.wait_ge(pt_lo_out, 2 * NU)
            turn_tiles(0, 4, (x2t_done, NT))
            turn_tiles(2, 5, (x2t_done, NT))
            pe.wait_ge(x2t_out, 2)
            pe.wait_ge(m_out, 1)
            for i, (bank, done) in enumerate(((6, sq_done), (2, sk_done))):
                for oc in range(DC):
                    for_bank = ps[:, bank + oc, :]
                    m = pe.matmul(for_bank, mbd[:, i, oc, :], xnT[:, oc, :], start=True, stop=True)
                m.then_inc(done, 1)
            pe.wait_ge(x1_ready, NT)
            for t in range(NT):
                for c in range(DC):
                    m = pe.matmul(ps[:, t // 2, (t % 2) * D + c * P:(t % 2) * D + (c + 1) * P],
                                  xnT[:, c, t * P:(t + 1) * P], mbd[:, 2, c, :], start=True, stop=True)
                if t % 2:
                    m.then_inc(sv_done, 1)
            pe.wait_ge(sqbd_ready, 1)
            pe.wait_ge(sk_lo_out, 1)
            for t in range(NT):
                for k in range(8):
                    c, pr, j = k // 4, k // 2 % 2, k % 2
                    b = 2 * t + j
                    dst = ps[:, 4 + t, k * SQ:(k + 1) * SQ]
                    lh = s_qbd_hi[:, c, b, 2 * pr:2 * pr + 2, :]
                    ll = s_qbd_lo[:, c, b, 2 * pr:2 * pr + 2, :]
                    kh = s_kh[:, c, b * SQ:(b + 1) * SQ]
                    kl = s_kl[:, c, b * SQ:(b + 1) * SQ]
                    pe.matmul(dst, ll, kh, start=True, stop=False)
                    pe.matmul(dst, lh, kl, start=False, stop=False)
                    m = pe.matmul(dst, lh, kh, start=False, stop=True)
                m.then_inc(ssc_done, 1)
            pe.wait_ge(sv_lo_out, 2)
            for t in range(NT):
                pe.wait_ge(sexp_ready, t + 1)
                if t >= 2:
                    pe.wait_ge(spt_lo_out, t - 1)
                for k in range(4):
                    m = pe.transpose(ps[:, t % 2, k * P:(k + 1) * P],
                                     s_sc[:, t, 2 * k:2 * k + 2, :], ident[:, :])
                m.then_inc(spt_done, 1)
                pe.wait_ge(spt_lo_out, t + 1)
                if t == 1:
                    pe.wait_ge(ssub_ready, 2)
                if t >= 2:
                    pe.wait_ge(son_ready, t - 1)
                for k in range(8):
                    c, pr, j = k // 4, k // 2 % 2, k % 2
                    rows = slice(64 * j, 64 * j + 64)
                    feats = slice(c * P + pr * 2 * DH, c * P + (pr + 1) * 2 * DH)
                    dst = ps[:, 2 + 2 * (t % 2) + j, (k // 2) * 2 * DH:(k // 2 + 1) * 2 * DH]
                    ph, pl = s_pTh[rows, t, k // 2, :], s_pTl[rows, t, k // 2, :]
                    pe.matmul(dst, pl, s_vh[rows, t, feats], start=True, stop=False)
                    pe.matmul(dst, ph, s_vl[rows, t, feats], start=False, stop=False)
                    m = pe.matmul(dst, ph, s_vh[rows, t, feats], start=False, stop=True)
                m.then_inc(spv_done, 1)
            for t in range(NT):
                pe.wait_ge(son_ready, t + 1)
                if t >= 2:
                    pe.wait_ge(x2_ready, t - 1)
                for j in range(2):
                    for h2 in range(2):
                        dst = ps[64 * j:64 * j + 64, 6 + t % 2, 0:D].rearrange(
                            "q (k h d) -> q k h d", h=2, d=DH)[:, :, h2, :]
                        src = s_on[:, t].rearrange("p (k j) d -> p k j d", j=2)[:, :, j, :]
                        m = pe.matmul(dst, ident[:, 64 * h2:64 * h2 + 64], src, start=True, stop=True)
                m.then_inc(ssh_done, 1)

            turn_tiles(0, 0, (x3t_done, 2 * NT))
            turn_tiles(2, 1, (x3t_done, 2 * NT))
            pe.wait_ge(x3t_out, 2)
            pe.wait_ge(in_router, 32)
            for hc in range(HC):
                if hc >= 2:
                    pe.wait_ge(r1_out, hc - 1)
                for dc in range(DC):
                    m = pe.matmul(ps[:, 2 + hc % 2, :], rw1_sb[:, dc, hc * P:(hc + 1) * P], xnT[:, dc, :],
                                  start=(dc == 0), stop=(dc == DC - 1))
                m.then_inc(r1_done, 1)
            pe.wait_ge(r1_out, HC)
            for t in range(NT):
                for hc in range(HC):
                    m = pe.matmul(ps[:, 0, t * E:(t + 1) * E], hT[:, hc, t * P:(t + 1) * P], rw2_sb[:, hc, :],
                                  start=(hc == 0), stop=(hc == HC - 1))
            m.then_inc(lg_done, 1)

            def hidden(e):
                pe.wait_ge(in_e[e % RING], 32 * (e // RING + 1))
                for hc in range(HC):
                    k = e * HC + hc
                    if k >= 2:
                        pe.wait_ge(h_out, k - 1)
                    for dc in range(DC):
                        m = pe.matmul(ps[:, 2 + hc % 2, :], w1_sb[:, e % RING, dc, hc * P:(hc + 1) * P],
                                      xnT[:, dc, :], start=(dc == 0), stop=(dc == DC - 1))
                    m.then_inc(h_done, 1)

            def output(e):
                pe.wait_ge(h_out, (e + 1) * HC)
                for t in range(NT):
                    bank = 4 + 2 * (e % 2) + t // 2
                    if e >= 2 and t % 2 == 0:
                        pe.wait_ge(y_out, 4 * (e - 2) + t + 2)
                    for hc in range(HC):
                        m = pe.matmul(ps[:, bank, (t % 2) * D:(t % 2 + 1) * D], hT[:, hc, t * P:(t + 1) * P],
                                      w2_sb[:, e % RING, hc, :], start=(hc == 0), stop=(hc == HC - 1))
                    if t % 2:
                        m.then_inc(y_done, 1)

            hidden(0)
            pe.wait_ge(we_ready, 1)
            for t in range(NT):
                m = pe.transpose(ps[0:E, 1, t * P:(t + 1) * P], we[:, t, :], ident[:, :])
            m.then_inc(wet_done, 1)
            pe.wait_ge(wet_out, 1)
            for t in range(NT):
                m = pe.matmul(ps[:, t // 2, (t % 2) * D:(t % 2 + 1) * D], weT[:, t, :], b2_sb[:, :],
                              start=True, stop=True)
            m.then_inc(b2_done, 1)
            output(0)
            for e in range(1, E):
                hidden(e)
                output(e)

        @block.scalar
        def _(act):
            for i in range(2):
                act.wait_ge(xt_done, i + 1)
                act.copy(xnT[:, :, 2 * i * P:(2 * i + 2) * P], ps[:, 4 + i, :].rearrange("p (c n) -> p c n", c=DC)).then_inc(xt_out, 1)
            for n in range(4):
                act.wait_ge(ct_done, 2 * n + 2)
                if n >= 2:
                    act.wait_ge(v_done, 2 * (n - 1))
                act.copy(ctxT[:, :, n % 2, 2 * P:4 * P], ps[:, 1, :].rearrange("p (c n) -> p c n", c=DC)).then_inc(ct_out_a, 1)
                for oc in range(DC):
                    act.wait_ge(k_done, DC * n + oc + 1)
                    act.wait_ge(wt_out, 4)
                    act.activation(kT_hi[:, oc, n * 512:(n + 1) * 512], ps[:, 2 + oc, :], ACT.Identity,
                                   bias=biasT[:, KB + oc:KB + oc + 1]).then_inc(k_hi_out, 1)
                for j in range(2):
                    act.wait_ge(v_done, 2 * n + j + 1)
                    if n == 0:
                        act.wait_ge(consts, 12)
                    t = 4 * n + 2 * j
                    act.copy(v_hi[:, t:t + 2, :, 0:XD],
                             ps[:, 4 + j, :].rearrange("p (t h d) -> p t h d", t=2, d=XD)).then_inc(v_hi_out, 1)
            def exps(u):
                act.wait_ge(max_ready, u + 1)
                if u >= 2:
                    act.wait_ge(pt_done, 2 * (u - 1))
                for pair in range(PAIRS):
                    m = act.activation(prob[:, u % 2, pair, :],
                                       ps[:, 2 * (u % 2) + pair // 2, (pair % 2) * SK:(pair % 2 + 1) * SK],
                                       ACT.Exp, bias=nmax[:, u, pair:pair + 1])
                m.then_inc(exp_ready, 1)

            exps(0)
            for u in range(NU):
                if u + 1 < NU:
                    exps(u + 1)
                for kt in range(2):
                    act.wait_ge(pt_done, 2 * u + kt + 1)
                    if u >= 2:
                        act.wait_ge(pv_done, u - 1)
                    act.copy(pT_hi[:, u % 2, kt], ps[:, 4 + kt, :].rearrange("p (g q) -> p g q", g=PAIRS)).then_inc(pt_hi_out, 1)
            for i in range(2):
                act.wait_ge(x2t_done, i + 1)
                act.copy(xnT[:, :, 2 * i * P:(2 * i + 2) * P], ps[:, 4 + i, :].rearrange("p (c n) -> p c n", c=DC)).then_inc(x2t_out, 1)
            act.wait_ge(sk_done, 1)
            for oc in range(DC):
                m = act.activation(s_kh[:, oc, :], ps[:, 2 + oc, :], ACT.Identity, bias=biasT[:, SKB + oc:SKB + oc + 1])
            m.then_inc(sk_hi_out, 1)
            for i in range(2):
                act.wait_ge(sv_done, i + 1)
                act.copy(s_vh[:, 2 * i:2 * i + 2, :], ps[:, i, :].rearrange("p (t d) -> p t d", t=2)).then_inc(sv_hi_out, 1)
            for t in range(NT):
                act.wait_ge(ssub_ready, t + 1)
                act.activation(s_sc[:, t], s_sc[:, t], ACT.Exp).then_inc(sexp_ready, 1)
            for t in range(NT):
                act.wait_ge(spt_done, t + 1)
                act.copy(s_pTh[:, t], ps[:, t % 2, :].rearrange("p (g q) -> p g q", g=4)).then_inc(spt_hi_out, 1)
            for i in range(2):
                act.wait_ge(x3t_done, i + 1)
                act.copy(xnT[:, :, 2 * i * P:(2 * i + 2) * P], ps[:, i, :].rearrange("p (c n) -> p c n", c=DC)).then_inc(x3t_out, 1)
            for hc in range(HC):
                act.wait_ge(r1_done, hc + 1)
                act.activation(hT[:, hc, :], ps[:, 2 + hc % 2, :], ACT.Silu, bias=biasT[:, RB + hc:RB + hc + 1]).then_inc(r1_out, 1)

            def hidden(e):
                for hc in range(HC):
                    k = e * HC + hc
                    act.wait_ge(h_done, k + 1)
                    if e:
                        act.wait_ge(y_done, 2 * e)
                    else:
                        act.wait_ge(lg_done, 1)
                    act.activation(hT[:, hc, :], ps[:, 2 + hc % 2, :], ACT.Silu, bias=biasT[:, EB + k:EB + k + 1]).then_inc(h_out, 1)

            act.wait_ge(gap_ready, 1)
            act.activation(th[:, :], gap[:, :], ACT.Tanh, scale=0.5).then_inc(th_ready, 1)
            for e in range(E):
                hidden(e)

        @block.vector
        def _(dve):
            step = [0]

            def link(ins):
                step[0] += 1
                ins.then_inc(dve_step, 1)
                dve.wait_ge(dve_step, step[0])

            def norm_stats(n, t):
                link(dve.bn_stats(stats[:, n, t, :], xs[:, t, :]))
                link(dve.bn_aggr(mv[:, n, t, :], stats[:, n, t, :]))
                dve.tensor_scalar(vareps[:, n, t:t + 1], mv[:, n, t, 1:2], EPS, None, ALU.add).then_inc(var_ready, 1)

            def norm_apply(n, t):
                dve.wait_ge(rstd_ready, n * NT + t + 1)
                dve.tensor_scalar(xn[:, t, :], xs[:, t, :], mv[:, n, t, 0:1], rstd[:, n, t:t + 1],
                                  ALU.subtract, ALU.mult).then_inc(xn_ready, 1)

            dve.wait_ge(in_x, 16)
            for t in range(NT):
                norm_stats(0, t)
            for t in range(NT):
                norm_apply(0, t)
            for i in range(3):
                dve.wait_ge(wt_done, i + 1)
                dve.tensor_copy(wT[:, i], ps[:, i, :].rearrange("p (c n) -> p c n", c=DC)).then_inc(wt_out, 1)
            dve.wait_ge(wt_done, 4)
            dve.tensor_copy(biasT[:, :], ps[:, 3, 0:NB]).then_inc(wt_out, 1)
            dve.wait_ge(in_mask, 16)
            dve.tensor_scalar(mask_row[:, :], mask_i[:, :], 0.0, MASKED, ALU.is_gt, ALU.mult).then_inc(mask_ready, 1)
            dve.wait_ge(wt_out, 4)
            for oc in range(DC):
                dve.wait_ge(q_done, oc + 1)
                link(dve.tensor_scalar(q32[:, oc, :], ps[:, 6 + oc, :], biasT[:, QB + oc:QB + oc + 1], XSCALE,
                                       ALU.add, ALU.mult))
                link(dve.tensor_copy(qh[:, oc, :], q32[:, oc, :]))
                dve.tensor_tensor(ql[:, oc, :], q32[:, oc, :], qh[:, oc, :], ALU.subtract).then_inc(q_out, 1)
            dve.wait_ge(q_out, DC)
            dve.wait_ge(consts, 7)

            def spread_queries(oc, heads):
                for h in heads:
                    for src, dst in ((qh, qbd_hi), (ql, qbd_lo)):
                        m = dve.tensor_scalar(dst[:, oc, :, h, :], src[:, oc, :].rearrange("p (b q) -> p b q", b=B),
                                              headmask[:, h:h + 1], None, ALU.mult)
                return m

            for n in range(4):
                dve.wait_ge(ct_done, 2 * n + 1)
                if n >= 2:
                    dve.wait_ge(v_done, 2 * (n - 1))
                dve.tensor_copy(ctxT[:, :, n % 2, 0:2 * P], ps[:, 0, :].rearrange("p (c n) -> p c n", c=DC)).then_inc(ct_out_d, 1)
                for oc in range(DC):
                    dve.wait_ge(k_hi_out, DC * n + oc + 1)
                    dve.scalar_tensor_tensor(out=kT_lo[:, oc, n * 512:(n + 1) * 512], in0=ps[:, 2 + oc, :],
                                             scalar=biasT[:, KB + oc:KB + oc + 1],
                                             in1=kT_hi[:, oc, n * 512:(n + 1) * 512],
                                             op0=ALU.add, op1=ALU.subtract).then_inc(k_lo_out, 1)
                for j in range(2):
                    dve.wait_ge(v_hi_out, 2 * n + j + 1)
                    t = 4 * n + 2 * j
                    dve.tensor_tensor(v_lo[:, t:t + 2, :, 0:XD],
                                      ps[:, 4 + j, :].rearrange("p (t h d) -> p t h d", t=2, d=XD),
                                      v_hi[:, t:t + 2, :, 0:XD], ALU.subtract).then_inc(v_lo_out, 1)
                half = range(4 * (n % 2), 4 * (n % 2) + 4)
                m = spread_queries(n // 2, half)
                if n % 2:
                    m.then_inc(qbd_ready, 1)
            dve.wait_ge(ut_done, 1)
            dve.tensor_copy(uT[:, 0:2], ps[:, 6, :].rearrange("p (i c n) -> p i c n", i=2, c=DC))
            dve.tensor_copy(uT[:, 2], ps[:, 7, 0:DC * P].rearrange("p (c n) -> p c n", c=DC)).then_inc(ut_out, 1)
            dve.wait_ge(m_done, 1)
            dve.tensor_copy(mbd[:, 0:2], ps[:, 6, :].rearrange("p (i c n) -> p i c n", i=2, c=DC))
            dve.tensor_copy(mbd[:, 2], ps[:, 7, 0:DC * P].rearrange("p (c n) -> p c n", c=DC)).then_inc(m_out, 1)
            dve.wait_ge(in_misc, 64)
            for t in range(NT):
                m = dve.tensor_tensor(xs[:, t, :], xs[:, t, :], vb_all[:, :], ALU.add)
            link(m)

            def maxima(u):
                dve.wait_ge(sc_done, u + 1)
                dve.tensor_reduce(nmax[:, u, :],
                                  ps[:, 2 * (u % 2):2 * (u % 2) + 2, :].rearrange("p a (i k) -> p (a i) k", i=2),
                                  AX.X, ALU.max, negate=True).then_inc(max_ready, 1)

            def normalise(b):
                dve.wait_ge(pv_done, DC * (b + 1))
                o = ps[:, 6 + b % 2, 0:DC * PAIRS * 2 * VW].rearrange("p (o h d) -> p o h d", h=2, d=VW)
                for h2 in range(2):
                    r = slice(64 * h2, 64 * h2 + 64)
                    m = dve.reciprocal(orec[r, b, :], o[r, :, h2, XD])
                link(m)
                for h2 in range(2):
                    r = slice(64 * h2, 64 * h2 + 64)
                    m = dve.tensor_tensor(on[r, b], o[r, :, h2, 0:XD],
                                          orec[r, b, :].unsqueeze(2).broadcast_to([64, DC * PAIRS, XD]), ALU.mult)
                m.then_inc(on_ready, 1)

            maxima(0)
            for u in range(NU):
                if u + 1 < NU:
                    maxima(u + 1)
                for kt in range(2):
                    dve.wait_ge(pt_hi_out, 2 * u + kt + 1)
                    dve.tensor_tensor(pT_lo[:, u % 2, kt], ps[:, 4 + kt, :].rearrange("p (g q) -> p g q", g=PAIRS),
                                      pT_hi[:, u % 2, kt], ALU.subtract).then_inc(pt_lo_out, 1)
                if u >= DC and u % DC == 0:
                    normalise(u // DC - 1)
            normalise(B - 1)

            for t in range(NT):
                dve.wait_ge(sh_done, t + 1)
                m = dve.tensor_tensor(xs[:, t, :], ps[:, t, 0:D], xs[:, t, :], ALU.add)
                m.then_inc(x1_ready, 1)
                dve.wait_ge(x1_ready, t + 1)
                norm_stats(1, t)
            for t in range(NT):
                norm_apply(1, t)
            for t in range(NT):
                m = dve.tensor_tensor(xs[:, t, :], xs[:, t, :], bv_all[:, :], ALU.add)
            link(m)
            dve.wait_ge(sq_done, 1)
            for oc in range(DC):
                link(dve.tensor_scalar(s_q32[:, oc, :], ps[:, 6 + oc, :], biasT[:, SQB + oc:SQB + oc + 1], SSCALE,
                                       ALU.add, ALU.mult))
            link(dve.tensor_copy(s_qh[:, :, :], s_q32[:, :, :]))
            link(dve.tensor_tensor(s_ql[:, :, :], s_q32[:, :, :], s_qh[:, :, :], ALU.subtract))
            for oc in range(DC):
                for h in range(P // DH):
                    for src, dst in ((s_qh, s_qbd_hi), (s_ql, s_qbd_lo)):
                        m = dve.tensor_scalar(dst[:, oc, :, h, :], src[:, oc, :].rearrange("p (b q) -> p b q", b=B),
                                              blockmask[:, h:h + 1], None, ALU.mult)
            m.then_inc(sqbd_ready, 1)
            dve.wait_ge(sk_hi_out, 1)
            for oc in range(DC):
                m = dve.scalar_tensor_tensor(out=s_kl[:, oc, :], in0=ps[:, 2 + oc, :],
                                             scalar=biasT[:, SKB + oc:SKB + oc + 1], in1=s_kh[:, oc, :],
                                             op0=ALU.add, op1=ALU.subtract)
            m.then_inc(sk_lo_out, 1)
            for i in range(2):
                dve.wait_ge(sv_hi_out, i + 1)
                dve.tensor_tensor(s_vl[:, 2 * i:2 * i + 2, :], ps[:, i, :].rearrange("p (t d) -> p t d", t=2),
                                  s_vh[:, 2 * i:2 * i + 2, :], ALU.subtract).then_inc(sv_lo_out, 1)
            for t in range(NT):
                dve.wait_ge(ssc_done, t + 1)
                s = ps[:, 4 + t, :].rearrange("p (k q) -> p k q", k=8)
                link(dve.tensor_reduce(s_max[:, t, :], s, AX.X, ALU.max))
                dve.tensor_tensor(s_sc[:, t], s, s_max[:, t, :].unsqueeze(2).broadcast_to([P, 8, SQ]),
                                  ALU.subtract).then_inc(ssub_ready, 1)
            for t in range(NT):
                dve.wait_ge(sexp_ready, t + 1)
                link(dve.tensor_reduce(s_sum[:, t, :], s_sc[:, t], AX.X, ALU.add))
                link(dve.reciprocal(s_rec[:, t, :], s_sum[:, t, :]))
            for t in range(NT):
                dve.wait_ge(spt_hi_out, t + 1)
                dve.tensor_tensor(s_pTl[:, t], ps[:, t % 2, :].rearrange("p (g q) -> p g q", g=4),
                                  s_pTh[:, t], ALU.subtract).then_inc(spt_lo_out, 1)
                dve.wait_ge(spv_done, t + 1)
                o = ps[:, 2 + 2 * (t % 2):4 + 2 * (t % 2), 0:D].rearrange("p j (k h d) -> p j k h d", k=4, h=2)
                for h2 in range(2):
                    r = slice(64 * h2, 64 * h2 + 64)
                    for j in range(2):
                        m = dve.tensor_tensor(s_on[r, t].rearrange("p (k j) d -> p k j d", j=2)[:, :, j, :],
                                              o[r, j, :, h2, :],
                                              s_rec[r, t, j::2].unsqueeze(2).broadcast_to([64, 4, DH]), ALU.mult)
                m.then_inc(son_ready, 1)
            for t in range(NT):
                dve.wait_ge(ssh_done, t + 1)
                dve.tensor_tensor(xs[:, t, :], ps[:, 6 + t % 2, 0:D], xs[:, t, :], ALU.add).then_inc(x2_ready, 1)
                dve.wait_ge(x2_ready, t + 1)
                norm_stats(2, t)
            for t in range(NT):
                norm_apply(2, t)

            dve.wait_ge(lg_done, 1)
            link(dve.tensor_tensor(logit[:, :, :], ps[:, 0, 0:NT * E].rearrange("p (t e) -> p t e", t=NT),
                                   rb2_all[:, :].unsqueeze(1).broadcast_to([P, NT, E]), ALU.add))
            for t in range(NT):
                m = dve.max(top[:, t, :], logit[:, t, :])
            link(m)
            dve.tensor_tensor(gap[:, :], top[:, :, 0], top[:, :, 1], ALU.subtract).then_inc(gap_ready, 1)
            for t in range(NT):
                m = dve.max_index(topi[:, t, :], top[:, t, :], logit[:, t, :])
            link(m)
            link(dve.tensor_copy(topf[:, :, :], topi[:, :, :]))
            dve.wait_ge(th_ready, 1)
            dve.tensor_scalar(p1[:, :], th[:, :], 0.5, 0.5, ALU.mult, ALU.add)
            link(dve.tensor_scalar(p2[:, :], th[:, :], -0.5, 0.5, ALU.mult, ALU.add))
            dve.wait_ge(consts, CONSTS)
            for t in range(NT):
                dve.tensor_scalar(we1[:, t, :], iota_f[:, :], topf[:, t, 0:1], p1[:, t:t + 1], ALU.is_equal, ALU.mult)
                m = dve.tensor_scalar(we2[:, t, :], iota_f[:, :], topf[:, t, 1:2], p2[:, t:t + 1], ALU.is_equal, ALU.mult)
            link(m)
            dve.tensor_tensor(we[:, :, :], we1[:, :, :], we2[:, :, :], ALU.add).then_inc(we_ready, 1)
            dve.wait_ge(wet_done, 1)
            dve.tensor_copy(weT[:, :, :], ps[0:E, 1, :].rearrange("e (t n) -> e t n", t=NT)).then_inc(wet_out, 1)
            dve.wait_ge(b2_done, 1)
            for t in range(NT):
                m = dve.tensor_tensor(acc[:, t, :], ps[:, t // 2, (t % 2) * D:(t % 2 + 1) * D], xs[:, t, :], ALU.add)
            link(m)
            for e in range(E):
                for t in range(NT):
                    if t % 2 == 0:
                        dve.wait_ge(y_done, 2 * e + t // 2 + 1)
                    if e:
                        dve.wait_ge(y_out, 4 * (e - 1) + t + 1)
                    dve.scalar_tensor_tensor(out=acc[:, t, :],
                                             in0=ps[:, 4 + 2 * (e % 2) + t // 2, (t % 2) * D:(t % 2 + 1) * D],
                                             scalar=we[:, t, e:e + 1], in1=acc[:, t, :],
                                             op0=ALU.mult, op1=ALU.add).then_inc(y_out, 1)


_INS = ["x", "ctx_1024", "mask_BxS2_ik0", "L0_xattn_q_w", "L0_xattn_q_b", "L0_xattn_k_w", "L0_xattn_k_b",
        "L0_xattn_v_w", "L0_xattn_v_b", "L0_attn_Uq", "L0_attn_Vq", "L0_attn_bq", "L0_attn_Uk", "L0_attn_Vk",
        "L0_attn_bk", "L0_attn_Uv", "L0_attn_Vv", "L0_attn_bv", "L0_ffn_rw1", "L0_ffn_rb1", "L0_ffn_rw2",
        "L0_ffn_rb2", "L0_ffn_w1", "L0_ffn_b1", "L0_ffn_w2", "L0_ffn_b2"]
_OUT = ((8, 64, 256), "float32")


def kernel(**inputs):
    import numpy as _np
    import concourse.bacc as _bacc
    from concourse import mybir as _mybir
    from concourse.bass_utils import run_bass_kernel_spmd as _run

    nc = _bacc.Bacc("TRN2", target_bir_lowering=False, num_devices=1)
    arrays, args = {}, []
    for name in _INS:
        a = _np.ascontiguousarray(inputs[name])
        arrays[f"in_{name}_dram"] = a
        args.append(nc.dram_tensor(f"in_{name}_dram", a.shape, _mybir.dt.from_np(a.dtype), kind="ExternalInput").ap())
    args.append(nc.dram_tensor("out_0_dram", _OUT[0], _mybir.dt.from_np(_np.dtype(_OUT[1])), kind="ExternalOutput").ap())
    perceiver_layer(nc, *args)
    r = _run(nc, [arrays], core_ids=[0])
    return r.results[0]["out_0_dram"]
```

```python
from contextlib import ExitStack

import concourse.bass as bass
from concourse import mybir

F32 = mybir.dt.float32
F16 = mybir.dt.float16
BF16 = mybir.dt.bfloat16
I32 = mybir.dt.int32
U32 = mybir.dt.uint32
ALU = mybir.AluOpType
ACT = mybir.ActivationFunctionType
AX = mybir.AxisListType

P = 128
EPS = 1e-5
MASKED = -1e30


def perceiver_layer(nc, x, ctx_in, mask, q_w, q_b, k_w, k_b, v_w, v_b, Uq, Vq, bq, Uk, Vk, bk, Uv, Vv, bv,
                    rw1, rb1, rw2, rb2, w1, b1, w2, b2, out):
    B, SQ, D = x.shape
    SK = ctx_in.shape[1]
    XH = 16
    XD = D // XH
    H, DH, R = Uq.shape
    E, _, HID = w1.shape
    DC = D // P
    NT = B * SQ // P
    KT = B * SK // P
    HC = HID // P
    NTOK = B * SQ
    NU = B * DC
    PAIRS = P // XD // 2
    NBLK = 15
    WSCALE = 64.0
    NCHUNK = 1 + 2 * E
    STAGE = 3
    XSCALE = XD ** -0.5
    SSCALE = DH ** -0.5
    VW = XD + 1

    es = ExitStack()
    with es:
        def sb(name, shape, dt=F32):
            return es.enter_context(nc.sbuf_tensor(name, shape, dt))

        def sem(name):
            return es.enter_context(nc.semaphore(name))

        xs = sb("xs", [P, NT, D])
        xn = sb("xn", [P, NT, D])
        xnT = sb("xnT", [P, DC, NTOK])
        stats = sb("stats", [P, 3, NT, 6])
        mv = sb("mv", [P, 3, NT, 2])
        vareps = sb("vareps", [P, 3, NT])
        rstd = sb("rstd", [P, 3, NT])
        minus_half = sb("minus_half", [P, NT])
        ident = sb("ident", [P, P])
        ident16 = sb("ident16", [P, P], F16)
        before = sb("before", [P, P], F16)
        ones16 = sb("ones16", [P, P], F16)
        headmask = sb("headmask", [P, P // XD])
        blockmask = sb("blockmask", [P, P // DH])
        iota_f = sb("iota_f", [P, NBLK])
        slot_ids = sb("slot_ids", [P, NBLK * P], F16)
        ones_row = sb("ones_row", [1, P], BF16)
        NB = 4 * DC + HC + E * HC
        biasT = sb("biasT", [P, NB])
        bv_all = sb("bv_all", [P, D])
        rb2_all = sb("rb2_all", [P, E])
        b2_sb = sb("b2_sb", [E, D])
        stage = sb("stage", [P, STAGE, DC * HID])
        rw2_sb = sb("rw2_sb", [P, HC, E])
        rw2p = sb("rw2p", [P, 2, HC, E], F16)
        x3p = sb("x3p", [P, 2, NT, D], F16)
        x3T = xnT[:, :, :].rearrange("p c n -> p (c n)").bitcast(F16).rearrange("p (l c n) -> p l c n", l=2, c=DC)
        logit = sb("logit", [P, NT, E])
        top = sb("top", [P, NT, 8])
        topi = sb("topi", [P, NT, 8], U32)
        topf = sb("topf", [P, NT, 8])
        gap = sb("gap", [P, NT])
        th = sb("th", [P, NT])
        p1 = sb("p1", [P, NT])
        p2 = sb("p2", [P, NT])
        pick = sb("pick", [P, 2, NT, E])
        picked = sb("picked", [P, NT, E], F16)
        we1 = sb("we1", [P, NT, E])
        we2 = sb("we2", [P, NT, E])
        we = sb("we", [P, NT, E])
        wep = sb("wep", [P, NT, E, 2], F16)
        weT = sb("weT", [E, NT, P])
        count = sb("count", [P, E])
        nblk = sb("nblk", [P, 3, E])
        nincl = sb("nincl", [P, E])
        first = sb("first", [P, E])
        gslot = sb("gslot", [P, NT, E])
        slot12 = sb("slot12", [P, 2, NT, E])
        slot = sb("slot", [P, 2, NT])
        owner3 = sb("owner3", [1, NBLK, E])
        owner_f = sb("owner_f", [1, NBLK])
        owner = sb("owner", [1, NBLK + 1], I32)
        onehot = sb("onehot", [P, 3, NT, P], F16)
        onehotT = sb("onehotT", [P, 4, NTOK], F16)
        xg = sb("xg", [P, 2, 2, DC, P], F16)
        h32 = sb("h32", [P, 2, 4 * P])
        hp = sb("hp", [P, 2, 2, HC, P], F16)
        rw1p = hp[:, :, :, :, :].rearrange("p a l c n -> p (a l c n)").rearrange("p (l c n) -> p l c n", l=2, c=DC)
        wslot = sb("wslot", [P, NBLK])
        y32 = sb("y32", [P, 2, D])
        yp = sb("yp", [P, 2, 2, D], F16)

        attn = es.enter_context(ExitStack())

        def asb(name, shape, dt=F32):
            return attn.enter_context(nc.sbuf_tensor(name, shape, dt))

        ctx_ring = asb("ctx_ring", [P, 8, NTOK])
        ctx_sb = ctx_ring[:, 0:4].rearrange("p a n -> p (a n)").rearrange("p (g k d) -> p g k d", g=2, d=D)
        ctxT = ctx_ring[:, 4:8].rearrange("p (c g) n -> p c g n", g=2)
        wT = asb("wT", [P, 3, DC, D])
        wraw = asb("wraw", [P, 3, DC, D])
        uvbd = wraw[:, :, :, :].rearrange("p i c d -> p (i c d)").rearrange("p (i c d) -> p i c d", i=6, d=P)
        uT = asb("uT", [P, 3, DC, P])
        uv = asb("uv", [P, 6, DC, R])
        brow = asb("brow", [NB, P])
        mbd = asb("mbd", [P, 3, DC, P])
        vb_all = asb("vb_all", [P, D])
        mask_row = asb("mask_row", [1, B * SK], BF16)
        kT_hi = asb("kT_hi", [P, DC, B * SK], F16)
        kT_lo = asb("kT_lo", [P, DC, B * SK], F16)
        v_hi = asb("v_hi", [P, KT, XH, VW], F16)
        v_lo = asb("v_lo", [P, KT, XH, VW], F16)
        q32 = xn[:, :, :].rearrange("p t d -> p (t d)").rearrange("p (c n) -> p c n", c=DC)
        qh = asb("qh", [P, DC, NTOK], F16)
        ql = asb("ql", [P, DC, NTOK], F16)
        qbd_hi = asb("qbd_hi", [P, DC, B, P // XD, SQ], F16)
        qbd_lo = asb("qbd_lo", [P, DC, B, P // XD, SQ], F16)
        nmax = asb("nmax", [P, NU, PAIRS])
        prob = asb("prob", [P, 2, PAIRS, SK])
        mask_i = prob[0:1].rearrange("p u g k -> p (u g k)").bitcast(I32)
        pT_hi = asb("pT_hi", [P, 2, 2, PAIRS, P], F16)
        pT_lo = asb("pT_lo", [P, 2, 2, PAIRS, P], F16)
        orec = asb("orec", [P, B, DC * PAIRS])
        on = onehotT[:, :, :].rearrange("p a n -> p (a n)").bitcast(F32).rearrange("p (b o d) -> p b o d", b=B, d=XD)
        s_q32, s_qh, s_ql = q32, qh, ql
        s_qbd_hi, s_qbd_lo = qbd_hi[:, :, :, 0:P // DH, :], qbd_lo[:, :, :, 0:P // DH, :]
        s_kh, s_kl = kT_hi[:, :, 0:NTOK], kT_lo[:, :, 0:NTOK]
        s_vh, s_vl = (a[:, 0:4].rearrange("p t h d -> p (t h d)")[:, 0:NT * D].rearrange("p (t d) -> p t d", d=D)
                      for a in (v_hi, v_lo))
        s_max = asb("s_max", [P, NT, 8])
        s_sc = prob[:, :, :, :].rearrange("p u g k -> p (u g k)").rearrange("p (t k q) -> p t k q", t=NT, q=SQ)
        s_sum = asb("s_sum", [P, NT, 8])
        s_rec = asb("s_rec", [P, NT, 8])
        s_pTh, s_pTl = (a[:, :, :, :, :].rearrange("p u k g q -> p (u k) g q") for a in (pT_hi, pT_lo))
        s_on = on.rearrange("p b o d -> p (b o d)").rearrange("p (t k d) -> p t k d", t=NT, d=DH)
        attn.close()

        wp = sb("wp", [P, E, 4, DC * HID], F16)
        rh = wp[:, E - 1].rearrange("p l n -> p (l n)").rearrange("p (l c n) -> p l c n", l=2, c=HC)

        ps = es.enter_context(nc.psum_tensor("ps", [P, 8, 512], F32))

        in_x, in_brow, in_mask, in_uv, in_misc, in_vb = (
            sem(n) for n in ("in_x", "in_brow", "in_mask", "in_uv", "in_misc", "in_vb"))
        in_w = [sem(f"in_w{i}") for i in range(3)]
        in_ctx = [sem(f"in_ctx{i}") for i in range(4)]
        in_stage = [sem(f"in_stage{i}") for i in range(STAGE)]
        in_rw2 = sem("in_rw2")
        consts = sem("consts")
        bd_ready = sem("bd_ready")
        rstd_ready = sem("rstd_ready")
        var_ready = sem("var_ready")
        xn_ready = sem("xn_ready")
        dve_step = sem("dve_step")
        mask_ready = sem("mask_ready")
        wt_done = sem("wt_done")
        wt_out = sem("wt_out")
        xt_done = sem("xt_done")
        xt_out = sem("xt_out")
        q_done = sem("q_done")
        q_out = sem("q_out")
        qbd_ready = sem("qbd_ready")
        ct_done = sem("ct_done")
        ct_out_d = sem("ct_out_d")
        ct_out_a = sem("ct_out_a")
        k_done = sem("k_done")
        k_hi_out = sem("k_hi_out")
        k_lo_out = sem("k_lo_out")
        v_done = sem("v_done")
        v_hi_out = sem("v_hi_out")
        v_lo_out = sem("v_lo_out")
        ut_done = sem("ut_done")
        ut_out = sem("ut_out")
        m_done = sem("m_done")
        m_out = sem("m_out")
        sc_done = sem("sc_done")
        max_ready = sem("max_ready")
        exp_ready = sem("exp_ready")
        pt_done = sem("pt_done")
        pt_hi_out = sem("pt_hi_out")
        pt_lo_out = sem("pt_lo_out")
        pv_done = sem("pv_done")
        on_ready = sem("on_ready")
        sh_done = sem("sh_done")
        x1_ready = sem("x1_ready")
        x2t_done = sem("x2t_done")
        x2t_out = sem("x2t_out")
        sq_done = sem("sq_done")
        sk_done = sem("sk_done")
        sv_done = sem("sv_done")
        sq_out = sem("sq_out")
        sqbd_ready = sem("sqbd_ready")
        sk_hi_out = sem("sk_hi_out")
        sk_lo_out = sem("sk_lo_out")
        sv_hi_out = sem("sv_hi_out")
        sv_lo_out = sem("sv_lo_out")
        ssc_done = sem("ssc_done")
        ssub_ready = sem("ssub_ready")
        sexp_ready = sem("sexp_ready")
        spt_done = sem("spt_done")
        spt_hi_out = sem("spt_hi_out")
        spt_lo_out = sem("spt_lo_out")
        spv_done = sem("spv_done")
        son_ready = sem("son_ready")
        ssh_done = sem("ssh_done")
        x2_ready = sem("x2_ready")
        x3t_done = sem("x3t_done")
        x3t_hi_out = sem("x3t_hi_out")
        x3t_lo_out = sem("x3t_lo_out")
        x3p_ready = sem("x3p_ready")
        split_hi = sem("split_hi")
        split_lo = sem("split_lo")
        rw2_ready = sem("rw2_ready")
        r1_done = sem("r1_done")
        r1_act = sem("r1_act")
        r1_hi = sem("r1_hi")
        r1_lo = sem("r1_lo")
        lg_done = sem("lg_done")
        gap_ready = sem("gap_ready")
        th_ready = sem("th_ready")
        picked_ready = sem("picked_ready")
        rank_done = sem("rank_done")
        owner_ready = sem("owner_ready")
        we_ready = sem("we_ready")
        wet_done = sem("wet_done")
        wet_out = sem("wet_out")
        first_choice = sem("first_choice")
        onehot_ready = sem("onehot_ready")
        xg_done = sem("xg_done")
        xg_out = sem("xg_out")
        turn_done = sem("turn_done")
        wslot_sum = sem("wslot_sum")
        turn_out = sem("turn_out")
        h_done = sem("h_done")
        h_act = sem("h_act")
        h_hi = sem("h_hi")
        h_lo = sem("h_lo")
        y_done = sem("y_done")
        y_act = sem("y_act")
        y_hi = sem("y_hi")
        y_pair = sem("y_pair")
        sum_done = sem("sum_done")
        all_summed = sem("all_summed")
        out_ready = sem("out_ready")
        stored = sem("stored")

        block = es.enter_context(nc.Block())

        QB, KB, SQB, SKB, RB, EB = 0, DC, 2 * DC, 3 * DC, 4 * DC, 4 * DC + HC

        CONSTS = 17

        @block.sync
        def _(sp):
            sp.dma_start(xs[:, :, :], x.rearrange("(t b) s d -> (b s) t d", b=2)).then_inc(in_x, 16)
            for i, w in enumerate((q_w, k_w, v_w)):
                sp.dma_start(wraw[:, i], w.rearrange("(c p) d -> p c d", p=P)).then_inc(in_w[i], 16)
            rows = [(q_b, 0), (k_b, DC)]
            for a, r in rows:
                sp.dma_start(brow[r:r + DC, :], a.rearrange("(c p) -> c p", p=P)).then_inc(in_brow, 16)
            for a, r in ((bq, SQB), (bk, SKB)):
                sp.dma_start(brow[r:r + DC, :], a.rearrange("(c h) d -> c (h d)", c=DC)).then_inc(in_brow, 16)
            sp.dma_start(brow[RB:RB + HC, :], rb1.rearrange("(c p) -> c p", p=P)).then_inc(in_brow, 16)
            sp.dma_start(brow[EB:EB + E * HC, :], b1.rearrange("e (c p) -> (e c) p", p=P)).then_inc(in_brow, 16)
            sp.dma_start(mask_i[:, :], mask.rearrange("b k -> (b k)").unsqueeze(0)).then_inc(in_mask, 16)
            ctx_g = ctx_in.rearrange("b (k p) d -> p (b k) d", p=P)
            for n in range(2):
                sp.dma_start(ctx_sb[:, n], ctx_g[:, 4 * n:4 * n + 4]).then_inc(in_ctx[n], 16)
            for i, a in enumerate((Vq, Vk, Vv, Uq, Uk, Uv)):
                sp.dma_start(uv[:, i], a.rearrange("(c h) r d -> (h r) c d", c=DC)).then_inc(in_uv, 16)
            sp.dma_start(vb_all[:, :], v_b.partition_broadcast(P)).then_inc(in_vb, 16)
            sp.dma_start(bv_all[:, :], bv.rearrange("h d -> (h d)").partition_broadcast(P)).then_inc(in_misc, 16)
            sp.dma_start(rb2_all[:, :], rb2.partition_broadcast(P)).then_inc(in_misc, 16)
            sp.dma_start(b2_sb[:, :], b2).then_inc(in_misc, 16)
            sp.dma_start(rw2_sb[:, :, :], rw2.rearrange("(c p) e -> p c e", p=P)).then_inc(in_rw2, 16)
            for n in range(2, 4):
                sp.wait_ge(ct_done, 2 * (n - 1))
                sp.dma_start(ctx_sb[:, n % 2], ctx_g[:, 4 * n:4 * n + 4]).then_inc(in_ctx[n], 16)
            for k in range(NCHUNK):
                if k >= STAGE:
                    sp.wait_ge(split_lo, k - STAGE + 1)
                if k == 0:
                    src = rw1.rearrange("(c p) h -> p c h", p=P)
                else:
                    src = (w1, w2)[(k - 1) % 2][(k - 1) // 2].rearrange("(c p) h -> p c h", p=P)
                sp.dma_start(stage[:, k % STAGE, :].rearrange("p (c h) -> p c h", c=src.shape[1]),
                             src).then_inc(in_stage[k % STAGE], 16)
            out_v = out.rearrange("(t b) s d -> (b s) t d", b=2)
            for t in range(NT):
                sp.wait_ge(out_ready, t + 1)
                sp.dma_start(out_v[:, t], xn[:, t]).then_inc(stored, 16)
            sp.wait_ge(stored, 16 * NT)

        @block.gpsimd
        def _(pool):
            step = [0]

            def link(ins):
                step[0] += 1
                ins.then_inc(consts, 1)
                pool.wait_ge(consts, step[0])

            def norm_scale(n, t):
                pool.wait_ge(var_ready, n * NT + t + 1)
                pool.tensor_tensor(rstd[:, n, t:t + 1], vareps[:, n, t:t + 1], minus_half[:, t:t + 1],
                                   ALU.pow).then_inc(rstd_ready, 1)

            link(pool.memset(ident[:, :], 0.0))
            link(pool.affine_select(out=ident[:, :], in_=ident[:, :], compare_op=ALU.not_equal, fill=1.0,
                                    base=0, pattern=[[-1, P]], channel_multiplier=1))
            link(pool.memset(minus_half[:, :], -0.5))
            for t in range(NT):
                norm_scale(0, t)
            link(pool.memset(ones_row[:, :], 1.0))
            for m, width in ((headmask, XD), (blockmask, DH)):
                n = P // width
                link(pool.memset(m[:, :], 1.0))
                link(pool.affine_select(out=m[:, :], in_=m[:, :], compare_op=ALU.is_ge, fill=0.0,
                                        base=0, pattern=[[-width, n]], channel_multiplier=1))
                link(pool.affine_select(out=m[:, :], in_=m[:, :], compare_op=ALU.is_ge, fill=0.0,
                                        base=width - 1, pattern=[[width, n]], channel_multiplier=-1))
            link(pool.memset(v_hi[:, :, :, XD:VW], 1.0))
            link(pool.memset(v_lo[:, :, :, XD:VW], 0.0))
            link(pool.tensor_copy(ident16[:, :], ident[:, :]))
            link(pool.memset(ones16[:, :], 1.0))
            link(pool.affine_select(out=before[:, :], in_=ones16[:, :], compare_op=ALU.is_gt, fill=0.0,
                                    base=0, pattern=[[1, P]], channel_multiplier=-1))
            link(pool.iota(iota_f[:, :], pattern=[[1, NBLK]], base=0, channel_multiplier=0,
                           allow_small_or_imprecise_dtypes=True))
            link(pool.iota(slot_ids[:, :], pattern=[[1, NBLK * P]], base=0, channel_multiplier=0,
                           allow_small_or_imprecise_dtypes=True))
            assert step[0] == CONSTS

            pool.wait_ge(in_uv, 96)
            pool.wait_ge(wt_done, 3)
            for i in range(6):
                pool.tensor_tensor(uvbd[:, i].rearrange("p c (h r) -> p c h r", r=R),
                                   uv[:, i].unsqueeze(2).broadcast_to([P, DC, P // DH, R]),
                                   blockmask[:, :].unsqueeze(1).unsqueeze(3).broadcast_to([P, DC, P // DH, R]),
                                   ALU.mult).then_inc(bd_ready, 1)
            for n in (1, 2):
                for t in range(NT):
                    norm_scale(n, t)
            for t in range(NT):
                pool.wait_ge(xn_ready, 2 * NT + t + 1)
                pool.tensor_copy(x3p[:, 0, t, :], xn[:, t, :]).then_inc(x3p_ready, 1)
                pool.wait_ge(x3p_ready, 2 * t + 1)
                pool.tensor_tensor(x3p[:, 1, t, :], xn[:, t, :], x3p[:, 0, t, :], ALU.subtract).then_inc(x3p_ready, 1)

        @block.tensor
        def _(pe):
            pe.wait_ge(consts, 2)
            for i in range(3):
                pe.wait_ge(in_w[i], 16)
                for dc in range(DC):
                    for oc in range(DC):
                        m = pe.transpose(ps[:, i, (dc * DC + oc) * P:(dc * DC + oc + 1) * P],
                                         wraw[:, i, oc, dc * P:(dc + 1) * P], ident[:, :])
                m.then_inc(wt_done, 1)
            pe.wait_ge(in_brow, 96)
            pe.transpose(ps[:, 3, 0:NB], brow[:, :], ident[0:NB, 0:NB]).then_inc(wt_done, 1)

            def turn_tiles(t, bank, done):
                for j in range(2):
                    pe.wait_ge(xn_ready, done[1] + t + j + 1)
                    for dc in range(DC):
                        m = pe.transpose(ps[:, bank, (dc * 2 + j) * P:(dc * 2 + j + 1) * P],
                                         xn[:, t + j, dc * P:(dc + 1) * P], ident[:, :])
                m.then_inc(done[0], 1)

            turn_tiles(0, 4, (xt_done, 0))
            turn_tiles(2, 5, (xt_done, 0))
            pe.wait_ge(wt_out, 4)
            pe.wait_ge(xt_out, 2)
            for oc in range(DC):
                for dc in range(DC):
                    m = pe.matmul(ps[:, 6 + oc, :], wT[:, 0, dc, oc * P:(oc + 1) * P], xnT[:, dc, :],
                                  start=(dc == 0), stop=(dc == DC - 1))
                m.then_inc(q_done, 1)
            def turn_context(n):
                pe.wait_ge(in_ctx[n], 16)
                if n:
                    pe.wait_ge(ct_out_d, n)
                    pe.wait_ge(ct_out_a, n)
                for j in range(2):
                    for i in range(2):
                        for dc in range(DC):
                            m = pe.transpose(ps[:, j, (dc * 2 + i) * P:(dc * 2 + i + 1) * P],
                                             ctx_sb[:, n % 2, 2 * j + i, dc * P:(dc + 1) * P], ident[:, :])
                    m.then_inc(ct_done, 1)

            turn_context(0)
            for n in range(4):
                if n + 1 < 4:
                    turn_context(n + 1)
                pe.wait_ge(ct_out_d, n + 1)
                pe.wait_ge(ct_out_a, n + 1)
                for oc in range(DC):
                    if n:
                        pe.wait_ge(k_lo_out, DC * (n - 1) + oc + 1)
                    for dc in range(DC):
                        m = pe.matmul(ps[:, 2 + oc, :], wT[:, 1, dc, oc * P:(oc + 1) * P], ctxT[:, dc, n % 2, :],
                                      start=(dc == 0), stop=(dc == DC - 1))
                    m.then_inc(k_done, 1)
                for j in range(2):
                    if n:
                        pe.wait_ge(v_lo_out, 2 * (n - 1) + j + 1)
                    for i in range(2):
                        for dc in range(DC):
                            m = pe.matmul(ps[:, 4 + j, i * D:(i + 1) * D],
                                          ctxT[:, dc, n % 2, (2 * j + i) * P:(2 * j + i + 1) * P], wT[:, 2, dc, :],
                                          start=(dc == 0), stop=(dc == DC - 1))
                    m.then_inc(v_done, 1)
            pe.wait_ge(bd_ready, 6)
            pe.wait_ge(q_out, DC)
            for i in range(3):
                for c in range(DC):
                    k = i * DC + c
                    m = pe.transpose(ps[:, 6 + k // 4, (k % 4) * P:(k % 4 + 1) * P], uvbd[:, 3 + i, c, :], ident[:, :])
            m.then_inc(ut_done, 1)
            pe.wait_ge(ut_out, 1)
            for i in range(3):
                for c in range(DC):
                    k = i * DC + c
                    m = pe.matmul(ps[:, 6 + k // 4, (k % 4) * P:(k % 4 + 1) * P], uvbd[:, i, c, :], uT[:, i, c, :],
                                  start=True, stop=True)
            m.then_inc(m_done, 1)

            def scores(u):
                b, c = divmod(u, DC)
                if u == 0:
                    pe.wait_ge(mask_ready, 1)
                    pe.wait_ge(k_lo_out, 4 * DC)
                    pe.wait_ge(ct_out_a, 4)
                if u < DC:
                    pe.wait_ge(qbd_ready, u + 1)
                if u >= 2:
                    pe.wait_ge(exp_ready, u - 1)
                for half in range(2):
                    bank = 2 * (u % 2) + half
                    pe.matmul(ps[:, bank, :], ones_row[:, :],
                              mask_row[:, b * SK:(b + 1) * SK].unsqueeze(1).broadcast_to([1, 2, SK]),
                              start=True, stop=False, skip_group_check=True)
                    for i in range(2):
                        pair = 2 * half + i
                        dst = ps[:, bank, i * SK:(i + 1) * SK]
                        lh = qbd_hi[:, c, b, 2 * pair:2 * pair + 2, :]
                        ll = qbd_lo[:, c, b, 2 * pair:2 * pair + 2, :]
                        keys = slice(b * SK, (b + 1) * SK)
                        pe.matmul(dst, ll, kT_hi[:, c, keys], start=False, stop=False, skip_group_check=True)
                        pe.matmul(dst, lh, kT_lo[:, c, keys], start=False, stop=False, skip_group_check=True)
                        m = pe.matmul(dst, lh, kT_hi[:, c, keys], start=False, stop=(i == 1),
                                      skip_group_check=True)
                m.then_inc(sc_done, 1)

            def turn_probs(u):
                pe.wait_ge(exp_ready, u + 1)
                for kt in range(2):
                    if u:
                        pe.wait_ge(pt_lo_out, 2 * (u - 1) + kt + 1)
                    else:
                        pe.wait_ge(v_lo_out, 8)
                    for pair in range(PAIRS):
                        m = pe.transpose(ps[:, 4 + kt, pair * P:(pair + 1) * P],
                                         prob[:, u % 2, pair, kt * P:(kt + 1) * P], ident[:, :])
                    m.then_inc(pt_done, 1)

            def times_values(u):
                b, c = divmod(u, DC)
                if u == 0:
                    pe.wait_ge(m_out, 1)
                if c == 0 and b >= 2:
                    pe.wait_ge(on_ready, b - 1)
                pe.wait_ge(pt_lo_out, 2 * u + 2)
                for pair in range(PAIRS):
                    o = c * PAIRS + pair
                    dst = ps[:, 6 + b % 2, o * 2 * VW:(o + 1) * 2 * VW]
                    h0 = 2 * o
                    n = 0
                    for kt in range(2):
                        vh = v_hi[:, 2 * b + kt, h0:h0 + 2, :]
                        vl = v_lo[:, 2 * b + kt, h0:h0 + 2, :]
                        for lhs, rhs in ((pT_lo, vh), (pT_hi, vl), (pT_hi, vh)):
                            m = pe.matmul(dst, lhs[:, u % 2, kt, pair, :], rhs, start=(n == 0), stop=(n == 5))
                            n += 1
                m.then_inc(pv_done, 1)

            scores(0)
            scores(1)
            for u in range(NU):
                turn_probs(u)
                if u + 2 < NU:
                    scores(u + 2)
                if u:
                    times_values(u - 1)
            times_values(NU - 1)

            def shift(t):
                for j in range(2):
                    b = 2 * t + j
                    pe.wait_ge(on_ready, b + 1)
                    for h2 in range(2):
                        dst = ps[64 * j:64 * j + 64, t, 0:D].rearrange(
                            "q (o h d) -> q o h d", h=2, d=XD)[:, :, h2, :]
                        m = pe.matmul(dst, ident[:, 64 * h2:64 * h2 + 64], on[:, b, :, :], start=True, stop=True)
                m.then_inc(sh_done, 1)

            pe.wait_ge(exp_ready, NU)
            for t in range(NT):
                shift(t)

            pe.wait_ge(pt_lo_out, 2 * NU)
            turn_tiles(0, 4, (x2t_done, NT))
            turn_tiles(2, 5, (x2t_done, NT))
            pe.wait_ge(x2t_out, 2)
            pe.wait_ge(m_out, 1)
            for i, (bank, done) in enumerate(((6, sq_done), (2, sk_done))):
                for oc in range(DC):
                    for_bank = ps[:, bank + oc, :]
                    m = pe.matmul(for_bank, mbd[:, i, oc, :], xnT[:, oc, :], start=True, stop=True)
                m.then_inc(done, 1)
            pe.wait_ge(x1_ready, NT)
            for t in range(NT):
                for c in range(DC):
                    m = pe.matmul(ps[:, t // 2, (t % 2) * D + c * P:(t % 2) * D + (c + 1) * P],
                                  xnT[:, c, t * P:(t + 1) * P], mbd[:, 2, c, :], start=True, stop=True)
                if t % 2:
                    m.then_inc(sv_done, 1)
            pe.wait_ge(sqbd_ready, 1)
            pe.wait_ge(sk_lo_out, 1)
            for t in range(NT):
                for k in range(8):
                    c, pr, j = k // 4, k // 2 % 2, k % 2
                    b = 2 * t + j
                    dst = ps[:, 4 + t, k * SQ:(k + 1) * SQ]
                    lh = s_qbd_hi[:, c, b, 2 * pr:2 * pr + 2, :]
                    ll = s_qbd_lo[:, c, b, 2 * pr:2 * pr + 2, :]
                    kh = s_kh[:, c, b * SQ:(b + 1) * SQ]
                    kl = s_kl[:, c, b * SQ:(b + 1) * SQ]
                    pe.matmul(dst, ll, kh, start=True, stop=False)
                    pe.matmul(dst, lh, kl, start=False, stop=False)
                    m = pe.matmul(dst, lh, kh, start=False, stop=True)
                m.then_inc(ssc_done, 1)
            pe.wait_ge(sv_lo_out, 2)
            for t in range(NT):
                pe.wait_ge(sexp_ready, t + 1)
                if t >= 2:
                    pe.wait_ge(spt_lo_out, t - 1)
                for k in range(4):
                    m = pe.transpose(ps[:, t % 2, k * P:(k + 1) * P],
                                     s_sc[:, t, 2 * k:2 * k + 2, :], ident[:, :])
                m.then_inc(spt_done, 1)
                pe.wait_ge(spt_lo_out, t + 1)
                if t == 1:
                    pe.wait_ge(ssub_ready, 2)
                if t >= 2:
                    pe.wait_ge(son_ready, t - 1)
                for k in range(8):
                    c, pr, j = k // 4, k // 2 % 2, k % 2
                    rows = slice(64 * j, 64 * j + 64)
                    feats = slice(c * P + pr * 2 * DH, c * P + (pr + 1) * 2 * DH)
                    dst = ps[:, 2 + 2 * (t % 2) + j, (k // 2) * 2 * DH:(k // 2 + 1) * 2 * DH]
                    ph, pl = s_pTh[rows, t, k // 2, :], s_pTl[rows, t, k // 2, :]
                    pe.matmul(dst, pl, s_vh[rows, t, feats], start=True, stop=False)
                    pe.matmul(dst, ph, s_vl[rows, t, feats], start=False, stop=False)
                    m = pe.matmul(dst, ph, s_vh[rows, t, feats], start=False, stop=True)
                m.then_inc(spv_done, 1)
            for t in range(NT):
                pe.wait_ge(son_ready, t + 1)
                if t >= 2:
                    pe.wait_ge(x2_ready, t - 1)
                for j in range(2):
                    for h2 in range(2):
                        dst = ps[64 * j:64 * j + 64, 6 + t % 2, 0:D].rearrange(
                            "q (k h d) -> q k h d", h=2, d=DH)[:, :, h2, :]
                        src = s_on[:, t].rearrange("p (k j) d -> p k j d", j=2)[:, :, j, :]
                        m = pe.matmul(dst, ident[:, 64 * h2:64 * h2 + 64], src, start=True, stop=True)
                m.then_inc(ssh_done, 1)

            turn_tiles(0, 0, (x3t_done, 2 * NT))
            turn_tiles(2, 1, (x3t_done, 2 * NT))
            pe.wait_ge(x3t_lo_out, 2)
            pe.wait_ge(split_lo, 1)
            pe.wait_ge(split_hi, 1)
            for hc in range(HC):
                if hc >= 2:
                    pe.wait_ge(r1_act, hc - 1)
                n = 0
                for dc in range(DC):
                    for wl, xl in ((1, 0), (0, 1), (0, 0)):
                        m = pe.matmul(ps[:, 2 + hc % 2, :], rw1p[:, wl, dc, hc * P:(hc + 1) * P], x3T[:, xl, dc, :],
                                      start=(n == 0), stop=(n == 5))
                        n += 1
                m.then_inc(r1_done, 1)
            pe.wait_ge(rw2_ready, 2)
            pe.wait_ge(r1_lo, HC)
            for t in range(NT):
                n = 0
                for hc in range(HC):
                    for hl, wl in ((1, 0), (0, 1), (0, 0)):
                        m = pe.matmul(ps[:, 4, t * E:(t + 1) * E], rh[:, hl, hc, t * P:(t + 1) * P], rw2p[:, wl, hc, :],
                                      start=(n == 0), stop=(n == 3 * HC - 1))
                        n += 1
            m.then_inc(lg_done, 1)
            pe.wait_ge(picked_ready, 1)
            for t in range(NT):
                for k in range(t + 1):
                    pe.matmul(ps[:, 5, t * E:(t + 1) * E], (before if k == t else ones16)[:, :], picked[:, k, :],
                              start=(k == 0), stop=(k == t))
            for t in range(NT):
                m = pe.matmul(ps[:, 6, 0:E], ones16[:, :], picked[:, t, :], start=(t == 0), stop=(t == NT - 1))
            m.then_inc(rank_done, 1)
            pe.wait_ge(we_ready, 2)
            for t in range(NT):
                m = pe.transpose(ps[0:E, 7, t * P:(t + 1) * P], we[:, t, :], ident[:, :])
            m.then_inc(wet_done, 1)
            pe.wait_ge(wet_out, 1)
            for t in range(NT):
                pe.matmul(ps[:, t // 2, (t % 2) * D:(t % 2 + 1) * D], weT[:, t, :], b2_sb[:, :],
                          start=(t % 2 == 0), stop=False, skip_group_check=True)

            pe.wait_ge(owner_ready, 1)
            blocks = pe.value_load(owner[0:1, NBLK:NBLK + 1], min_val=E, max_val=NBLK)
            expert = {}

            def if_used(stage, b):
                if E <= b < NBLK:
                    with pe.If(blocks > b):
                        stage(b)
                elif 0 <= b < E:
                    stage(b)

            def load_expert(b):
                if b < NBLK:
                    expert[b] = pe.value_load(owner[0:1, b:b + 1], min_val=0, max_val=E - 1)

            turned = ps[:, 6, :].bitcast(F16)

            def gather(b):
                pe.wait_ge(onehot_ready, b + 1)
                if b:
                    pe.wait_ge(xg_out, b)
                    pe.wait_ge(turn_out, b)
                else:
                    pe.wait_ge(x3p_ready, 2 * NT)
                for l in range(2):
                    for dc in range(DC):
                        for t in range(NT):
                            m = pe.matmul(ps[:, 5, (l * DC + dc) * P:(l * DC + dc + 1) * P],
                                          x3p[:, l, t, dc * P:(dc + 1) * P], onehot[:, b % 3, t, :],
                                          start=(t == 0), stop=(t == NT - 1))
                m.then_inc(xg_done, 1)
                for t in range(NT):
                    pe.transpose(turned[:, t * P:(t + 1) * P], onehot[:, b % 3, t, :], ident16[:, :])
                for t in range(NT):
                    m = pe.matmul(ps[:, 6, 2 * P:2 * P + 2],
                                  onehot[:, b % 3, t, :], wep[:, t, bass.ds(expert[b], 1), :].rearrange("p e l -> p (e l)"),
                                  start=(t == 0), stop=(t == NT - 1))
                m.then_inc(turn_done, 1)

            def hidden(b):
                pe.wait_ge(xg_out, b + 1)
                pe.wait_ge(split_hi, 2 * min(b, E - 1) + 2)
                pe.wait_ge(split_lo, 2 * min(b, E - 1) + 2)
                for half in range(2):
                    if b:
                        pe.wait_ge(h_act, 2 * (b - 1) + half + 1)
                    for i in range(4):
                        hc = 4 * half + i
                        n = 0
                        for dc in range(DC):
                            for wl, xl in ((1, 0), (0, 1), (0, 0)):
                                w = wp[:, bass.ds(expert[b], 1), wl, dc * HID + hc * P:dc * HID + (hc + 1) * P]
                                m = pe.matmul(ps[:, 2 + half, i * P:(i + 1) * P], w.rearrange("p e n -> p (e n)"),
                                              xg[:, b % 2, xl, dc, :], start=(n == 0), stop=(n == 5))
                                n += 1
                    m.then_inc(h_done, 1)

            def output(b):
                pe.wait_ge(split_hi, 2 * min(b, E - 1) + 3)
                pe.wait_ge(split_lo, 2 * min(b, E - 1) + 3)
                if b:
                    pe.wait_ge(y_act, b)
                n = 0
                for hc in range(HC):
                    if hc % 4 == 0:
                        pe.wait_ge(h_lo, 2 * b + hc // 4 + 1)
                    for hl, wl in ((1, 0), (0, 1), (0, 0)):
                        w = wp[:, bass.ds(expert[b], 1), 2 + wl, hc * D:(hc + 1) * D]
                        m = pe.matmul(ps[:, 4, 0:D], hp[:, b % 2, hl, hc, :], w.rearrange("p e n -> p (e n)"),
                                      start=(n == 0), stop=(n == 3 * HC - 1))
                        n += 1
                m.then_inc(y_done, 1)

            def combine(b):
                pe.wait_ge(y_pair, b + 1)
                for t in range(NT):
                    for l in (1, 0):
                        m = pe.matmul(ps[:, t // 2, (t % 2) * D:(t % 2 + 1) * D], onehotT[:, b % 4, t * P:(t + 1) * P],
                                      yp[:, b % 2, l, :], start=False, stop=False,
                                      skip_group_check=True)
                m.then_inc(sum_done, 1)

            load_expert(0)
            load_expert(1)
            gather(0)
            gather(1)
            hidden(0)
            for b in range(NBLK):
                load_expert(b + 2)
                if_used(gather, b + 2)
                if_used(hidden, b + 1)
                if_used(output, b)
                if_used(combine, b - 1)
            if_used(combine, NBLK - 1)
            pe.drain().then_inc(all_summed, 1)

        @block.scalar
        def _(act):
            for i in range(2):
                act.wait_ge(xt_done, i + 1)
                act.copy(xnT[:, :, 2 * i * P:(2 * i + 2) * P], ps[:, 4 + i, :].rearrange("p (c n) -> p c n", c=DC)).then_inc(xt_out, 1)
            def split(k):
                act.wait_ge(in_stage[k % STAGE], 16 * (k // STAGE + 1))
                dst = rw1p[:, 0].rearrange("p c n -> p (c n)") if k == 0 else wp[:, (k - 1) // 2, 2 * ((k - 1) % 2), :]
                act.mul(dst, stage[:, k % STAGE, :], WSCALE).then_inc(split_hi, 1)

            def turned_context(n):
                act.wait_ge(ct_done, 2 * n + 2)
                if n >= 2:
                    act.wait_ge(v_done, 2 * (n - 1))
                act.copy(ctxT[:, :, n % 2, 2 * P:4 * P], ps[:, 1, :].rearrange("p (c n) -> p c n", c=DC)).then_inc(ct_out_a, 1)

            turned_context(0)
            for n in range(4):
                if n + 1 < 4:
                    turned_context(n + 1)
                for oc in range(DC):
                    act.wait_ge(k_done, DC * n + oc + 1)
                    act.wait_ge(wt_out, 4)
                    act.activation(kT_hi[:, oc, n * 512:(n + 1) * 512], ps[:, 2 + oc, :], ACT.Identity,
                                   bias=biasT[:, KB + oc:KB + oc + 1]).then_inc(k_hi_out, 1)
                for j in range(2):
                    act.wait_ge(v_done, 2 * n + j + 1)
                    if n == 0:
                        act.wait_ge(consts, 12)
                    t = 4 * n + 2 * j
                    act.copy(v_hi[:, t:t + 2, :, 0:XD],
                             ps[:, 4 + j, :].rearrange("p (t h d) -> p t h d", t=2, d=XD)).then_inc(v_hi_out, 1)
            split(0)
            def exps(u):
                act.wait_ge(max_ready, u + 1)
                if u >= 2:
                    act.wait_ge(pt_done, 2 * (u - 1))
                for pair in range(PAIRS):
                    m = act.activation(prob[:, u % 2, pair, :],
                                       ps[:, 2 * (u % 2) + pair // 2, (pair % 2) * SK:(pair % 2 + 1) * SK],
                                       ACT.Exp, bias=nmax[:, u, pair:pair + 1])
                m.then_inc(exp_ready, 1)

            exps(0)
            for u in range(NU):
                if u + 1 < NU:
                    exps(u + 1)
                for kt in range(2):
                    act.wait_ge(pt_done, 2 * u + kt + 1)
                    if u >= 2:
                        act.wait_ge(pv_done, u - 1)
                    act.copy(pT_hi[:, u % 2, kt], ps[:, 4 + kt, :].rearrange("p (g q) -> p g q", g=PAIRS)).then_inc(pt_hi_out, 1)
                if u in (4, 6, 8, 10):
                    if u == 4:
                        act.wait_ge(m_out, 1)
                    split(u // 2 - 1)
            for i in range(2):
                act.wait_ge(x2t_done, i + 1)
                act.copy(xnT[:, :, 2 * i * P:(2 * i + 2) * P], ps[:, 4 + i, :].rearrange("p (c n) -> p c n", c=DC)).then_inc(x2t_out, 1)
            act.wait_ge(sk_done, 1)
            for oc in range(DC):
                m = act.activation(s_kh[:, oc, :], ps[:, 2 + oc, :], ACT.Identity, bias=biasT[:, SKB + oc:SKB + oc + 1])
            m.then_inc(sk_hi_out, 1)
            for i in range(2):
                act.wait_ge(sv_done, i + 1)
                act.copy(s_vh[:, 2 * i:2 * i + 2, :], ps[:, i, :].rearrange("p (t d) -> p t d", t=2)).then_inc(sv_hi_out, 1)
            for t in range(NT):
                act.wait_ge(ssub_ready, t + 1)
                act.activation(s_sc[:, t], s_sc[:, t], ACT.Exp).then_inc(sexp_ready, 1)
            for t in range(NT):
                act.wait_ge(spt_done, t + 1)
                act.copy(s_pTh[:, t], ps[:, t % 2, :].rearrange("p (g q) -> p g q", g=4)).then_inc(spt_hi_out, 1)
            for i in range(2):
                act.wait_ge(x3t_done, i + 1)
                act.copy(x3T[:, 0, :, 2 * i * P:(2 * i + 2) * P],
                         ps[:, i, :].rearrange("p (c n) -> p c n", c=DC)).then_inc(x3t_hi_out, 1)
            for hc in range(HC):
                act.wait_ge(r1_done, hc + 1)
                if hc >= 2:
                    act.wait_ge(r1_lo, hc - 1)
                act.activation(h32[:, hc % 2, :], ps[:, 2 + hc % 2, :], ACT.Silu,
                               bias=biasT[:, RB + hc:RB + hc + 1], scale=1 / WSCALE).then_inc(r1_act, 1)
                if hc in (1, 3, 5):
                    split(5 + hc // 2)
            act.wait_ge(gap_ready, 1)
            act.activation(th[:, :], gap[:, :], ACT.Tanh, scale=0.5).then_inc(th_ready, 1)
            split(8)
            act.wait_ge(owner_ready, 1)
            blocks = act.value_load(owner[0:1, NBLK:NBLK + 1], min_val=E, max_val=NBLK)

            def gathered(b):
                act.wait_ge(xg_done, b + 1)
                if b >= 2:
                    act.wait_ge(h_done, 2 * (b - 1))
                act.copy(xg[:, b % 2], ps[:, 5, :].rearrange("p (l c n) -> p l c n", l=2, c=DC)).then_inc(xg_out, 1)

            def hidden(b):
                expert = act.value_load(owner[0:1, b:b + 1], min_val=0, max_val=E - 1)
                for half in range(2):
                    act.wait_ge(h_done, 2 * b + half + 1)
                    if b:
                        act.wait_ge(h_lo, 2 * (b - 1) + half + 1)
                    for i in range(4):
                        bias = biasT[:, EB:EB + E * HC].rearrange("p (e c) -> p e c", c=HC)[
                            :, bass.ds(expert, 1), 4 * half + i]
                        m = act.activation(h32[:, half, i * P:(i + 1) * P], ps[:, 2 + half, i * P:(i + 1) * P],
                                           ACT.Silu, bias=bias, scale=1 / WSCALE)
                    m.then_inc(h_act, 1)

            def output(b):
                act.wait_ge(y_done, b + 1)
                act.wait_ge(turn_out, b + 1)
                if b >= 2:
                    act.wait_ge(y_pair, b - 1)
                act.mul(y32[:, b % 2, :], ps[:, 4, 0:D], wslot[:, b:b + 1]).then_inc(y_act, 1)

            def if_used(stage, b):
                if E <= b < NBLK:
                    with act.If(blocks > b):
                        stage(b)
                elif b < E:
                    stage(b)

            gathered(0)
            gathered(1)
            hidden(0)
            for b in range(NBLK):
                if_used(gathered, b + 2)
                if_used(hidden, b + 1)
                if_used(output, b)
                if b < 4:
                    split(9 + 2 * b)
                    split(10 + 2 * b)

        @block.vector
        def _(dve):
            step = [0]

            def link(ins):
                step[0] += 1
                ins.then_inc(dve_step, 1)
                dve.wait_ge(dve_step, step[0])

            def norm_stats(n, t):
                link(dve.bn_stats(stats[:, n, t, :], xs[:, t, :]))
                link(dve.bn_aggr(mv[:, n, t, :], stats[:, n, t, :]))
                dve.tensor_scalar(vareps[:, n, t:t + 1], mv[:, n, t, 1:2], EPS, None, ALU.add).then_inc(var_ready, 1)

            def norm_apply(n, t):
                dve.wait_ge(rstd_ready, n * NT + t + 1)
                dve.tensor_scalar(xn[:, t, :], xs[:, t, :], mv[:, n, t, 0:1], rstd[:, n, t:t + 1],
                                  ALU.subtract, ALU.mult).then_inc(xn_ready, 1)

            dve.wait_ge(in_x, 16)
            for t in range(NT):
                norm_stats(0, t)
            for t in range(NT):
                norm_apply(0, t)
            for i in range(3):
                dve.wait_ge(wt_done, i + 1)
                dve.tensor_copy(wT[:, i], ps[:, i, :].rearrange("p (c n) -> p c n", c=DC)).then_inc(wt_out, 1)
            dve.wait_ge(wt_done, 4)
            dve.tensor_copy(biasT[:, :], ps[:, 3, 0:NB]).then_inc(wt_out, 1)
            dve.wait_ge(in_mask, 16)
            dve.tensor_scalar(mask_row[:, :], mask_i[:, :], 0.0, MASKED, ALU.is_gt, ALU.mult).then_inc(mask_ready, 1)
            dve.wait_ge(wt_out, 4)
            for oc in range(DC):
                dve.wait_ge(q_done, oc + 1)
                link(dve.tensor_scalar(q32[:, oc, :], ps[:, 6 + oc, :], biasT[:, QB + oc:QB + oc + 1], XSCALE,
                                       ALU.add, ALU.mult))
                link(dve.tensor_copy(qh[:, oc, :], q32[:, oc, :]))
                dve.tensor_tensor(ql[:, oc, :], q32[:, oc, :], qh[:, oc, :], ALU.subtract).then_inc(q_out, 1)
            dve.wait_ge(q_out, DC)
            dve.wait_ge(consts, 7)

            def spread_queries(oc, heads):
                for h in heads:
                    for src, dst in ((qh, qbd_hi), (ql, qbd_lo)):
                        m = dve.tensor_scalar(dst[:, oc, :, h, :], src[:, oc, :].rearrange("p (b q) -> p b q", b=B),
                                              headmask[:, h:h + 1], None, ALU.mult)
                return m

            def split(k):
                dve.wait_ge(split_hi, k + 1)
                if k == 0:
                    hi, lo = (rw1p[:, l].rearrange("p c n -> p (c n)") for l in range(2))
                else:
                    hi, lo = (wp[:, (k - 1) // 2, 2 * ((k - 1) % 2) + l, :] for l in range(2))
                dve.scalar_tensor_tensor(out=lo, in0=stage[:, k % STAGE, :], scalar=WSCALE, in1=hi,
                                         op0=ALU.mult, op1=ALU.subtract).then_inc(split_lo, 1)

            def turned_context(n):
                dve.wait_ge(ct_done, 2 * n + 1)
                if n >= 2:
                    dve.wait_ge(v_done, 2 * (n - 1))
                dve.tensor_copy(ctxT[:, :, n % 2, 0:2 * P], ps[:, 0, :].rearrange("p (c n) -> p c n", c=DC)).then_inc(ct_out_d, 1)

            turned_context(0)
            for n in range(4):
                if n + 1 < 4:
                    turned_context(n + 1)
                for oc in range(DC):
                    dve.wait_ge(k_hi_out, DC * n + oc + 1)
                    dve.scalar_tensor_tensor(out=kT_lo[:, oc, n * 512:(n + 1) * 512], in0=ps[:, 2 + oc, :],
                                             scalar=biasT[:, KB + oc:KB + oc + 1],
                                             in1=kT_hi[:, oc, n * 512:(n + 1) * 512],
                                             op0=ALU.add, op1=ALU.subtract).then_inc(k_lo_out, 1)
                for j in range(2):
                    dve.wait_ge(v_hi_out, 2 * n + j + 1)
                    t = 4 * n + 2 * j
                    dve.tensor_tensor(v_lo[:, t:t + 2, :, 0:XD],
                                      ps[:, 4 + j, :].rearrange("p (t h d) -> p t h d", t=2, d=XD),
                                      v_hi[:, t:t + 2, :, 0:XD], ALU.subtract).then_inc(v_lo_out, 1)
                half = range(4 * (n % 2), 4 * (n % 2) + 4)
                m = spread_queries(n // 2, half)
                if n % 2:
                    m.then_inc(qbd_ready, 1)
            dve.wait_ge(ut_done, 1)
            dve.tensor_copy(uT[:, 0:2], ps[:, 6, :].rearrange("p (i c n) -> p i c n", i=2, c=DC))
            dve.tensor_copy(uT[:, 2], ps[:, 7, 0:DC * P].rearrange("p (c n) -> p c n", c=DC)).then_inc(ut_out, 1)
            dve.wait_ge(m_done, 1)
            dve.tensor_copy(mbd[:, 0:2], ps[:, 6, :].rearrange("p (i c n) -> p i c n", i=2, c=DC))
            dve.tensor_copy(mbd[:, 2], ps[:, 7, 0:DC * P].rearrange("p (c n) -> p c n", c=DC)).then_inc(m_out, 1)
            dve.wait_ge(in_vb, 16)
            for t in range(NT):
                m = dve.tensor_tensor(xs[:, t, :], xs[:, t, :], vb_all[:, :], ALU.add)
            link(m)

            def maxima(u):
                dve.wait_ge(sc_done, u + 1)
                dve.tensor_reduce(nmax[:, u, :],
                                  ps[:, 2 * (u % 2):2 * (u % 2) + 2, :].rearrange("p a (i k) -> p (a i) k", i=2),
                                  AX.X, ALU.max, negate=True).then_inc(max_ready, 1)

            def normalise(b):
                dve.wait_ge(pv_done, DC * (b + 1))
                o = ps[:, 6 + b % 2, 0:DC * PAIRS * 2 * VW].rearrange("p (o h d) -> p o h d", h=2, d=VW)
                for h2 in range(2):
                    r = slice(64 * h2, 64 * h2 + 64)
                    m = dve.reciprocal(orec[r, b, :], o[r, :, h2, XD])
                link(m)
                for h2 in range(2):
                    r = slice(64 * h2, 64 * h2 + 64)
                    m = dve.tensor_tensor(on[r, b], o[r, :, h2, 0:XD],
                                          orec[r, b, :].unsqueeze(2).broadcast_to([64, DC * PAIRS, XD]), ALU.mult)
                m.then_inc(on_ready, 1)

            split(0)
            dve.wait_ge(in_rw2, 16)
            dve.tensor_scalar(rw2p[:, 0], rw2_sb[:, :, :], WSCALE, None, ALU.mult).then_inc(rw2_ready, 1)
            dve.wait_ge(rw2_ready, 1)
            dve.scalar_tensor_tensor(out=rw2p[:, 1], in0=rw2_sb[:, :, :], scalar=WSCALE, in1=rw2p[:, 0],
                                     op0=ALU.mult, op1=ALU.subtract).then_inc(rw2_ready, 1)
            maxima(0)
            maxima(1)
            for u in range(NU):
                if u + 2 < NU:
                    maxima(u + 2)
                for kt in range(2):
                    dve.wait_ge(pt_hi_out, 2 * u + kt + 1)
                    dve.tensor_tensor(pT_lo[:, u % 2, kt], ps[:, 4 + kt, :].rearrange("p (g q) -> p g q", g=PAIRS),
                                      pT_hi[:, u % 2, kt], ALU.subtract).then_inc(pt_lo_out, 1)
                if u >= DC and u % DC == 0:
                    normalise(u // DC - 1)
                if u in (4, 6, 8, 10):
                    split(u // 2 - 1)
            normalise(B - 1)

            for t in range(NT):
                dve.wait_ge(sh_done, t + 1)
                m = dve.tensor_tensor(xs[:, t, :], ps[:, t, 0:D], xs[:, t, :], ALU.add)
                m.then_inc(x1_ready, 1)
                dve.wait_ge(x1_ready, t + 1)
                norm_stats(1, t)
            for t in range(NT):
                norm_apply(1, t)
            dve.wait_ge(in_misc, 48)
            for t in range(NT):
                m = dve.tensor_tensor(xs[:, t, :], xs[:, t, :], bv_all[:, :], ALU.add)
            link(m)
            dve.wait_ge(sq_done, 1)
            for oc in range(DC):
                link(dve.tensor_scalar(s_q32[:, oc, :], ps[:, 6 + oc, :], biasT[:, SQB + oc:SQB + oc + 1], SSCALE,
                                       ALU.add, ALU.mult))
            link(dve.tensor_copy(s_qh[:, :, :], s_q32[:, :, :]))
            link(dve.tensor_tensor(s_ql[:, :, :], s_q32[:, :, :], s_qh[:, :, :], ALU.subtract))
            for oc in range(DC):
                for h in range(P // DH):
                    for src, dst in ((s_qh, s_qbd_hi), (s_ql, s_qbd_lo)):
                        m = dve.tensor_scalar(dst[:, oc, :, h, :], src[:, oc, :].rearrange("p (b q) -> p b q", b=B),
                                              blockmask[:, h:h + 1], None, ALU.mult)
            m.then_inc(sqbd_ready, 1)
            dve.wait_ge(sk_hi_out, 1)
            for oc in range(DC):
                m = dve.scalar_tensor_tensor(out=s_kl[:, oc, :], in0=ps[:, 2 + oc, :],
                                             scalar=biasT[:, SKB + oc:SKB + oc + 1], in1=s_kh[:, oc, :],
                                             op0=ALU.add, op1=ALU.subtract)
            m.then_inc(sk_lo_out, 1)
            for i in range(2):
                dve.wait_ge(sv_hi_out, i + 1)
                dve.tensor_tensor(s_vl[:, 2 * i:2 * i + 2, :], ps[:, i, :].rearrange("p (t d) -> p t d", t=2),
                                  s_vh[:, 2 * i:2 * i + 2, :], ALU.subtract).then_inc(sv_lo_out, 1)
            for t in range(NT):
                dve.wait_ge(ssc_done, t + 1)
                s = ps[:, 4 + t, :].rearrange("p (k q) -> p k q", k=8)
                link(dve.tensor_reduce(s_max[:, t, :], s, AX.X, ALU.max))
                dve.tensor_tensor(s_sc[:, t], s, s_max[:, t, :].unsqueeze(2).broadcast_to([P, 8, SQ]),
                                  ALU.subtract).then_inc(ssub_ready, 1)
            for t in range(NT):
                dve.wait_ge(sexp_ready, t + 1)
                link(dve.tensor_reduce(s_sum[:, t, :], s_sc[:, t], AX.X, ALU.add))
                link(dve.reciprocal(s_rec[:, t, :], s_sum[:, t, :]))
            for t in range(NT):
                dve.wait_ge(spt_hi_out, t + 1)
                dve.tensor_tensor(s_pTl[:, t], ps[:, t % 2, :].rearrange("p (g q) -> p g q", g=4),
                                  s_pTh[:, t], ALU.subtract).then_inc(spt_lo_out, 1)
                dve.wait_ge(spv_done, t + 1)
                o = ps[:, 2 + 2 * (t % 2):4 + 2 * (t % 2), 0:D].rearrange("p j (k h d) -> p j k h d", k=4, h=2)
                for h2 in range(2):
                    r = slice(64 * h2, 64 * h2 + 64)
                    for j in range(2):
                        m = dve.tensor_tensor(s_on[r, t].rearrange("p (k j) d -> p k j d", j=2)[:, :, j, :],
                                              o[r, j, :, h2, :],
                                              s_rec[r, t, j::2].unsqueeze(2).broadcast_to([64, 4, DH]), ALU.mult)
                m.then_inc(son_ready, 1)
            for t in range(NT):
                dve.wait_ge(ssh_done, t + 1)
                dve.tensor_tensor(xs[:, t, :], ps[:, 6 + t % 2, 0:D], xs[:, t, :], ALU.add).then_inc(x2_ready, 1)
                dve.wait_ge(x2_ready, t + 1)
                norm_stats(2, t)
            for t in range(NT):
                norm_apply(2, t)

            for i in range(2):
                dve.wait_ge(x3t_hi_out, i + 1)
                dve.tensor_tensor(x3T[:, 1, :, 2 * i * P:(2 * i + 2) * P],
                                  ps[:, i, :].rearrange("p (c n) -> p c n", c=DC),
                                  x3T[:, 0, :, 2 * i * P:(2 * i + 2) * P], ALU.subtract).then_inc(x3t_lo_out, 1)
            for hc in range(HC):
                dve.wait_ge(r1_act, hc + 1)
                dve.tensor_copy(rh[:, 0, hc, :], h32[:, hc % 2, :]).then_inc(r1_hi, 1)
                dve.wait_ge(r1_hi, hc + 1)
                dve.tensor_tensor(rh[:, 1, hc, :], h32[:, hc % 2, :], rh[:, 0, hc, :], ALU.subtract).then_inc(r1_lo, 1)
                if hc == 4:
                    split(5)

            dve.wait_ge(lg_done, 1)
            link(dve.scalar_tensor_tensor(out=logit[:, :, :], in0=ps[:, 4, 0:NT * E].rearrange("p (t e) -> p t e", t=NT),
                                          scalar=1 / WSCALE, in1=rb2_all[:, :].unsqueeze(1).broadcast_to([P, NT, E]),
                                          op0=ALU.mult, op1=ALU.add))
            for t in range(NT):
                m = dve.max(top[:, t, :], logit[:, t, :])
            link(m)
            dve.tensor_tensor(gap[:, :], top[:, :, 0], top[:, :, 1], ALU.subtract).then_inc(gap_ready, 1)
            for t in range(NT):
                m = dve.max_index(topi[:, t, :], top[:, t, :], logit[:, t, :])
            link(m)
            link(dve.tensor_copy(topf[:, :, :], topi[:, :, :]))
            dve.wait_ge(consts, CONSTS)
            for k in range(2):
                m = dve.tensor_tensor(pick[:, k], iota_f[:, 0:E].unsqueeze(1).broadcast_to([P, NT, E]),
                                      topf[:, :, k].unsqueeze(2).broadcast_to([P, NT, E]), ALU.is_equal)
            link(m)
            dve.tensor_tensor(picked[:, :, :], pick[:, 0], pick[:, 1], ALU.add).then_inc(picked_ready, 1)
            dve.wait_ge(th_ready, 1)
            dve.tensor_scalar(p1[:, :], th[:, :], 0.5, 0.5, ALU.mult, ALU.add)
            link(dve.tensor_scalar(p2[:, :], th[:, :], -0.5, 0.5, ALU.mult, ALU.add))
            dve.tensor_tensor(we1[:, :, :], pick[:, 0], p1[:, :].unsqueeze(2).broadcast_to([P, NT, E]), ALU.mult)
            link(dve.tensor_tensor(we2[:, :, :], pick[:, 1], p2[:, :].unsqueeze(2).broadcast_to([P, NT, E]), ALU.mult))
            link(dve.tensor_tensor(we[:, :, :], we1[:, :, :], we2[:, :, :], ALU.add))
            dve.tensor_copy(wep[:, :, :, 0], we[:, :, :]).then_inc(we_ready, 1)
            dve.wait_ge(we_ready, 1)
            dve.tensor_tensor(wep[:, :, :, 1], we[:, :, :], wep[:, :, :, 0], ALU.subtract).then_inc(we_ready, 1)
            dve.wait_ge(rank_done, 1)
            link(dve.tensor_copy(count[:, :], ps[:, 6, 0:E]))
            link(dve.tensor_scalar(nblk[:, 0, :], count[:, :], float(P), 1.0, ALU.is_gt, ALU.add))
            link(dve.scalar_tensor_tensor(out=nblk[:, 1, :], in0=count[:, :], scalar=2.0 * P, in1=nblk[:, 0, :],
                                          op0=ALU.is_gt, op1=ALU.add))
            link(dve.scalar_tensor_tensor(out=nblk[:, 2, :], in0=count[:, :], scalar=3.0 * P, in1=nblk[:, 1, :],
                                          op0=ALU.is_gt, op1=ALU.add))
            link(dve.tensor_tensor_scan(nincl[:, :], ones16[:, 0:E], nblk[:, 2, :], 0.0, ALU.mult, ALU.add))
            link(dve.tensor_tensor(first[:, :], nincl[:, :], nblk[:, 2, :], ALU.subtract))
            link(dve.tensor_tensor(owner3[:, :, :], first[0:1, :].unsqueeze(1).broadcast_to([1, NBLK, E]),
                                   iota_f[0:1, :].unsqueeze(2).broadcast_to([1, NBLK, E]), ALU.is_le))
            link(dve.tensor_reduce(owner_f[:, :], owner3[:, :, :], AX.X, ALU.add))
            dve.tensor_copy(owner[:, NBLK:], nincl[0:1, E - 1:E])
            dve.tensor_scalar(owner[:, 0:NBLK], owner_f[:, :], -1.0, None, ALU.add).then_inc(owner_ready, 1)
            for t in range(NT):
                m = dve.scalar_tensor_tensor(out=gslot[:, t, :], in0=first[:, :], scalar=float(P),
                                             in1=ps[:, 5, t * E:(t + 1) * E], op0=ALU.mult, op1=ALU.add)
            link(m)
            for k in range(2):
                m = dve.tensor_tensor(slot12[:, k], pick[:, k], gslot[:, :, :], ALU.mult)
            link(m)
            link(dve.tensor_reduce(slot[:, :, :], slot12[:, :, :, :], AX.X, ALU.add))

            def one_hot(b):
                if b >= 3:
                    dve.wait_ge(turn_done, b - 2)
                for t in range(NT):
                    m = dve.tensor_scalar(onehot[:, b % 3, t, :], slot_ids[:, b * P:(b + 1) * P],
                                          slot[:, 0, t:t + 1], None, ALU.is_equal)
                m.then_inc(first_choice, 1)
                dve.wait_ge(first_choice, b + 1)
                for t in range(NT):
                    m = dve.scalar_tensor_tensor(out=onehot[:, b % 3, t, :], in0=slot_ids[:, b * P:(b + 1) * P],
                                                 scalar=slot[:, 1, t:t + 1], in1=onehot[:, b % 3, t, :],
                                                 op0=ALU.is_equal, op1=ALU.add)
                m.then_inc(onehot_ready, 1)

            def turned(b):
                dve.wait_ge(turn_done, b + 1)
                if b >= 4:
                    dve.wait_ge(sum_done, b - 3)
                dve.tensor_copy(onehotT[:, b % 4, :], ps[:, 6, 0:2 * P].bitcast(F16))
                dve.tensor_reduce(wslot[:, b:b + 1], ps[:, 6, 2 * P:2 * P + 2], AX.X, ALU.add).then_inc(wslot_sum, 1)
                dve.wait_ge(wslot_sum, b + 1)
                dve.tensor_scalar(wslot[:, b:b + 1], wslot[:, b:b + 1], 1 / WSCALE, None, ALU.mult).then_inc(turn_out, 1)

            def hidden(b):
                for half in range(2):
                    dve.wait_ge(h_act, 2 * b + half + 1)
                    if b >= 2:
                        dve.wait_ge(y_done, b - 1)
                    src = h32[:, half, :].rearrange("p (c n) -> p c n", c=4)
                    dve.tensor_copy(hp[:, b % 2, 0, 4 * half:4 * half + 4, :], src).then_inc(h_hi, 1)
                    dve.wait_ge(h_hi, 2 * b + half + 1)
                    dve.tensor_tensor(hp[:, b % 2, 1, 4 * half:4 * half + 4, :], src,
                                      hp[:, b % 2, 0, 4 * half:4 * half + 4, :], ALU.subtract).then_inc(h_lo, 1)

            def output(b):
                dve.wait_ge(y_act, b + 1)
                if b >= 2:
                    dve.wait_ge(sum_done, b - 1)
                dve.tensor_copy(yp[:, b % 2, 0, :], y32[:, b % 2, :]).then_inc(y_hi, 1)
                dve.wait_ge(y_hi, b + 1)
                dve.tensor_tensor(yp[:, b % 2, 1, :], y32[:, b % 2, :], yp[:, b % 2, 0, :], ALU.subtract).then_inc(y_pair, 1)

            def if_used(stage, b):
                if E <= b < NBLK:
                    with dve.If(blocks > b):
                        stage(b)
                elif b < E:
                    stage(b)

            one_hot(0)
            dve.wait_ge(wet_done, 1)
            dve.tensor_copy(weT[:, :, :], ps[0:E, 7, :].rearrange("e (t n) -> e t n", t=NT)).then_inc(wet_out, 1)
            one_hot(1)
            one_hot(2)
            split(6)
            turned(0)
            turned(1)
            split(7)
            split(8)
            hidden(0)
            dve.wait_ge(owner_ready, 1)
            blocks = dve.value_load(owner[0:1, NBLK:NBLK + 1], min_val=E, max_val=NBLK)
            for b in range(NBLK):
                if_used(one_hot, b + 3)
                if_used(turned, b + 2)
                if_used(hidden, b + 1)
                if_used(output, b)
                if b < 4:
                    split(9 + 2 * b)
                    split(10 + 2 * b)
            dve.wait_ge(all_summed, 1)
            for t in range(NT):
                dve.tensor_tensor(xn[:, t, :], ps[:, t // 2, (t % 2) * D:(t % 2 + 1) * D], xs[:, t, :],
                                  ALU.add).then_inc(out_ready, 1)


_INS = ["x", "ctx_1024", "mask_BxS2_ik0", "L0_xattn_q_w", "L0_xattn_q_b", "L0_xattn_k_w", "L0_xattn_k_b",
        "L0_xattn_v_w", "L0_xattn_v_b", "L0_attn_Uq", "L0_attn_Vq", "L0_attn_bq", "L0_attn_Uk", "L0_attn_Vk",
        "L0_attn_bk", "L0_attn_Uv", "L0_attn_Vv", "L0_attn_bv", "L0_ffn_rw1", "L0_ffn_rb1", "L0_ffn_rw2",
        "L0_ffn_rb2", "L0_ffn_w1", "L0_ffn_b1", "L0_ffn_w2", "L0_ffn_b2"]
_OUT = ((8, 64, 256), "float32")


def kernel(**inputs):
    import numpy as _np
    import concourse.bacc as _bacc
    from concourse import mybir as _mybir
    from concourse.bass_utils import run_bass_kernel_spmd as _run

    nc = _bacc.Bacc("TRN2", target_bir_lowering=False, num_devices=1)
    arrays, args = {}, []
    for name in _INS:
        a = _np.ascontiguousarray(inputs[name])
        arrays[f"in_{name}_dram"] = a
        args.append(nc.dram_tensor(f"in_{name}_dram", a.shape, _mybir.dt.from_np(a.dtype), kind="ExternalInput").ap())
    args.append(nc.dram_tensor("out_0_dram", _OUT[0], _mybir.dt.from_np(_np.dtype(_OUT[1])), kind="ExternalOutput").ap())
    perceiver_layer(nc, *args)
    r = _run(nc, [arrays], core_ids=[0])
    return r.results[0]["out_0_dram"]
```

```python
from contextlib import ExitStack

import concourse.bass as bass
from concourse import mybir

F32 = mybir.dt.float32
F16 = mybir.dt.float16
BF16 = mybir.dt.bfloat16
I32 = mybir.dt.int32
U32 = mybir.dt.uint32
U8 = mybir.dt.uint8
ALU = mybir.AluOpType
ACT = mybir.ActivationFunctionType
AX = mybir.AxisListType

P = 128
EPS = 1e-5
MASKED = -1e30


def perceiver_layer(nc, x, ctx_in, mask, q_w, q_b, k_w, k_b, v_w, v_b, Uq, Vq, bq, Uk, Vk, bk, Uv, Vv, bv,
                    rw1, rb1, rw2, rb2, w1, b1, w2, b2, out):
    B, SQ, D = x.shape
    SK = ctx_in.shape[1]
    XH = 16
    XD = D // XH
    H, DH, R = Uq.shape
    E, _, HID = w1.shape
    DC = D // P
    NT = B * SQ // P
    KT = B * SK // P
    HC = HID // P
    NTOK = B * SQ
    NU = B * DC
    PAIRS = P // XD // 2
    NH = 2 * NU
    HB = 2 * DC
    SPLIT_AT = (2, 4, 6)
    BY_POOL = (0, 2)
    ROUTER_AT = (1, 1, 1, 1, 1, 1, 1, 1)
    TAIL = NT - 1
    EXTRA = 2 * NTOK // P - 1
    NBLK = E + EXTRA
    WSCALE = 64.0
    NCHUNK = 1 + 2 * E
    STAGE = 3
    XSCALE = XD ** -0.5
    SSCALE = DH ** -0.5
    VW = XD + 1

    es = ExitStack()
    with es:
        def sb(name, shape, dt=F32):
            return es.enter_context(nc.sbuf_tensor(name, shape, dt))

        def sem(name):
            return es.enter_context(nc.semaphore(name))

        xs = sb("xs", [P, NT, D])
        xn = sb("xn", [P, NT, D])
        xnT = sb("xnT", [P, DC, NTOK])
        stats = sb("stats", [P, 3, NT, 6])
        mv = sb("mv", [P, 3, NT, 2])
        vareps = sb("vareps", [P, 3, NT])
        rstd = sb("rstd", [P, 3, NT])
        minus_half = sb("minus_half", [P, NT])
        wscale = sb("wscale", [P, 1])
        wscale_inv = sb("wscale_inv", [P, 1])
        ident = sb("ident", [P, P])
        ident16 = sb("ident16", [P, P], F16)
        before = sb("before", [P, P], F16)
        ones16 = sb("ones16", [P, P], F16)
        headmask = sb("headmask", [P, P // XD])
        blockmask = sb("blockmask", [P, P // DH])
        iota_f = sb("iota_f", [P, NBLK])
        limits = sb("limits", [P, 3])
        own_base = sb("own_base", [P, E])
        behind = sb("behind", [1, E])
        minus_one = sb("minus_one", [P, 1 + E])
        slot_ids = sb("slot_ids", [P, NBLK * P], F16)
        ones_row = sb("ones_row", [1, P], BF16)
        NB = 4 * DC + HC + E * HC
        biasT = sb("biasT", [P, NB])
        bv_all = sb("bv_all", [P, D])
        rb2_all = sb("rb2_all", [P, E])
        b2_sb = sb("b2_sb", [E, D])
        stage = sb("stage", [P, STAGE, DC * HID])
        rw2_sb = sb("rw2_sb", [P, HC, E])
        rw2p = sb("rw2p", [P, 2, HC, E], F16)
        x3p = sb("x3p", [P, 2, NT, D], F16)
        x3T = xnT[:, :, :].rearrange("p c n -> p (c n)").bitcast(F16).rearrange("p (l c n) -> p l c n", l=2, c=DC)
        s_max = sb("s_max", [P, NT, 8])
        s_sum = sb("s_sum", [P, NT, 8])
        s_rec = sb("s_rec", [P, NT, 8])
        logit = sb("logit", [P, NT, E])
        top = sb("top", [P, NT, 8])
        topi = sb("topi", [P, NT, 8], U32)
        gap = sb("gap", [P, NT])
        th = sb("th", [P, NT])
        p1 = sb("p1", [P, NT])
        p2 = sb("p2", [P, NT])
        pick = sb("pick", [P, 2, NT, E])
        picked = sb("picked", [P, NT, E], F16)
        we1 = sb("we1", [P, NT, E])
        we2 = sb("we2", [P, NT, E])
        we = sb("we", [P, NT, E])
        wep = sb("wep", [P, NT, E, 2], F16)
        weT = sb("weT", [E, NT, P])
        count = sb("count", [P, E])
        over = sb("over", [P, E, 3])
        extra = sb("extra", [P, 1 + E])
        jump = sb("jump", [P, 1 + E])
        extra_to = sb("extra_to", [1, E])
        own_slot = sb("own_slot", [P, NT, E])
        skip = sb("skip", [P, NT, E])
        gslot = sb("gslot", [P, NT, E])
        slot12 = sb("slot12", [P, 2, NT, E])
        slot = sb("slot", [P, 2, NT])
        owner3 = sb("owner3", [1, EXTRA, E])
        owner_f = sb("owner_f", [1, EXTRA])
        owner = sb("owner", [1, EXTRA + 1], I32)
        onehot = sb("onehot", [P, 3, NT, P], F16)
        onehotT = sb("onehotT", [P, 4, NTOK], F16)
        xg = sb("xg", [P, 2, 2, DC, P], F16)
        h32 = sb("h32", [P, 2, 4 * P])
        hp = sb("hp", [P, 2, 2, HC, P], F16)
        rw1p = hp[:, :, :, :, :].rearrange("p a l c n -> p (a l c n)").rearrange("p (l c n) -> p l c n", l=2, c=DC)
        wslot = sb("wslot", [P, NBLK])
        y32 = sb("y32", [P, 2, D])
        yp = sb("yp", [P, 2, 2, D], F16)

        attn = es.enter_context(ExitStack())

        def asb(name, shape, dt=F32):
            return attn.enter_context(nc.sbuf_tensor(name, shape, dt))

        ctx_ring = asb("ctx_ring", [P, 8, NTOK])
        ctx_sb = ctx_ring[:, 0:4].rearrange("p a n -> p (a n)").rearrange("p (g k d) -> p g k d", g=2, d=D)
        ctx_hi, ctx_lo = (ctx_ring[:, 4 + 2 * l:6 + 2 * l].rearrange("p a n -> p (a n)").bitcast(F16).rearrange(
            "p (c g n) -> p c g n", c=DC, g=2) for l in range(2))
        wT = asb("wT", [P, DC, D])
        wkv = asb("wkv", [P, 2, 2, DC, D], F16)
        wraw = asb("wraw", [P, 3, DC, D])
        uvbd = wraw[:, :, :, :].rearrange("p i c d -> p (i c d)").rearrange("p (i c d) -> p i c d", i=6, d=P)
        uT = asb("uT", [P, 3, DC, P])
        uv = asb("uv", [P, 6, DC, R])
        brow = asb("brow", [NB, P])
        mbd = asb("mbd", [P, 3, DC, P])
        vb_all = asb("vb_all", [P, D])
        mask_row = asb("mask_row", [1, B * SK], BF16)
        kT_hi = asb("kT_hi", [P, DC, B * SK], F16)
        kT_lo = asb("kT_lo", [P, DC, B * SK], F16)
        v_hi = asb("v_hi", [P, KT, XH, VW], F16)
        v_lo = asb("v_lo", [P, KT, XH, VW], F16)
        q32 = xn[:, :, :].rearrange("p t d -> p (t d)").rearrange("p (c n) -> p c n", c=DC)
        qh = asb("qh", [P, DC, NTOK], F16)
        ql = asb("ql", [P, DC, NTOK], F16)
        qbd_hi = asb("qbd_hi", [P, DC, B, P // XD, SQ], F16)
        qbd_lo = asb("qbd_lo", [P, DC, B, P // XD, SQ], F16)
        nmax = asb("nmax", [P, NH, 2])
        prob = asb("prob", [P, 4, 2, SK])
        mask_i = prob[0:1].rearrange("p u g k -> p (u g k)").bitcast(I32)
        pT_hi = asb("pT_hi", [P, 4, 2, 2, P], F16)
        pT_lo = asb("pT_lo", [P, 4, 2, 2, P], F16)
        ctx_small = pT_hi[:, :, :, :, :].rearrange("p a k g q -> p (a k g q)").rearrange("p (c g n) -> p c g n", c=DC, g=2)
        wkv_rest = pT_lo[:, :, :, :, :].rearrange("p a k g q -> p (a k g q)").bitcast(F32).rearrange(
            "p (i c d) -> p i c d", i=2, c=DC)
        orec = asb("orec", [P, B, DC * PAIRS])
        on = onehotT[:, :, :].rearrange("p a n -> p (a n)").bitcast(F32).rearrange("p (b o d) -> p b o d", b=B, d=XD)
        s_xT = h32[:, 0, D:2 * D].rearrange("p (c n) -> p c n", c=DC)
        s_sc = h32[:, 1, :].rearrange("p (k q) -> p k q", q=SQ)
        s_pTh, s_pTl = (y32[:, i, :].bitcast(F16).rearrange("p (g q) -> p g q", g=4) for i in range(2))
        s_qh, s_ql = qh, ql
        s_qbd_hi, s_qbd_lo = qbd_hi[:, :, :, 0:P // DH, :], qbd_lo[:, :, :, 0:P // DH, :]
        s_kh, s_kl = kT_hi[:, :, 0:NTOK], kT_lo[:, :, 0:NTOK]
        s_vh, s_vl = (a[:, 0:4].rearrange("p t h d -> p (t h d)")[:, 0:NT * D].rearrange("p (t d) -> p t d", d=D)
                      for a in (v_hi, v_lo))
        s_on = on.rearrange("p b o d -> p (b o d)").rearrange("p (t k d) -> p t k d", t=NT, d=DH)
        r32 = qbd_lo[:, 1, 0:TAIL].rearrange("p b h q -> p (b h q)").bitcast(F32).rearrange("p (a n) -> p a n", a=2)
        attn.close()

        wp = sb("wp", [P, E, 4, DC * HID], F16)
        wp_bytes = wp[:, :, :, :].rearrange("p e l n -> p (e l n)").bitcast(U8).rearrange("p (e n) -> p e n", e=E)

        def weights(expert, part, start, n):
            at = 2 * (part * DC * HID + start)
            return wp_bytes[:, expert, at:at + 2 * n].rearrange("p e n -> p (e n)").bitcast(F16)

        rh = wp[:, E - 1].rearrange("p l n -> p (l n)").rearrange("p (l c n) -> p l c n", l=2, c=HC)

        ps = es.enter_context(nc.psum_tensor("ps", [P, 8, 512], F32))

        heads = [(c, h) for c in range(DC) for h in range(P // XD)]
        spread_at = (heads[0:6], heads[6:11], heads[11:16], ())

        in_x, in_brow, in_mask, in_uv, in_misc, in_vb = (
            sem(n) for n in ("in_x", "in_brow", "in_mask", "in_uv", "in_misc", "in_vb"))
        in_w = [sem(f"in_w{i}") for i in range(3)]
        in_ctx = [sem(f"in_ctx{i}") for i in range(4)]
        in_stage = [sem(f"in_stage{i}") for i in range(STAGE)]
        in_rw2 = sem("in_rw2")
        consts = sem("consts")
        bd_ready = sem("bd_ready")
        rstd_ready = sem("rstd_ready")
        var_ready = sem("var_ready")
        vb_added = sem("vb_added")
        bv_added = sem("bv_added")
        xn_ready = sem("xn_ready")
        dve_step = sem("dve_step")
        mask_ready = sem("mask_ready")
        wt_done = sem("wt_done")
        wt_out = sem("wt_out")
        xt_done = sem("xt_done")
        xt_out = sem("xt_out")
        q_done = sem("q_done")
        q_out = sem("q_out")
        qbd_ready = sem("qbd_ready")
        qbd_hi_ready = sem("qbd_hi_ready")
        ct_done = sem("ct_done")
        ct_hi_d = sem("ct_hi_d")
        ct_out_a = sem("ct_out_a")
        ct_out_d = sem("ct_out_d")
        ct_small = sem("ct_small")
        wkv_hi_out = sem("wkv_hi_out")
        wkv_ready = sem("wkv_ready")
        k_done = sem("k_done")
        k_hi_out = sem("k_hi_out")
        k_lo_out = sem("k_lo_out")
        v_done = sem("v_done")
        v_hi_out = sem("v_hi_out")
        v_lo_out = sem("v_lo_out")
        ut_done = sem("ut_done")
        ut_out = sem("ut_out")
        m_done = sem("m_done")
        m_out = sem("m_out")
        sc_done = sem("sc_done")
        max_ready = sem("max_ready")
        exp_ready = sem("exp_ready")
        pt_done = sem("pt_done")
        pt_hi_out = sem("pt_hi_out")
        pt_lo_out = sem("pt_lo_out")
        pv_done = sem("pv_done")
        on_ready = sem("on_ready")
        sh_done = sem("sh_done")
        x1_ready = sem("x1_ready")
        x2t_done = sem("x2t_done")
        x2t_out = sem("x2t_out")
        sq_done = sem("sq_done")
        sq_hi_out = sem("sq_hi_out")
        skv_done = sem("skv_done")
        skv_hi_out = sem("skv_hi_out")
        skv_lo_out = sem("skv_lo_out")
        sqbd_hi_ready = sem("sqbd_hi_ready")
        sqbd_ready = sem("sqbd_ready")
        ssc_done = sem("ssc_done")
        ssub_ready = sem("ssub_ready")
        sexp_ready = sem("sexp_ready")
        spt_done = sem("spt_done")
        spt_hi_out = sem("spt_hi_out")
        spt_lo_out = sem("spt_lo_out")
        spv_done = sem("spv_done")
        son_ready = sem("son_ready")
        ssh_done = sem("ssh_done")
        x2_ready = sem("x2_ready")
        x3t_done = sem("x3t_done")
        x3t_hi_out = sem("x3t_hi_out")
        x3t_lo_out = sem("x3t_lo_out")
        x3p_hi = sem("x3p_hi")
        x3p_lo = sem("x3p_lo")
        split_hi = sem("split_hi")
        split_hi_p = sem("split_hi_p")
        split_lo_d = sem("split_lo_d")
        chunk_scaled = sem("chunk_scaled")
        split_lo_p = sem("split_lo_p")
        rw2_ready = sem("rw2_ready")
        r1_done = sem("r1_done")
        r1_act = sem("r1_act")
        r1_hi = sem("r1_hi")
        r1_lo = sem("r1_lo")
        lg_done = sem("lg_done")
        gap_ready = sem("gap_ready")
        th_ready = sem("th_ready")
        picked_ready = sem("picked_ready")
        rank_done = sem("rank_done")
        owner_ready = sem("owner_ready")
        we_ready = sem("we_ready")
        wet_done = sem("wet_done")
        wet_out = sem("wet_out")
        first_choice = sem("first_choice")
        onehot_ready = sem("onehot_ready")
        xg_done = sem("xg_done")
        xg_out = sem("xg_out")
        turn_done = sem("turn_done")
        wslot_sum = sem("wslot_sum")
        turn_out = sem("turn_out")
        h_done = sem("h_done")
        h_act = sem("h_act")
        h_hi = sem("h_hi")
        h_lo = sem("h_lo")
        y_done = sem("y_done")
        y_act = sem("y_act")
        y_hi = sem("y_hi")
        y_pair = sem("y_pair")
        sum_done = sem("sum_done")
        all_summed = sem("all_summed")
        out_ready = sem("out_ready")
        stored = sem("stored")

        def xn_count(n, t):
            return t + 1 if n == 0 else NT + 2 * t + n

        def last_tile_steps(late):
            hcs = [range(sum(ROUTER_AT[:k]), sum(ROUTER_AT[:k + 1])) for k in range(8)]
            return [(NH + 1 + k, hcs[k - late] if k >= late else ()) for k in range(8)], hcs[7] if late else ()

        def self_step(stages, h):
            t, k = divmod(h - 2 * HB - 1, 8)
            if t >= 0 and k in stages:
                stages[k](t)

        def wait_low_part(engine, k):
            if k % 2 == 0:
                engine.wait_ge(split_lo_p, k // 2 + 1)
            else:
                engine.wait_ge(split_lo_d, (k + 1) // 2)

        def wait_high_part(engine, k):
            if k in BY_POOL:
                engine.wait_ge(split_hi_p, BY_POOL.index(k) + 1)
            else:
                engine.wait_ge(split_hi, k + 1 - sum(j < k for j in BY_POOL))

        def parts(k):
            if k == 0:
                return [rw1p[:, l].rearrange("p c n -> p (c n)") for l in range(2)]
            return [wp[:, (k - 1) // 2, 2 * ((k - 1) % 2) + l, :] for l in range(2)]

        block = es.enter_context(nc.Block())

        QB, KB, SQB, SKB, RB, EB = 0, DC, 2 * DC, 3 * DC, 4 * DC, 4 * DC + HC

        CONSTS = 19

        @block.sync
        def _(sp):
            ctx_g = ctx_in.rearrange("b (k p) d -> p (b k) d", p=P)
            sp.dma_start(xs[:, :, :], x.rearrange("(t b) s d -> (b s) t d", b=2)).then_inc(in_x, 16)
            for i, w in enumerate((q_w, k_w, v_w)):
                sp.dma_start(wraw[:, i], w.rearrange("(c p) d -> p c d", p=P)).then_inc(in_w[i], 16)
            for n in range(2):
                sp.dma_start(ctx_sb[:, n], ctx_g[:, 4 * n:4 * n + 4]).then_inc(in_ctx[n], 16)
            for a, r in ((q_b, 0), (k_b, DC)):
                sp.dma_start(brow[r:r + DC, :], a.rearrange("(c p) -> c p", p=P)).then_inc(in_brow, 16)
            for a, r in ((bq, SQB), (bk, SKB)):
                sp.dma_start(brow[r:r + DC, :], a.rearrange("(c h) d -> c (h d)", c=DC)).then_inc(in_brow, 16)
            sp.dma_start(brow[RB:RB + HC, :], rb1.rearrange("(c p) -> c p", p=P)).then_inc(in_brow, 16)
            sp.dma_start(brow[EB:EB + E * HC, :], b1.rearrange("e (c p) -> (e c) p", p=P)).then_inc(in_brow, 16)
            sp.dma_start(mask_i[:, :], mask.rearrange("b k -> (b k)").unsqueeze(0)).then_inc(in_mask, 16)
            for i, a in enumerate((Vq, Vk, Vv, Uq, Uk, Uv)):
                sp.dma_start(uv[:, i], a.rearrange("(c h) r d -> (h r) c d", c=DC)).then_inc(in_uv, 16)
            sp.dma_start(vb_all[:, :], v_b.partition_broadcast(P)).then_inc(in_vb, 16)
            sp.dma_start(bv_all[:, :], bv.rearrange("h d -> (h d)").partition_broadcast(P)).then_inc(in_misc, 16)
            sp.dma_start(rb2_all[:, :], rb2.partition_broadcast(P)).then_inc(in_misc, 16)
            sp.dma_start(b2_sb[:, :], b2).then_inc(in_misc, 16)
            sp.dma_start(rw2_sb[:, :, :], rw2.rearrange("(c p) e -> p c e", p=P)).then_inc(in_rw2, 16)
            for n in range(2, 4):
                sp.wait_ge(ct_done, 2 * (n - 1))
                sp.dma_start(ctx_sb[:, n % 2], ctx_g[:, 4 * n:4 * n + 4]).then_inc(in_ctx[n], 16)
            for k in range(NCHUNK):
                if k >= STAGE:
                    wait_low_part(sp, k - STAGE)
                if k == 0:
                    src = rw1.rearrange("(c p) h -> p c h", p=P)
                else:
                    src = (w1, w2)[(k - 1) % 2][(k - 1) // 2].rearrange("(c p) h -> p c h", p=P)
                sp.dma_start(stage[:, k % STAGE, :].rearrange("p (c h) -> p c h", c=src.shape[1]),
                             src).then_inc(in_stage[k % STAGE], 16)
            out_v = out.rearrange("(t b) s d -> (b s) t d", b=2)
            for t in range(NT):
                sp.wait_ge(out_ready, t + 1)
                sp.dma_start(out_v[:, t], xn[:, t]).then_inc(stored, 16)
            sp.wait_ge(stored, 16 * NT)

        @block.gpsimd
        def _(pool):
            step = [0]

            def link(ins):
                step[0] += 1
                ins.then_inc(consts, 1)
                pool.wait_ge(consts, step[0])

            def norm_scale(n, t):
                pool.wait_ge(var_ready, xn_count(n, t))
                pool.tensor_tensor(rstd[:, n, t:t + 1], vareps[:, n, t:t + 1], minus_half[:, t:t + 1],
                                   ALU.pow).then_inc(rstd_ready, 1)

            link(pool.memset(ident[:, :], 0.0))
            link(pool.affine_select(out=ident[:, :], in_=ident[:, :], compare_op=ALU.not_equal, fill=1.0,
                                    base=0, pattern=[[-1, P]], channel_multiplier=1))
            pool.memset(wscale[:, :], WSCALE)
            pool.memset(wscale_inv[:, :], 1 / WSCALE)
            link(pool.memset(minus_half[:, :], -0.5))
            for t in range(NT):
                norm_scale(0, t)
            link(pool.memset(ones_row[:, :], 1.0))
            for m, width in ((headmask, XD), (blockmask, DH)):
                n = P // width
                link(pool.memset(m[:, :], 1.0))
                link(pool.affine_select(out=m[:, :], in_=m[:, :], compare_op=ALU.is_ge, fill=0.0,
                                        base=0, pattern=[[-width, n]], channel_multiplier=1))
                link(pool.affine_select(out=m[:, :], in_=m[:, :], compare_op=ALU.is_ge, fill=0.0,
                                        base=width - 1, pattern=[[width, n]], channel_multiplier=-1))
            link(pool.memset(v_hi[:, :, :, XD:VW], 1.0))
            link(pool.memset(v_lo[:, :, :, XD:VW], 0.0))
            link(pool.tensor_copy(ident16[:, :], ident[:, :]))
            link(pool.memset(ones16[:, :], 1.0))
            link(pool.affine_select(out=before[:, :], in_=ones16[:, :], compare_op=ALU.is_gt, fill=0.0,
                                    base=0, pattern=[[1, P]], channel_multiplier=-1))
            link(pool.iota(iota_f[:, :], pattern=[[1, NBLK]], base=0, channel_multiplier=0,
                           allow_small_or_imprecise_dtypes=True))
            for k in range(3):
                pool.memset(limits[:, k:k + 1], float((k + 1) * P))
            link(pool.iota(own_base[:, :], pattern=[[P, E]], base=0, channel_multiplier=0,
                           allow_small_or_imprecise_dtypes=True))
            pool.memset(minus_one[:, :], -1.0)
            pool.memset(extra[:, 0:1], 0.0)
            link(pool.iota(behind[:, :], pattern=[[-1, E]], base=E - 2, channel_multiplier=0,
                           allow_small_or_imprecise_dtypes=True))
            link(pool.iota(slot_ids[:, :], pattern=[[1, NBLK * P]], base=0, channel_multiplier=0,
                           allow_small_or_imprecise_dtypes=True))
            assert step[0] == CONSTS

            def small_context(n):
                pool.wait_ge(ct_hi_d, n + 1)
                pool.wait_ge(ct_out_a, n + 1)
                if n >= 2:
                    pool.wait_ge(v_done, 2 * (n - 1))
                pool.tensor_tensor(ctx_small[:, :, n % 2, :], ctx_hi[:, :, n % 2, :],
                                   wscale_inv[:, 0:1].unsqueeze(2).broadcast_to([P, DC, 4 * P]), ALU.mult).then_inc(ct_small, 1)

            small_context(0)
            pool.wait_ge(in_uv, 96)
            pool.wait_ge(wt_done, 3)
            for i in range(6):
                pool.tensor_tensor(uvbd[:, i].rearrange("p c (h r) -> p c h r", r=R),
                                   uv[:, i].unsqueeze(2).broadcast_to([P, DC, P // DH, R]),
                                   blockmask[:, :].unsqueeze(1).unsqueeze(3).broadcast_to([P, DC, P // DH, R]),
                                   ALU.mult).then_inc(bd_ready, 1)
            small_context(1)

            pool.wait_ge(in_vb, 16)
            pool.wait_ge(xn_ready, NT)
            for t in range(NT):
                pool.tensor_tensor(xs[:, t, :], xs[:, t, :], vb_all[:, :], ALU.add).then_inc(vb_added, 1)
            small_context(2)
            small_context(3)

            def scale_chunk(k):
                w = stage[:, k % STAGE, :]
                if k in BY_POOL:
                    pool.wait_ge(in_stage[k % STAGE], 16 * (k // STAGE + 1))
                    pool.tensor_tensor(parts(k)[0], w, wscale[:, 0:1].broadcast_to([P, DC * HID]),
                                       ALU.mult).then_inc(split_hi_p, 1)
                wait_high_part(pool, k)
                pool.tensor_tensor(w, w, wscale[:, 0:1].broadcast_to([P, DC * HID]), ALU.mult).then_inc(chunk_scaled, 1)

            def low_part(k):
                pool.wait_ge(chunk_scaled, k // 2 + 1)
                hi, lo = parts(k)
                pool.tensor_tensor(lo, stage[:, k % STAGE, :], hi, ALU.subtract).then_inc(split_lo_p, 1)

            def split(k):
                scale_chunk(k)
                low_part(k)

            split(0)
            pool.wait_ge(v_done, 2 * 4)
            split(2)
            for t in range(NT):
                norm_scale(1, t)
                pool.wait_ge(sq_hi_out, t + 1)
                for c in range(DC):
                    m = pool.tensor_tensor(
                        s_qbd_hi[:, c, 2 * t:2 * t + 2, :, :],
                        s_qh[:, c, t * P:(t + 1) * P].rearrange("p (b q) -> p b q", b=2).unsqueeze(2).broadcast_to(
                            [P, 2, P // DH, SQ]),
                        blockmask[:, :].unsqueeze(1).unsqueeze(3).broadcast_to([P, 2, P // DH, SQ]), ALU.mult)
                m.then_inc(sqbd_hi_ready, 1)
                pool.wait_ge(xn_ready, xn_count(1, t))
                pool.wait_ge(in_misc, 48)
                pool.tensor_tensor(xs[:, t, :], xs[:, t, :], bv_all[:, :], ALU.add).then_inc(bv_added, 1)
                if t == 0:
                    scale_chunk(4)
                if t == 1:
                    low_part(4)
                norm_scale(2, t)
                pool.wait_ge(xn_ready, xn_count(2, t))
                pool.wait_ge(x3p_hi, t + 1)
                pool.tensor_tensor(x3p[:, 1, t, :], xn[:, t, :], x3p[:, 0, t, :], ALU.subtract).then_inc(x3p_lo, 1)
            for k in range(6, NCHUNK, 2):
                split(k)

        @block.tensor
        def _(pe):
            pe.wait_ge(consts, 2)
            for i in range(3):
                pe.wait_ge(in_w[i], 16)
                for dc in range(DC):
                    for oc in range(DC):
                        m = pe.transpose(ps[:, i, (dc * DC + oc) * P:(dc * DC + oc + 1) * P],
                                         wraw[:, i, oc, dc * P:(dc + 1) * P], ident[:, :])
                m.then_inc(wt_done, 1)
            pe.wait_ge(in_brow, 96)
            pe.transpose(ps[:, 3, 0:NB], brow[:, :], ident[0:NB, 0:NB]).then_inc(wt_done, 1)

            for i in range(2):
                for j in range(2):
                    t = 2 * i + j
                    pe.wait_ge(xn_ready, xn_count(0, t))
                    for dc in range(DC):
                        m = pe.transpose(ps[:, 4 + i, (dc * 2 + j) * P:(dc * 2 + j + 1) * P],
                                         xn[:, t, dc * P:(dc + 1) * P], ident[:, :])
                m.then_inc(xt_done, 1)
            pe.wait_ge(wt_out, 4)
            def turn_context(n):
                pe.wait_ge(in_ctx[n], 16)
                if n:
                    pe.wait_ge(ct_out_d, n)
                    pe.wait_ge(ct_out_a, n)
                for j in range(2):
                    for i in range(2):
                        for dc in range(DC):
                            m = pe.transpose(ps[:, j, (dc * 2 + i) * P:(dc * 2 + i + 1) * P],
                                             ctx_sb[:, n % 2, 2 * j + i, dc * P:(dc + 1) * P], ident[:, :])
                    m.then_inc(ct_done, 1)

            def turn_u():
                pe.wait_ge(bd_ready, 6)
                pe.wait_ge(q_out, DC)
                for i in range(3):
                    for c in range(DC):
                        k = i * DC + c
                        m = pe.transpose(ps[:, 6 + k // 4, (k % 4) * P:(k % 4 + 1) * P], uvbd[:, 3 + i, c, :],
                                         ident[:, :])
                m.then_inc(ut_done, 1)

            def compose_uv():
                pe.wait_ge(ut_out, 1)
                for i in range(3):
                    for c in range(DC):
                        k = i * DC + c
                        m = pe.matmul(ps[:, 6 + k // 4, (k % 4) * P:(k % 4 + 1) * P], uvbd[:, i, c, :], uT[:, i, c, :],
                                      start=True, stop=True)
                m.then_inc(m_done, 1)

            turn_context(0)
            pe.wait_ge(xt_out, 2)
            for oc in range(DC):
                for dc in range(DC):
                    m = pe.matmul(ps[:, 6 + oc, :], wT[:, dc, oc * P:(oc + 1) * P], xnT[:, dc, :],
                                  start=(dc == 0), stop=(dc == DC - 1))
                m.then_inc(q_done, 1)
            for n in range(4):
                if n + 1 < 4:
                    turn_context(n + 1)
                pe.wait_ge(ct_out_d, n + 1)
                pe.wait_ge(ct_out_a, n + 1)
                pe.wait_ge(ct_small, n + 1)
                if n == 0:
                    pe.wait_ge(wkv_ready, 1)
                part_pairs = ((0, ctx_lo), (1, ctx_small), (0, ctx_hi))
                for oc in range(DC):
                    if n:
                        pe.wait_ge(k_lo_out, DC * (n - 1) + oc + 1)
                    i = 0
                    for dc in range(DC):
                        for wl, c_part in part_pairs:
                            m = pe.matmul(ps[:, 2 + oc, :], wkv[:, wl, 0, dc, oc * P:(oc + 1) * P],
                                          c_part[:, dc, n % 2, :], start=(i == 0), stop=(i == 3 * DC - 1))
                            i += 1
                    m.then_inc(k_done, 1)
                for j in range(2):
                    if n:
                        pe.wait_ge(v_lo_out, 2 * (n - 1) + j + 1)
                    for i in range(2):
                        k = 0
                        for dc in range(DC):
                            for wl, c_part in part_pairs:
                                m = pe.matmul(ps[:, 4 + j, i * D:(i + 1) * D],
                                              c_part[:, dc, n % 2, (2 * j + i) * P:(2 * j + i + 1) * P],
                                              wkv[:, wl, 1, dc, :], start=(k == 0), stop=(k == 3 * DC - 1))
                                k += 1
                    m.then_inc(v_done, 1)
                if n == 1:
                    turn_u()
                if n == 2:
                    compose_uv()
            def scores(h):
                b, c = divmod(h // 2, DC)
                if h == 0:
                    pe.wait_ge(mask_ready, 1)
                    pe.wait_ge(k_lo_out, 4 * DC)
                    pe.wait_ge(ct_out_a, 4)
                if h < HB:
                    pe.wait_ge(qbd_ready, c + 1)
                    pe.wait_ge(qbd_hi_ready, c + 1)
                if h >= 3:
                    pe.wait_ge(exp_ready, h - 2)
                bank = h % 3
                pe.matmul(ps[:, bank, :], ones_row[:, :],
                          mask_row[:, b * SK:(b + 1) * SK].unsqueeze(1).broadcast_to([1, 2, SK]),
                          start=True, stop=False, skip_group_check=True)
                for i in range(2):
                    pair = 2 * (h % 2) + i
                    dst = ps[:, bank, i * SK:(i + 1) * SK]
                    lh = qbd_hi[:, c, b, 2 * pair:2 * pair + 2, :]
                    ll = qbd_lo[:, c, b, 2 * pair:2 * pair + 2, :]
                    keys = slice(b * SK, (b + 1) * SK)
                    pe.matmul(dst, ll, kT_hi[:, c, keys], start=False, stop=False, skip_group_check=True)
                    pe.matmul(dst, lh, kT_lo[:, c, keys], start=False, stop=False, skip_group_check=True)
                    m = pe.matmul(dst, lh, kT_hi[:, c, keys], start=False, stop=(i == 1), skip_group_check=True)
                m.then_inc(sc_done, 1)

            def turn_probs(h):
                pe.wait_ge(exp_ready, h + 1)
                if h >= 2:
                    pe.wait_ge(pt_lo_out, h - 1)
                else:
                    pe.wait_ge(v_lo_out, 8)
                for kt in range(2):
                    for i in range(2):
                        m = pe.transpose(ps[:, 4 + h % 2, (2 * kt + i) * P:(2 * kt + i + 1) * P],
                                         prob[:, h % 4, i, kt * P:(kt + 1) * P], ident[:, :])
                m.then_inc(pt_done, 1)

            def times_values(h):
                b, c = divmod(h // 2, DC)
                if h == 0:
                    pe.wait_ge(m_out, 1)
                elif h % HB == 0:
                    pe.wait_ge(on_ready, b)
                pe.wait_ge(pt_lo_out, h + 1)
                for i in range(2):
                    o = c * PAIRS + 2 * (h % 2) + i
                    dst = ps[:, 6, o * 2 * VW:(o + 1) * 2 * VW]
                    n = 0
                    for kt in range(2):
                        vh = v_hi[:, 2 * b + kt, 2 * o:2 * o + 2, :]
                        vl = v_lo[:, 2 * b + kt, 2 * o:2 * o + 2, :]
                        for lhs, rhs in ((pT_lo, vh), (pT_hi, vl), (pT_hi, vh)):
                            m = pe.matmul(dst, lhs[:, h % 4, kt, i, :], rhs, start=(n == 0), stop=(n == 5))
                            n += 1
                m.then_inc(pv_done, 1)

            def shift_heads(t, src):
                for j in range(2):
                    for h2 in range(2):
                        rhs = src(j)
                        dst = ps[64 * j:64 * j + 64, 7, 0:D].rearrange(
                            "q (o h d) -> q o h d", h=2, d=rhs.shape[-1])[:, :, h2, :]
                        m = pe.matmul(dst, ident[:, 64 * h2:64 * h2 + 64], rhs, start=True, stop=True)
                return m

            def shift_cross(t):
                pe.wait_ge(on_ready, 2 * t + 2)
                if t:
                    pe.wait_ge(x2_ready, t)
                shift_heads(t, lambda j: on[:, 2 * t + j, :, :]).then_inc(sh_done, 1)

            def turn_tile(t):
                for dc in range(DC):
                    m = pe.transpose(ps[:, 3, dc * P:(dc + 1) * P], xn[:, t, dc * P:(dc + 1) * P], ident[:, :])
                return m

            def turn_x1(t):
                pe.wait_ge(xn_ready, xn_count(1, t))
                if t:
                    pe.wait_ge(x3t_lo_out, t)
                turn_tile(t).then_inc(x2t_done, 1)

            def project(t):
                pe.wait_ge(x2t_out, t + 1)
                for c in range(DC):
                    m = pe.matmul(ps[:, 7, c * P:(c + 1) * P], mbd[:, 0, c, :], s_xT[:, c, :], start=True, stop=True)
                m.then_inc(sq_done, 1)
                for c in range(DC):
                    pe.matmul(ps[:, 3, c * P:(c + 1) * P], mbd[:, 1, c, :], s_xT[:, c, :], start=True, stop=True)
                for c in range(DC):
                    m = pe.matmul(ps[:, 3, D + c * P:D + (c + 1) * P], s_xT[:, c, :], mbd[:, 2, c, :],
                                  start=True, stop=True)
                m.then_inc(skv_done, 1)

            def self_scores(t):
                pe.wait_ge(sqbd_hi_ready, t + 1)
                pe.wait_ge(sqbd_ready, t + 1)
                pe.wait_ge(skv_lo_out, t + 1)
                for k in range(8):
                    c, pr, j = k // 4, k // 2 % 2, k % 2
                    b = 2 * t + j
                    dst = ps[:, 7, k * SQ:(k + 1) * SQ]
                    lh = s_qbd_hi[:, c, b, 2 * pr:2 * pr + 2, :]
                    ll = s_qbd_lo[:, c, b, 2 * pr:2 * pr + 2, :]
                    kh = s_kh[:, c, b * SQ:(b + 1) * SQ]
                    kl = s_kl[:, c, b * SQ:(b + 1) * SQ]
                    pe.matmul(dst, ll, kh, start=True, stop=False)
                    pe.matmul(dst, lh, kl, start=False, stop=False)
                    m = pe.matmul(dst, lh, kh, start=False, stop=True)
                m.then_inc(ssc_done, 1)

            def self_turn(t):
                pe.wait_ge(sexp_ready, t + 1)
                for k in range(4):
                    m = pe.transpose(ps[:, 3, k * P:(k + 1) * P], s_sc[:, 2 * k:2 * k + 2, :], ident[:, :])
                m.then_inc(spt_done, 1)

            def self_values(t):
                pe.wait_ge(spt_lo_out, t + 1)
                for k in range(8):
                    c, pr, j = k // 4, k // 2 % 2, k % 2
                    rows = slice(64 * j, 64 * j + 64)
                    feats = slice(c * P + pr * 2 * DH, c * P + (pr + 1) * 2 * DH)
                    dst = ps[:, (7, 3)[j], (k // 2) * 2 * DH:(k // 2 + 1) * 2 * DH]
                    ph, pl = s_pTh[rows, k // 2, :], s_pTl[rows, k // 2, :]
                    pe.matmul(dst, pl, s_vh[rows, t, feats], start=True, stop=False)
                    pe.matmul(dst, ph, s_vl[rows, t, feats], start=False, stop=False)
                    m = pe.matmul(dst, ph, s_vh[rows, t, feats], start=False, stop=True)
                m.then_inc(spv_done, 1)

            def shift_self(t):
                pe.wait_ge(son_ready, t + 1)
                shift_heads(t, lambda j: s_on[:, t].rearrange("p (k j) d -> p k j d", j=2)[:, :, j, :]).then_inc(ssh_done, 1)

            def turn_x2(t):
                pe.wait_ge(xn_ready, xn_count(2, t))
                turn_tile(t).then_inc(x3t_done, 1)

            first_stages = {2: turn_x1, 4: self_scores, 5: self_turn}
            last_stages = {0: shift_cross, 2: project, 5: self_values, 6: shift_self, 7: turn_x2}

            def router_products(dst, hc, cols):
                n = 0
                for dc in range(DC):
                    for wl, xl in ((1, 0), (0, 1), (0, 0)):
                        m = pe.matmul(dst, rw1p[:, wl, dc, hc * P:(hc + 1) * P], x3T[:, xl, dc, cols],
                                      start=(n == 0), stop=(n == 5))
                        n += 1
                return m

            for h in range(3):
                scores(h)
            for h in range(NH):
                self_step(first_stages, h)
                turn_probs(h)
                if h + 3 < NH:
                    scores(h + 3)
                if h:
                    times_values(h - 1)
                self_step(last_stages, h)
            times_values(NH - 1)
            self_step(last_stages, NH)
            early = slice(0, TAIL * P)
            for h, hcs in last_tile_steps(0)[0]:
                self_step(first_stages, h)
                self_step(last_stages, h)
                for hc in hcs:
                    if hc == 0:
                        wait_low_part(pe, 0)
                        pe.wait_ge(x3t_lo_out, TAIL)
                    if hc >= 3:
                        pe.wait_ge(r1_act, hc - 2)
                    router_products(ps[:, hc % 3, early], hc, early).then_inc(r1_done, 1)
            pe.wait_ge(x3t_lo_out, NT)
            for half in range(2):
                for i in range(4):
                    m = router_products(ps[:, (3, 7)[half], i * P:(i + 1) * P], 4 * half + i, slice(TAIL * P, NTOK))
                m.then_inc(r1_done, 1)
            pe.wait_ge(rw2_ready, 2)
            pe.wait_ge(r1_lo, HC)
            for t in range(NT):
                if t == TAIL:
                    pe.wait_ge(r1_lo, HC + 2)
                n = 0
                for hc in range(HC):
                    for hl, wl in ((1, 0), (0, 1), (0, 0)):
                        m = pe.matmul(ps[:, 4, t * E:(t + 1) * E], rh[:, hl, hc, t * P:(t + 1) * P], rw2p[:, wl, hc, :],
                                      start=(n == 0), stop=(n == 3 * HC - 1))
                        n += 1
            m.then_inc(lg_done, 1)
            pe.wait_ge(picked_ready, 1)
            for t in range(NT):
                for k in range(t + 1):
                    pe.matmul(ps[:, 5, t * E:(t + 1) * E], (before if k == t else ones16)[:, :], picked[:, k, :],
                              start=(k == 0), stop=(k == t))
            for t in range(NT):
                m = pe.matmul(ps[:, 6, 0:E], ones16[:, :], picked[:, t, :], start=(t == 0), stop=(t == NT - 1))
            m.then_inc(rank_done, 1)
            extra_expert = {}

            def expert(b):
                return slice(b, b + 1) if b < E else bass.ds(extra_expert[b], 1)

            def if_used(stage, b):
                if E <= b < NBLK:
                    with pe.If(extras > b - E):
                        stage(b)
                elif 0 <= b < E:
                    stage(b)

            def load_expert(b):
                if E <= b < NBLK:
                    extra_expert[b] = pe.value_load(owner[0:1, b - E:b - E + 1], min_val=0, max_val=E - 1)

            turned = ps[:, 6, :].bitcast(F16)

            def gather(b):
                if b:
                    pe.wait_ge(xg_out, b)
                else:
                    pe.wait_ge(x3p_lo, NT)
                for t in range(NT):
                    pe.wait_ge(onehot_ready, NT * b + t + 1)
                    for l in range(2):
                        for dc in range(DC):
                            m = pe.matmul(ps[:, 5, (l * DC + dc) * P:(l * DC + dc + 1) * P],
                                          x3p[:, l, t, dc * P:(dc + 1) * P], onehot[:, b % 3, t, :],
                                          start=(t == l == dc == 0), stop=(t == NT - 1), skip_group_check=True)
                m.then_inc(xg_done, 1)

            def gather_and_turn(b):
                gather(b)
                turn(b)

            def turn(b):
                if b:
                    pe.wait_ge(turn_out, b)
                for t in range(NT):
                    pe.transpose(turned[:, t * P:(t + 1) * P], onehot[:, b % 3, t, :], ident16[:, :])
                if b == 0:
                    pe.wait_ge(we_ready, 2)
                for t in range(NT):
                    m = pe.matmul(ps[:, 6, 2 * P:2 * P + 2],
                                  onehot[:, b % 3, t, :], wep[:, t, expert(b), :].rearrange("p e l -> p (e l)"),
                                  start=(t == 0), stop=(t == NT - 1))
                m.then_inc(turn_done, 1)

            def hidden_chunk(b, hc):
                half, i = divmod(hc, 4)
                if hc == 0:
                    pe.wait_ge(xg_out, b + 1)
                    wait_high_part(pe, 2 * min(b, E - 1) + 1)
                    wait_low_part(pe, 2 * min(b, E - 1) + 1)
                if i == 0 and b:
                    pe.wait_ge(h_act, 2 * (b - 1) + half + 1)
                n = 0
                for dc in range(DC):
                    for wl, xl in ((1, 0), (0, 1), (0, 0)):
                        m = pe.matmul(ps[:, 2 + half, i * P:(i + 1) * P],
                                      weights(expert(b), wl, dc * HID + hc * P, P), xg[:, b % 2, xl, dc, :],
                                      start=(n == 0), stop=(n == 5))
                        n += 1
                if i == 3:
                    m.then_inc(h_done, 1)

            def output_chunk(b, hc):
                if hc == 0:
                    wait_high_part(pe, 2 * min(b, E - 1) + 2)
                    wait_low_part(pe, 2 * min(b, E - 1) + 2)
                    if b:
                        pe.wait_ge(y_act, b)
                if hc % 4 == 0:
                    pe.wait_ge(h_lo, 2 * b + hc // 4 + 1)
                for hl, wl in ((1, 0), (0, 1), (0, 0)):
                    m = pe.matmul(ps[:, 4, 0:D], hp[:, b % 2, hl, hc, :], weights(expert(b), 2 + wl, hc * D, D),
                                  start=(hc == 0 and hl == 1), stop=(hc == HC - 1 and hl == wl == 0))
                if hc == HC - 1:
                    m.then_inc(y_done, 1)

            def hidden(b):
                for hc in range(HC):
                    hidden_chunk(b, hc)

            def output(b):
                for hc in range(HC):
                    output_chunk(b, hc)

            def output_and_next_hidden(b):
                if b + 1 < E:
                    hidden(b + 1)
                    output(b)
                elif b + 1 < NBLK:
                    with pe.If(extras > b + 1 - E):
                        for hc in range(HC):
                            output_chunk(b, hc)
                            hidden_chunk(b + 1, hc)
                    with pe.Else():
                        if_used(output, b)
                else:
                    if_used(output, b)

            def combine(b):
                pe.wait_ge(y_pair, b + 1)
                for t in range(NT):
                    for l in (1, 0):
                        m = pe.matmul(ps[:, t // 2, (t % 2) * D:(t % 2 + 1) * D], onehotT[:, b % 4, t * P:(t + 1) * P],
                                      yp[:, b % 2, l, :], start=False, stop=False,
                                      skip_group_check=True)
                m.then_inc(sum_done, 1)

            gather(0)
            gather(1)
            turn(0)
            hidden(0)
            turn(1)
            pe.wait_ge(we_ready, 2)
            for t in range(NT):
                m = pe.transpose(ps[0:E, 7, t * P:(t + 1) * P], we[:, t, :], ident[:, :])
            m.then_inc(wet_done, 1)

            def start_sums():
                pe.wait_ge(wet_out, 1)
                for t in range(NT):
                    pe.matmul(ps[:, t // 2, (t % 2) * D:(t % 2 + 1) * D], weT[:, t, :], b2_sb[:, :],
                              start=(t % 2 == 0), stop=False, skip_group_check=True)

            pe.wait_ge(owner_ready, 1)
            extras = pe.value_load(owner[0:1, EXTRA:], min_val=0, max_val=EXTRA)
            for b in range(NBLK):
                load_expert(b + 2)
                if_used(gather_and_turn, b + 2)
                output_and_next_hidden(b)
                if b == 0:
                    start_sums()
                if_used(combine, b - 1)
            if_used(combine, NBLK - 1)
            pe.drain().then_inc(all_summed, 1)

        @block.scalar
        def _(act):
            for i in range(2):
                act.wait_ge(wt_done, i + 2)
                act.copy(wkv[:, 0, i], ps[:, i + 1, :].rearrange("p (c n) -> p c n", c=DC)).then_inc(wkv_hi_out, 1)
            for i in range(2):
                act.wait_ge(xt_done, i + 1)
                act.copy(xnT[:, :, 2 * i * P:(2 * i + 2) * P], ps[:, 4 + i, :].rearrange("p (c n) -> p c n", c=DC)).then_inc(xt_out, 1)
            def split(k):
                act.wait_ge(in_stage[k % STAGE], 16 * (k // STAGE + 1))
                act.mul(parts(k)[0], stage[:, k % STAGE, :], WSCALE).then_inc(split_hi, 1)

            def turned_context(n):
                act.wait_ge(ct_done, 2 * n + 2)
                if n >= 2:
                    act.wait_ge(v_done, 2 * (n - 1))
                act.copy(ctx_hi[:, :, n % 2, 2 * P:4 * P], ps[:, 1, :].rearrange("p (c n) -> p c n", c=DC)).then_inc(ct_out_a, 1)

            turned_context(0)
            for n in range(4):
                if n + 1 < 4:
                    turned_context(n + 1)
                for oc in range(DC):
                    act.wait_ge(k_done, DC * n + oc + 1)
                    act.wait_ge(wt_out, 4)
                    act.activation(kT_hi[:, oc, n * 512:(n + 1) * 512], ps[:, 2 + oc, :], ACT.Identity,
                                   bias=biasT[:, KB + oc:KB + oc + 1]).then_inc(k_hi_out, 1)
                for j in range(2):
                    act.wait_ge(v_done, 2 * n + j + 1)
                    if n == 0:
                        act.wait_ge(consts, 12)
                    t = 4 * n + 2 * j
                    act.copy(v_hi[:, t:t + 2, :, 0:XD],
                             ps[:, 4 + j, :].rearrange("p (t h d) -> p t h d", t=2, d=XD)).then_inc(v_hi_out, 1)
                if n == 0:
                    act.wait_ge(q_out, DC)
                for oc, h in spread_at[n]:
                    m = act.mul(qbd_hi[:, oc, :, h, :], qh[:, oc, :].rearrange("p (b q) -> p b q", b=B),
                                headmask[:, h:h + 1])
                    if h == P // XD - 1:
                        m.then_inc(qbd_hi_ready, 1)
                for done, dst, out in ((ut_done, uT, ut_out), (m_done, mbd, m_out)):
                    if n == (1 if dst is uT else 2):
                        act.wait_ge(done, 1)
                        act.copy(dst[:, 0:2], ps[:, 6, :].rearrange("p (i c n) -> p i c n", i=2, c=DC))
                        act.copy(dst[:, 2], ps[:, 7, 0:DC * P].rearrange("p (c n) -> p c n", c=DC)).then_inc(out, 1)
            def exps(h):
                act.wait_ge(max_ready, h + 1)
                if h >= 4:
                    act.wait_ge(pt_done, h - 3)
                for i in range(2):
                    m = act.activation(prob[:, h % 4, i, :], ps[:, h % 3, i * SK:(i + 1) * SK],
                                       ACT.Exp, bias=nmax[:, h, i:i + 1])
                m.then_inc(exp_ready, 1)

            def probs_high(h):
                act.wait_ge(pt_done, h + 1)
                if h >= 4:
                    act.wait_ge(pv_done, h - 3)
                act.copy(pT_hi[:, h % 4], ps[:, 4 + h % 2, :].rearrange("p (k g q) -> p k g q", k=2, g=2)).then_inc(pt_hi_out, 1)

            def x1_turned(t):
                act.wait_ge(x2t_done, t + 1)
                act.copy(s_xT[:, :, :], ps[:, 3, 0:D].rearrange("p (c n) -> p c n", c=DC)).then_inc(x2t_out, 1)

            def queries_keys_values_high(t):
                act.wait_ge(sq_done, t + 1)
                for c in range(DC):
                    m = act.activation(s_qh[:, c, t * P:(t + 1) * P], ps[:, 7, c * P:(c + 1) * P], ACT.Identity,
                                       bias=biasT[:, SQB + c:SQB + c + 1])
                m.then_inc(sq_hi_out, 1)
                act.wait_ge(skv_done, t + 1)
                for c in range(DC):
                    act.activation(s_kh[:, c, t * P:(t + 1) * P], ps[:, 3, c * P:(c + 1) * P], ACT.Identity,
                                   bias=biasT[:, SKB + c:SKB + c + 1])
                act.copy(s_vh[:, t, :], ps[:, 3, D:2 * D]).then_inc(skv_hi_out, 1)

            def self_exp(t):
                act.wait_ge(ssub_ready, t + 1)
                act.activation(s_sc[:, :, :], s_sc[:, :, :], ACT.Exp, scale=SSCALE).then_inc(sexp_ready, 1)

            def self_probs_high(t):
                act.wait_ge(spt_done, t + 1)
                act.copy(s_pTh[:, :, :], ps[:, 3, :].rearrange("p (g q) -> p g q", g=4)).then_inc(spt_hi_out, 1)

            def x2_turned(t):
                act.wait_ge(xn_ready, xn_count(2, t))
                act.wait_ge(x3t_done, t + 1)
                act.copy(x3T[:, 0, :, t * P:(t + 1) * P], ps[:, 3, 0:D].rearrange("p (c n) -> p c n", c=DC)).then_inc(x3t_hi_out, 1)
                act.copy(x3p[:, 0, t, :], xn[:, t, :]).then_inc(x3p_hi, 1)

            first_stages = {2: x1_turned, 5: self_probs_high}
            last_stages = {2: queries_keys_values_high, 4: self_exp, 7: x2_turned}

            exps(0)
            exps(1)
            for h in range(NH):
                self_step(first_stages, h)
                if h + 2 < NH:
                    exps(h + 2)
                probs_high(h)
                if h in SPLIT_AT:
                    split((1, 3, 4)[SPLIT_AT.index(h)])
                self_step(last_stages, h)
            self_step(last_stages, NH)
            def router_silu(hc):
                act.wait_ge(r1_done, hc + 1)
                if hc >= 2:
                    act.wait_ge(r1_lo, hc - 1)
                act.activation(r32[:, hc % 2, :], ps[:, hc % 3, 0:TAIL * P], ACT.Silu,
                               bias=biasT[:, RB + hc:RB + hc + 1], scale=1 / WSCALE).then_inc(r1_act, 1)

            steps, rest = last_tile_steps(1)
            for h, hcs in steps:
                for hc in hcs:
                    router_silu(hc)
                self_step(first_stages, h)
                self_step(last_stages, h)
                if h == NH + 6:
                    split(5)
                    split(6)
            for hc in rest:
                router_silu(hc)
            for half in range(2):
                act.wait_ge(r1_done, HC + half + 1)
                for i in range(4):
                    hc = 4 * half + i
                    m = act.activation(h32[:, half, i * P:(i + 1) * P], ps[:, (3, 7)[half], i * P:(i + 1) * P],
                                       ACT.Silu, bias=biasT[:, RB + hc:RB + hc + 1], scale=1 / WSCALE)
                m.then_inc(r1_act, 1)
            act.wait_ge(gap_ready, 1)
            act.activation(th[:, :], gap[:, :], ACT.Tanh, scale=0.5).then_inc(th_ready, 1)
            split(7)
            split(8)

            def gathered(b):
                act.wait_ge(xg_done, b + 1)
                if b >= 2:
                    act.wait_ge(h_done, 2 * (b - 1))
                act.copy(xg[:, b % 2], ps[:, 5, :].rearrange("p (l c n) -> p l c n", l=2, c=DC)).then_inc(xg_out, 1)

            def hidden(b):
                if b >= E:
                    expert = act.value_load(owner[0:1, b - E:b - E + 1], min_val=0, max_val=E - 1)
                for half in range(2):
                    act.wait_ge(h_done, 2 * b + half + 1)
                    if b:
                        act.wait_ge(h_lo, 2 * (b - 1) + half + 1)
                    for i in range(4):
                        biases = biasT[:, EB:EB + E * HC].rearrange("p (e c) -> p e c", c=HC)[:, :, 4 * half + i]
                        bias = biases[:, b:b + 1] if b < E else biases[:, bass.ds(expert, 1)]
                        m = act.activation(h32[:, half, i * P:(i + 1) * P], ps[:, 2 + half, i * P:(i + 1) * P],
                                           ACT.Silu, bias=bias, scale=1 / WSCALE)
                    m.then_inc(h_act, 1)

            def output(b):
                act.wait_ge(y_done, b + 1)
                act.wait_ge(turn_out, b + 1)
                if b >= 2:
                    act.wait_ge(y_pair, b - 1)
                act.mul(y32[:, b % 2, :], ps[:, 4, 0:D], wslot[:, b:b + 1]).then_inc(y_act, 1)

            def if_used(stage, b):
                if E <= b < NBLK:
                    with act.If(extras > b - E):
                        stage(b)
                elif b < E:
                    stage(b)

            gathered(0)
            gathered(1)
            hidden(0)
            act.wait_ge(owner_ready, 1)
            extras = act.value_load(owner[0:1, EXTRA:], min_val=0, max_val=EXTRA)
            for b in range(NBLK):
                if_used(gathered, b + 2)
                if_used(hidden, b + 1)
                if_used(output, b)
                if b < 4:
                    split(9 + 2 * b)
                    split(10 + 2 * b)

        @block.vector
        def _(dve):
            step = [0]

            def link(ins):
                step[0] += 1
                ins.then_inc(dve_step, 1)
                dve.wait_ge(dve_step, step[0])

            def norm_stats(n, t):
                link(dve.bn_stats(stats[:, n, t, :], xs[:, t, :]))
                link(dve.bn_aggr(mv[:, n, t, :], stats[:, n, t, :]))
                dve.tensor_scalar(vareps[:, n, t:t + 1], mv[:, n, t, 1:2], EPS, None, ALU.add).then_inc(var_ready, 1)

            def norm_apply(n, t):
                dve.wait_ge(rstd_ready, xn_count(n, t))
                dve.tensor_scalar(xn[:, t, :], xs[:, t, :], mv[:, n, t, 0:1], rstd[:, n, t:t + 1],
                                  ALU.subtract, ALU.mult).then_inc(xn_ready, 1)

            dve.wait_ge(in_x, 16)
            for t in range(NT):
                norm_stats(0, t)
            for t in range(NT):
                norm_apply(0, t)
            dve.wait_ge(wt_done, 1)
            dve.tensor_copy(wT[:, :, :], ps[:, 0, :].rearrange("p (c n) -> p c n", c=DC)).then_inc(wt_out, 1)
            for i in range(2):
                dve.wait_ge(wkv_hi_out, i + 1)
                dve.tensor_tensor(wkv_rest[:, i], ps[:, i + 1, :].rearrange("p (c n) -> p c n", c=DC), wkv[:, 0, i],
                                  ALU.subtract).then_inc(wt_out, 1)
            dve.wait_ge(wt_done, 4)
            dve.tensor_copy(biasT[:, :], ps[:, 3, 0:NB]).then_inc(wt_out, 1)
            dve.wait_ge(wt_out, 3)
            dve.tensor_scalar(wkv[:, 1], wkv_rest[:, :, :, :], WSCALE, None, ALU.mult).then_inc(wkv_ready, 1)
            def turned_context(n):
                dve.wait_ge(ct_done, 2 * n + 1)
                if n >= 2:
                    dve.wait_ge(v_done, 2 * (n - 1))
                dve.tensor_copy(ctx_hi[:, :, n % 2, 0:2 * P], ps[:, 0, :].rearrange("p (c n) -> p c n", c=DC)).then_inc(ct_hi_d, 1)
                for j, done in ((0, ct_hi_d), (1, ct_out_a)):
                    dve.wait_ge(done, n + 1)
                    cols = slice(2 * j * P, 2 * (j + 1) * P)
                    m = dve.tensor_tensor(ctx_lo[:, :, n % 2, cols], ps[:, j, :].rearrange("p (c n) -> p c n", c=DC),
                                          ctx_hi[:, :, n % 2, cols], ALU.subtract)
                m.then_inc(ct_out_d, 1)

            turned_context(0)
            dve.wait_ge(in_mask, 16)
            dve.tensor_scalar(mask_row[:, :], mask_i[:, :], 0.0, MASKED, ALU.is_gt, ALU.mult).then_inc(mask_ready, 1)
            dve.wait_ge(wt_out, 4)
            for oc in range(DC):
                dve.wait_ge(q_done, oc + 1)
                link(dve.tensor_scalar(q32[:, oc, :], ps[:, 6 + oc, :], biasT[:, QB + oc:QB + oc + 1], XSCALE,
                                       ALU.add, ALU.mult))
                link(dve.tensor_copy(qh[:, oc, :], q32[:, oc, :]))
                dve.tensor_tensor(ql[:, oc, :], q32[:, oc, :], qh[:, oc, :], ALU.subtract).then_inc(q_out, 1)
            dve.wait_ge(q_out, DC)
            dve.wait_ge(consts, 7)

            def spread_queries(n):
                for oc, h in spread_at[n]:
                    m = dve.tensor_scalar(qbd_lo[:, oc, :, h, :], ql[:, oc, :].rearrange("p (b q) -> p b q", b=B),
                                          headmask[:, h:h + 1], None, ALU.mult)
                    if h == P // XD - 1:
                        m.then_inc(qbd_ready, 1)

            def split(k):
                wait_high_part(dve, k)
                hi, lo = parts(k)
                dve.scalar_tensor_tensor(out=lo, in0=stage[:, k % STAGE, :], scalar=WSCALE, in1=hi,
                                         op0=ALU.mult, op1=ALU.subtract).then_inc(split_lo_d, 1)

            for n in range(4):
                if n + 1 < 4:
                    turned_context(n + 1)
                for oc in range(DC):
                    dve.wait_ge(k_hi_out, DC * n + oc + 1)
                    dve.scalar_tensor_tensor(out=kT_lo[:, oc, n * 512:(n + 1) * 512], in0=ps[:, 2 + oc, :],
                                             scalar=biasT[:, KB + oc:KB + oc + 1],
                                             in1=kT_hi[:, oc, n * 512:(n + 1) * 512],
                                             op0=ALU.add, op1=ALU.subtract).then_inc(k_lo_out, 1)
                for j in range(2):
                    dve.wait_ge(v_hi_out, 2 * n + j + 1)
                    t = 4 * n + 2 * j
                    dve.tensor_tensor(v_lo[:, t:t + 2, :, 0:XD],
                                      ps[:, 4 + j, :].rearrange("p (t h d) -> p t h d", t=2, d=XD),
                                      v_hi[:, t:t + 2, :, 0:XD], ALU.subtract).then_inc(v_lo_out, 1)
                spread_queries(n)
            def maxima(h):
                dve.wait_ge(sc_done, h + 1)
                dve.tensor_reduce(nmax[:, h, :], ps[:, h % 3, :].rearrange("p (i k) -> p i k", i=2),
                                  AX.X, ALU.max, negate=True).then_inc(max_ready, 1)

            def probs_low(h):
                dve.wait_ge(pt_hi_out, h + 1)
                dve.tensor_tensor(pT_lo[:, h % 4], ps[:, 4 + h % 2, :].rearrange("p (k g q) -> p k g q", k=2, g=2),
                                  pT_hi[:, h % 4], ALU.subtract).then_inc(pt_lo_out, 1)

            def normalise(b):
                dve.wait_ge(pv_done, HB * (b + 1))
                o = ps[:, 6, 0:DC * PAIRS * 2 * VW].rearrange("p (o h d) -> p o h d", h=2, d=VW)
                for h2 in range(2):
                    r = slice(64 * h2, 64 * h2 + 64)
                    m = dve.reciprocal(orec[r, b, :], o[r, :, h2, XD])
                link(m)
                for h2 in range(2):
                    r = slice(64 * h2, 64 * h2 + 64)
                    m = dve.tensor_tensor(on[r, b], o[r, :, h2, 0:XD],
                                          orec[r, b, :].unsqueeze(2).broadcast_to([64, DC * PAIRS, XD]), ALU.mult)
                m.then_inc(on_ready, 1)

            def add_to_stream(n, t, done, ready):
                dve.wait_ge(done, t + 1)
                dve.tensor_tensor(xs[:, t, :], ps[:, 7, 0:D], xs[:, t, :], ALU.add).then_inc(ready, 1)
                dve.wait_ge(ready, t + 1)
                norm_stats(n, t)

            def add_cross(t):
                dve.wait_ge(vb_added, NT)
                add_to_stream(1, t, sh_done, x1_ready)

            def spread_self(t):
                cols = slice(t * P, (t + 1) * P)
                dve.wait_ge(sq_hi_out, t + 1)
                for c in range(DC):
                    m = dve.scalar_tensor_tensor(out=s_ql[:, c, cols], in0=ps[:, 7, c * P:(c + 1) * P],
                                                 scalar=biasT[:, SQB + c:SQB + c + 1], in1=s_qh[:, c, cols],
                                                 op0=ALU.add, op1=ALU.subtract)
                link(m)
                for h in range(P // DH):
                    m = dve.tensor_scalar(s_qbd_lo[:, :, 2 * t:2 * t + 2, h, :],
                                          s_ql[:, :, cols].rearrange("p c (b q) -> p c b q", b=2),
                                          blockmask[:, h:h + 1], None, ALU.mult)
                m.then_inc(sqbd_ready, 1)
                dve.wait_ge(skv_hi_out, t + 1)
                for c in range(DC):
                    dve.scalar_tensor_tensor(out=s_kl[:, c, cols], in0=ps[:, 3, c * P:(c + 1) * P],
                                             scalar=biasT[:, SKB + c:SKB + c + 1], in1=s_kh[:, c, cols],
                                             op0=ALU.add, op1=ALU.subtract)
                dve.tensor_tensor(s_vl[:, t, :], ps[:, 3, D:2 * D], s_vh[:, t, :], ALU.subtract).then_inc(skv_lo_out, 1)

            def self_centre(t):
                dve.wait_ge(ssc_done, t + 1)
                s = ps[:, 7, :].rearrange("p (k q) -> p k q", k=8)
                link(dve.tensor_reduce(s_max[:, t, :], s, AX.X, ALU.max))
                dve.tensor_tensor(s_sc[:, :, :], s, s_max[:, t, :].unsqueeze(2).broadcast_to([P, 8, SQ]),
                                  ALU.subtract).then_inc(ssub_ready, 1)

            def self_sums(t):
                dve.wait_ge(sexp_ready, t + 1)
                link(dve.tensor_reduce(s_sum[:, t, :], s_sc[:, :, :], AX.X, ALU.add))
                link(dve.reciprocal(s_rec[:, t, :], s_sum[:, t, :]))
                dve.wait_ge(spt_hi_out, t + 1)
                dve.tensor_tensor(s_pTl[:, :, :], ps[:, 3, :].rearrange("p (g q) -> p g q", g=4),
                                  s_pTh[:, :, :], ALU.subtract).then_inc(spt_lo_out, 1)

            def self_normalise(t):
                dve.wait_ge(spv_done, t + 1)
                for j in range(2):
                    o = ps[:, (7, 3)[j], 0:D].rearrange("p (k h d) -> p k h d", k=4, h=2)
                    for h2 in range(2):
                        r = slice(64 * h2, 64 * h2 + 64)
                        m = dve.tensor_tensor(s_on[r, t].rearrange("p (k j) d -> p k j d", j=2)[:, :, j, :],
                                              o[r, :, h2, :],
                                              s_rec[r, t, j::2].unsqueeze(2).broadcast_to([64, 4, DH]), ALU.mult)
                m.then_inc(son_ready, 1)

            def add_self(t):
                dve.wait_ge(bv_added, t + 1)
                add_to_stream(2, t, ssh_done, x2_ready)

            def x2_low(t):
                dve.wait_ge(x3t_hi_out, t + 1)
                dve.tensor_tensor(x3T[:, 1, :, t * P:(t + 1) * P], ps[:, 3, 0:D].rearrange("p (c n) -> p c n", c=DC),
                                  x3T[:, 0, :, t * P:(t + 1) * P], ALU.subtract).then_inc(x3t_lo_out, 1)

            def norm_x1(t):
                norm_apply(1, t)

            def norm_x2(t):
                norm_apply(2, t)

            first_stages = {4: self_centre, 5: self_sums}
            norm_stages = {1: norm_x1, 7: norm_x2}
            last_stages = {0: add_cross, 2: spread_self, 5: self_normalise, 6: add_self, 7: x2_low}

            def rw2_pair():
                dve.wait_ge(in_rw2, 16)
                dve.tensor_scalar(rw2p[:, 0], rw2_sb[:, :, :], WSCALE, None, ALU.mult).then_inc(rw2_ready, 1)
                dve.wait_ge(rw2_ready, 1)
                dve.scalar_tensor_tensor(out=rw2p[:, 1], in0=rw2_sb[:, :, :], scalar=WSCALE, in1=rw2p[:, 0],
                                         op0=ALU.mult, op1=ALU.subtract).then_inc(rw2_ready, 1)

            for h in range(3):
                maxima(h)
            for h in range(NH):
                self_step(first_stages, h)
                if h + 3 < NH:
                    maxima(h + 3)
                self_step(norm_stages, h)
                probs_low(h)
                if h % HB == 0 and h:
                    normalise(h // HB - 1)
                if h == 4:
                    rw2_pair()
                if h - 1 in SPLIT_AT[0:2]:
                    split((1, 3)[SPLIT_AT.index(h - 1)])
                self_step(last_stages, h)
            self_step(norm_stages, NH)
            normalise(B - 1)
            self_step(last_stages, NH)
            def router_pair(hc):
                dve.wait_ge(r1_act, hc + 1)
                dve.tensor_copy(rh[:, 0, hc, 0:TAIL * P], r32[:, hc % 2, :]).then_inc(r1_hi, 1)
                dve.wait_ge(r1_hi, hc + 1)
                dve.tensor_tensor(rh[:, 1, hc, 0:TAIL * P], r32[:, hc % 2, :], rh[:, 0, hc, 0:TAIL * P],
                                  ALU.subtract).then_inc(r1_lo, 1)

            steps, rest = last_tile_steps(1)
            for h, hcs in steps:
                self_step(first_stages, h)
                self_step(norm_stages, h)
                for hc in hcs:
                    router_pair(hc)
                self_step(last_stages, h)
            split(5)
            for hc in rest:
                router_pair(hc)
            for half in range(2):
                dve.wait_ge(r1_act, HC + half + 1)
                hcs = slice(4 * half, 4 * half + 4)
                src = h32[:, half, :].rearrange("p (c n) -> p c n", c=4)
                dve.tensor_copy(rh[:, 0, hcs, TAIL * P:], src).then_inc(r1_hi, 1)
                dve.wait_ge(r1_hi, HC + half + 1)
                dve.tensor_tensor(rh[:, 1, hcs, TAIL * P:], src, rh[:, 0, hcs, TAIL * P:], ALU.subtract).then_inc(r1_lo, 1)

            dve.wait_ge(lg_done, 1)
            link(dve.scalar_tensor_tensor(out=logit[:, :, :], in0=ps[:, 4, 0:NT * E].rearrange("p (t e) -> p t e", t=NT),
                                          scalar=1 / WSCALE, in1=rb2_all[:, :].unsqueeze(1).broadcast_to([P, NT, E]),
                                          op0=ALU.mult, op1=ALU.add))
            for t in range(NT):
                m = dve.max(top[:, t, :], logit[:, t, :])
            link(m)
            dve.tensor_tensor(gap[:, :], top[:, :, 0], top[:, :, 1], ALU.subtract).then_inc(gap_ready, 1)
            for t in range(NT):
                m = dve.max_index(topi[:, t, :], top[:, t, :], logit[:, t, :])
            link(m)
            dve.wait_ge(consts, CONSTS)
            for k in range(2):
                m = dve.tensor_tensor(pick[:, k], iota_f[:, 0:E].unsqueeze(1).broadcast_to([P, NT, E]),
                                      topi[:, :, k].unsqueeze(2).broadcast_to([P, NT, E]), ALU.is_equal)
            link(m)
            dve.tensor_tensor(picked[:, :, :], pick[:, 0], pick[:, 1], ALU.add).then_inc(picked_ready, 1)
            dve.wait_ge(rank_done, 1)
            dve.tensor_tensor(own_slot[:, :, :], ps[:, 5, 0:NT * E].rearrange("p (t e) -> p t e", t=NT),
                              own_base[:, :].unsqueeze(1).broadcast_to([P, NT, E]), ALU.add)
            link(dve.tensor_tensor(over[:, :, :], ps[:, 6, 0:E].unsqueeze(2).broadcast_to([P, E, 3]),
                                   limits[:, :].unsqueeze(1).broadcast_to([P, E, 3]), ALU.is_gt))
            link(dve.tensor_reduce(extra[:, 1:], over[:, :, :], AX.X, ALU.add))
            link(dve.tensor_tensor_scan(jump[:, :], minus_one[:, :], extra[:, :], float(E), ALU.add, ALU.add))
            link(dve.scalar_tensor_tensor(out=skip[:, :, :], in0=ps[:, 5, 0:NT * E].rearrange("p (t e) -> p t e", t=NT),
                                          scalar=float(P), in1=jump[:, 0:E].unsqueeze(1).broadcast_to([P, NT, E]),
                                          op0=ALU.is_ge, op1=ALU.mult))
            link(dve.scalar_tensor_tensor(out=gslot[:, :, :], in0=skip[:, :, :], scalar=float(P), in1=own_slot[:, :, :],
                                          op0=ALU.mult, op1=ALU.add))
            for k in range(2):
                m = dve.tensor_tensor(slot12[:, k], pick[:, k], gslot[:, :, :], ALU.mult)
            link(m)
            link(dve.tensor_reduce(slot[:, :, :], slot12[:, :, :, :], AX.X, ALU.add))

            def one_hot(b):
                if b >= 3:
                    dve.wait_ge(turn_done, b - 2)
                for t in range(NT):
                    m = dve.tensor_scalar(onehot[:, b % 3, t, :], slot_ids[:, b * P:(b + 1) * P],
                                          slot[:, 0, t:t + 1], None, ALU.is_equal)
                m.then_inc(first_choice, 1)
                dve.wait_ge(first_choice, b + 1)
                for t in range(NT):
                    m = dve.scalar_tensor_tensor(out=onehot[:, b % 3, t, :], in0=slot_ids[:, b * P:(b + 1) * P],
                                                 scalar=slot[:, 1, t:t + 1], in1=onehot[:, b % 3, t, :],
                                                 op0=ALU.is_equal, op1=ALU.add)
                    m.then_inc(onehot_ready, 1)

            def turned(b):
                dve.wait_ge(turn_done, b + 1)
                if b >= 4:
                    dve.wait_ge(sum_done, b - 3)
                dve.tensor_copy(onehotT[:, b % 4, :], ps[:, 6, 0:2 * P].bitcast(F16))
                dve.tensor_reduce(wslot[:, b:b + 1], ps[:, 6, 2 * P:2 * P + 2], AX.X, ALU.add).then_inc(wslot_sum, 1)
                dve.wait_ge(wslot_sum, b + 1)
                dve.tensor_scalar(wslot[:, b:b + 1], wslot[:, b:b + 1], 1 / WSCALE, None, ALU.mult).then_inc(turn_out, 1)

            def hidden(b):
                for half in range(2):
                    dve.wait_ge(h_act, 2 * b + half + 1)
                    if b >= 2:
                        dve.wait_ge(y_done, b - 1)
                    src = h32[:, half, :].rearrange("p (c n) -> p c n", c=4)
                    dve.tensor_copy(hp[:, b % 2, 0, 4 * half:4 * half + 4, :], src).then_inc(h_hi, 1)
                    dve.wait_ge(h_hi, 2 * b + half + 1)
                    dve.tensor_tensor(hp[:, b % 2, 1, 4 * half:4 * half + 4, :], src,
                                      hp[:, b % 2, 0, 4 * half:4 * half + 4, :], ALU.subtract).then_inc(h_lo, 1)

            def output(b):
                dve.wait_ge(y_act, b + 1)
                if b >= 2:
                    dve.wait_ge(sum_done, b - 1)
                dve.tensor_copy(yp[:, b % 2, 0, :], y32[:, b % 2, :]).then_inc(y_hi, 1)
                dve.wait_ge(y_hi, b + 1)
                dve.tensor_tensor(yp[:, b % 2, 1, :], y32[:, b % 2, :], yp[:, b % 2, 0, :], ALU.subtract).then_inc(y_pair, 1)

            def if_used(stage, b):
                if E <= b < NBLK:
                    with dve.If(extras > b - E):
                        stage(b)
                elif b < E:
                    stage(b)

            one_hot(0)
            one_hot(1)
            dve.wait_ge(th_ready, 1)
            dve.tensor_scalar(p1[:, :], th[:, :], 0.5, 0.5, ALU.mult, ALU.add)
            link(dve.tensor_scalar(p2[:, :], th[:, :], -0.5, 0.5, ALU.mult, ALU.add))
            dve.tensor_tensor(we1[:, :, :], pick[:, 0], p1[:, :].unsqueeze(2).broadcast_to([P, NT, E]), ALU.mult)
            link(dve.tensor_tensor(we2[:, :, :], pick[:, 1], p2[:, :].unsqueeze(2).broadcast_to([P, NT, E]), ALU.mult))
            link(dve.tensor_tensor(we[:, :, :], we1[:, :, :], we2[:, :, :], ALU.add))
            dve.tensor_copy(wep[:, :, :, 0], we[:, :, :]).then_inc(we_ready, 1)
            dve.wait_ge(we_ready, 1)
            dve.tensor_tensor(wep[:, :, :, 1], we[:, :, :], wep[:, :, :, 0], ALU.subtract).then_inc(we_ready, 1)
            one_hot(2)
            link(dve.tensor_tensor(extra_to[:, :], jump[0:1, 1:], behind[0:1, :], ALU.subtract))
            link(dve.tensor_tensor(owner3[:, :, :], extra_to[0:1, :].unsqueeze(1).broadcast_to([1, EXTRA, E]),
                                   iota_f[0:1, 0:EXTRA].unsqueeze(2).broadcast_to([1, EXTRA, E]), ALU.is_le))
            link(dve.tensor_reduce(owner_f[:, :], owner3[:, :, :], AX.X, ALU.add))
            dve.tensor_copy(owner[:, EXTRA:], extra_to[0:1, E - 1:E])
            dve.tensor_scalar(owner[:, 0:EXTRA], owner_f[:, :], float(E - 1), None, ALU.min).then_inc(owner_ready, 1)
            turned(0)
            turned(1)
            hidden(0)
            dve.wait_ge(wet_done, 1)
            dve.tensor_copy(weT[:, :, :], ps[0:E, 7, :].rearrange("e (t n) -> e t n", t=NT)).then_inc(wet_out, 1)
            split(7)
            dve.wait_ge(owner_ready, 1)
            extras = dve.value_load(owner[0:1, EXTRA:], min_val=0, max_val=EXTRA)
            for b in range(NBLK):
                if_used(one_hot, b + 3)
                if_used(turned, b + 2)
                if_used(hidden, b + 1)
                if_used(output, b)
                if b < 4:
                    split(9 + 2 * b)
            dve.wait_ge(all_summed, 1)
            for t in range(NT):
                dve.tensor_tensor(xn[:, t, :], ps[:, t // 2, (t % 2) * D:(t % 2 + 1) * D], xs[:, t, :],
                                  ALU.add).then_inc(out_ready, 1)


_INS = ["x", "ctx_1024", "mask_BxS2_ik0", "L0_xattn_q_w", "L0_xattn_q_b", "L0_xattn_k_w", "L0_xattn_k_b",
        "L0_xattn_v_w", "L0_xattn_v_b", "L0_attn_Uq", "L0_attn_Vq", "L0_attn_bq", "L0_attn_Uk", "L0_attn_Vk",
        "L0_attn_bk", "L0_attn_Uv", "L0_attn_Vv", "L0_attn_bv", "L0_ffn_rw1", "L0_ffn_rb1", "L0_ffn_rw2",
        "L0_ffn_rb2", "L0_ffn_w1", "L0_ffn_b1", "L0_ffn_w2", "L0_ffn_b2"]
_OUT = ((8, 64, 256), "float32")


def kernel(**inputs):
    import numpy as _np
    import concourse.bacc as _bacc
    from concourse import mybir as _mybir
    from concourse.bass_utils import run_bass_kernel_spmd as _run

    nc = _bacc.Bacc("TRN2", target_bir_lowering=False, num_devices=1)
    arrays, args = {}, []
    for name in _INS:
        a = _np.ascontiguousarray(inputs[name])
        arrays[f"in_{name}_dram"] = a
        args.append(nc.dram_tensor(f"in_{name}_dram", a.shape, _mybir.dt.from_np(a.dtype), kind="ExternalInput").ap())
    args.append(nc.dram_tensor("out_0_dram", _OUT[0], _mybir.dt.from_np(_np.dtype(_OUT[1])), kind="ExternalOutput").ap())
    perceiver_layer(nc, *args)
    r = _run(nc, [arrays], core_ids=[0])
    return r.results[0]["out_0_dram"]
```
